# Optimizing a Trainium2 kernel written in Bass

```python
import numpy as np
import jax
import jax.numpy as jnp

def _softmax(x, axis=-1):
    return jax.nn.softmax(x, axis=axis)

def _gelu(x):
    return jax.nn.gelu(x, approximate=True)

def _silu(x):
    return jax.nn.silu(x)

def _sigmoid(x):
    return jax.nn.sigmoid(x)

def _layernorm(x, axis=-1, eps=1e-05):
    m = jnp.mean(x, axis=axis, keepdims=True)
    v = jnp.var(x, axis=axis, keepdims=True)
    return (x - m) / jnp.sqrt(v + eps)

def _scatter_add(tgt, idx, src, axis=0):
    return tgt.at[idx].add(src)

def _segment_sum(src, seg, n):
    return jax.ops.segment_sum(src, seg, n)
kernel_name = 'mk_adj_ffn_d1_adj_r2_77c9ef'

def setup_inputs(seed: int=0):
    np.random.seed(seed)
    _w = jnp.asarray

    def _rec_inputs():
        import jax
        import jax.numpy as jnp
        _gk = jax.random.key(seed)
        x = -8.776e-05 + 1 * jax.random.normal(jax.random.fold_in(_gk, 1), (10000, 128), jnp.float32)
        _a = jax.random.bernoulli(jax.random.fold_in(_gk, 2), 0.0004, (10000, 10000))
        _a = jnp.logical_or(_a, jnp.swapaxes(_a, -1, -2))
        _a = jnp.logical_or(_a, jnp.eye(10000, dtype=bool))
        _af = _a.astype(jnp.float32)
        _af = _af * jax.random.uniform(jax.random.fold_in(_gk, 3), (10000, 10000), jnp.float32, 0.05, 1)
        adj = _af
        return (x, adj)
    x, adj = _rec_inputs()

    def _L0_gnn_setup():
        import jax, jax.numpy as jnp
        import numpy as np
        N_USER = 10000
        N_ITEM = 10000
        HID = 128
        key = jax.random.key(seed)
        k1, k2, k3, k4, k5, k6, k7 = jax.random.split(key, 7)
        scale = 1.0 / np.sqrt(HID)
        return {'user_feat': jax.random.normal(k1, (N_USER, HID), dtype=jnp.float32), 'item_feat': jax.random.normal(k2, (N_ITEM, HID), dtype=jnp.float32), 'adj': jax.random.uniform(k3, (N_USER, N_ITEM), dtype=jnp.float32), 'W_item': jax.random.uniform(k4, (HID, HID), dtype=jnp.float32, minval=-scale, maxval=scale), 'b_item': jax.random.uniform(k5, (HID,), dtype=jnp.float32, minval=-scale, maxval=scale), 'W_user': jax.random.uniform(k6, (HID, HID), dtype=jnp.float32, minval=-scale, maxval=scale), 'b_user': jax.random.uniform(k7, (HID,), dtype=jnp.float32, minval=-scale, maxval=scale)}
    _L0_gnn_all = _L0_gnn_setup()
    _L0_gnn_in = {k: v for k, v in _L0_gnn_all.items() if k in ('item_feat', 'W_item', 'b_item', 'W_user', 'b_user')}
    del _L0_gnn_all

    def _L0_ffn_setup():
        import jax, jax.numpy as jnp
        import numpy as np
        B, N, D = (16, 2048, 128)
        NUM_EXPERTS, TOP_K, HEADS = (4, 2, 4)
        N_EDGES = 524288
        LN_EPS = 1e-05

        def _layernorm(x, g, b):
            mu = x.mean(-1, keepdims=True)
            var = ((x - mu) ** 2).mean(-1, keepdims=True)
            return (x - mu) * jax.lax.rsqrt(var + LN_EPS) * g + b

        def _forward(x, edge_index, W_gat, att_src, att_dst, b_gat, ln_gamma, ln_beta, W1, b1, W2, b2):
            Bc, Nc, Dc = x.shape
            M = Bc * Nc
            x_flat = x.reshape(M, Dc)
            h = (x_flat @ W_gat).reshape(M, HEADS, NUM_EXPERTS)
            loops = jnp.arange(M, dtype=edge_index.dtype)
            src = jnp.concatenate([edge_index[0], loops])
            dst = jnp.concatenate([edge_index[1], loops])
            a_src = (h * att_src).sum(-1)
            a_dst = (h * att_dst).sum(-1)
            e = jax.nn.leaky_relu(a_src[src] + a_dst[dst], negative_slope=0.2)
            e_max = jax.ops.segment_max(e, dst, num_segments=M)
            ee = jnp.exp(e - e_max[dst])
            denom = jax.ops.segment_sum(ee, dst, num_segments=M)
            alpha = ee / (denom[dst] + 1e-16)
            msg = h[src] * alpha[:, :, None]
            agg = jax.ops.segment_sum(msg, dst, num_segments=M).reshape(M, HEADS * NUM_EXPERTS) + b_gat
            scores = _layernorm(agg, ln_gamma, ln_beta).reshape(M, HEADS, NUM_EXPERTS).mean(1)
            scores = scores.reshape(Bc, Nc, NUM_EXPERTS)
            topk_s, topk_i = jax.lax.top_k(scores, TOP_K)
            w = jax.nn.softmax(topk_s, axis=-1)
            out = jnp.zeros_like(x)
            for ei in range(NUM_EXPERTS):
                g = jnp.where(topk_i == ei, w, 0.0).sum(-1)
                hh = jax.nn.gelu(x @ W1[ei] + b1[ei], approximate=False)
                out = out + g[..., None] * (hh @ W2[ei] + b2[ei])
            return out
        key = jax.random.key(seed)
        ks = jax.random.split(key, 8)
        s = 0.05
        return {'x': jax.random.normal(ks[0], (B, N, D), jnp.float32), 'W_gat': jax.random.normal(ks[1], (D, HEADS * NUM_EXPERTS), jnp.float32) * s, 'att_src': jax.random.normal(ks[2], (HEADS, NUM_EXPERTS), jnp.float32) * s, 'att_dst': jax.random.normal(ks[3], (HEADS, NUM_EXPERTS), jnp.float32) * s, 'b_gat': jnp.zeros((HEADS * NUM_EXPERTS,), jnp.float32), 'ln_gamma': jnp.ones((HEADS * NUM_EXPERTS,), jnp.float32), 'ln_beta': jnp.zeros((HEADS * NUM_EXPERTS,), jnp.float32), 'W1': jax.random.normal(ks[4], (NUM_EXPERTS, D, 2 * D), jnp.float32) * s, 'b1': jnp.zeros((NUM_EXPERTS, 2 * D), jnp.float32), 'W2': jax.random.normal(ks[5], (NUM_EXPERTS, 2 * D, D), jnp.float32) * s, 'b2': jnp.zeros((NUM_EXPERTS, D), jnp.float32), 'edge_index': jax.random.randint(ks[6], (2, N_EDGES), 0, B * N, jnp.int32)}
    _L0_ffn_all = _L0_ffn_setup()
    _L0_ffn_in = {k: v for k, v in _L0_ffn_all.items() if k in ('W_gat', 'att_src', 'att_dst', 'b_gat', 'ln_gamma', 'ln_beta', 'W1', 'b1', 'W2', 'b2', 'edge_index')}
    del _L0_ffn_all
    return {'x': x, 'adj': adj, 'L0_gnn_item_feat': _L0_gnn_in['item_feat'], 'L0_gnn_W_item': _L0_gnn_in['W_item'], 'L0_gnn_b_item': _L0_gnn_in['b_item'], 'L0_gnn_W_user': _L0_gnn_in['W_user'], 'L0_gnn_b_user': _L0_gnn_in['b_user'], 'L0_ffn_W_gat': _L0_ffn_in['W_gat'], 'L0_ffn_att_src': _L0_ffn_in['att_src'], 'L0_ffn_att_dst': _L0_ffn_in['att_dst'], 'L0_ffn_b_gat': _L0_ffn_in['b_gat'], 'L0_ffn_ln_gamma': _L0_ffn_in['ln_gamma'], 'L0_ffn_ln_beta': _L0_ffn_in['ln_beta'], 'L0_ffn_W1': _L0_ffn_in['W1'], 'L0_ffn_b1': _L0_ffn_in['b1'], 'L0_ffn_W2': _L0_ffn_in['W2'], 'L0_ffn_b2': _L0_ffn_in['b2'], 'L0_ffn_edge_index': _L0_ffn_in['edge_index']}

def reference(x, adj, L0_gnn_item_feat, L0_gnn_W_item, L0_gnn_b_item, L0_gnn_W_user, L0_gnn_b_user, L0_ffn_W_gat, L0_ffn_att_src, L0_ffn_att_dst, L0_ffn_b_gat, L0_ffn_ln_gamma, L0_ffn_ln_beta, L0_ffn_W1, L0_ffn_b1, L0_ffn_W2, L0_ffn_b2, L0_ffn_edge_index):
    import jax
    import jax.numpy as jnp

    def _L0_gnn_ref(user_feat, item_feat, adj, W_item, b_item, W_user, b_user):
        import jax, jax.numpy as jnp
        import numpy as np
        N_USER = 10000
        N_ITEM = 10000
        HID = 128
        h = item_feat @ W_item.T + b_item
        b = user_feat @ W_user.T + b_user
        return jax.nn.relu(adj @ h + b)

    def _L0_ffn_ref(x, W_gat, att_src, att_dst, b_gat, ln_gamma, ln_beta, W1, b1, W2, b2, edge_index):
        import jax, jax.numpy as jnp
        import numpy as np
        B, N, D = (16, 2048, 128)
        NUM_EXPERTS, TOP_K, HEADS = (4, 2, 4)
        N_EDGES = 524288
        LN_EPS = 1e-05

        def _layernorm(x, g, b):
            mu = x.mean(-1, keepdims=True)
            var = ((x - mu) ** 2).mean(-1, keepdims=True)
            return (x - mu) * jax.lax.rsqrt(var + LN_EPS) * g + b

        def _forward(x, edge_index, W_gat, att_src, att_dst, b_gat, ln_gamma, ln_beta, W1, b1, W2, b2):
            Bc, Nc, Dc = x.shape
            M = Bc * Nc
            x_flat = x.reshape(M, Dc)
            h = (x_flat @ W_gat).reshape(M, HEADS, NUM_EXPERTS)
            loops = jnp.arange(M, dtype=edge_index.dtype)
            src = jnp.concatenate([edge_index[0], loops])
            dst = jnp.concatenate([edge_index[1], loops])
            a_src = (h * att_src).sum(-1)
            a_dst = (h * att_dst).sum(-1)
            e = jax.nn.leaky_relu(a_src[src] + a_dst[dst], negative_slope=0.2)
            e_max = jax.ops.segment_max(e, dst, num_segments=M)
            ee = jnp.exp(e - e_max[dst])
            denom = jax.ops.segment_sum(ee, dst, num_segments=M)
            alpha = ee / (denom[dst] + 1e-16)
            msg = h[src] * alpha[:, :, None]
            agg = jax.ops.segment_sum(msg, dst, num_segments=M).reshape(M, HEADS * NUM_EXPERTS) + b_gat
            scores = _layernorm(agg, ln_gamma, ln_beta).reshape(M, HEADS, NUM_EXPERTS).mean(1)
            scores = scores.reshape(Bc, Nc, NUM_EXPERTS)
            topk_s, topk_i = jax.lax.top_k(scores, TOP_K)
            w = jax.nn.softmax(topk_s, axis=-1)
            out = jnp.zeros_like(x)
            for ei in range(NUM_EXPERTS):
                g = jnp.where(topk_i == ei, w, 0.0).sum(-1)
                hh = jax.nn.gelu(x @ W1[ei] + b1[ei], approximate=False)
                out = out + g[..., None] * (hh @ W2[ei] + b2[ei])
            return out
        return _forward(x, edge_index, W_gat, att_src, att_dst, b_gat, ln_gamma, ln_beta, W1, b1, W2, b2)
    x = x + _L0_gnn_ref(_layernorm(x, axis=-1), L0_gnn_item_feat, adj, L0_gnn_W_item, L0_gnn_b_item, L0_gnn_W_user, L0_gnn_b_user)
    x = x + _L0_ffn_ref(_layernorm(x, axis=-1)[None], L0_ffn_W_gat, L0_ffn_att_src, L0_ffn_att_dst, L0_ffn_b_gat, L0_ffn_ln_gamma, L0_ffn_ln_beta, L0_ffn_W1, L0_ffn_b1, L0_ffn_W2, L0_ffn_b2, L0_ffn_edge_index)[0]
    return x

_drawn_inputs = setup_inputs


def setup_inputs(seed=0):
    import zlib

    import numpy as np

    out = dict(_drawn_inputs(seed))
    spreads = {'L0_ffn_b_gat': (0.0, 0.1),
     'L0_ffn_ln_gamma': (1.0, 0.2),
     'L0_ffn_ln_beta': (0.0, 0.1),
     'L0_ffn_b1': (0.0, 0.31),
     'L0_ffn_b2': (0.0, 0.1)}
    factors = {'L0_ffn_att_dst': 3.573}
    for name, (base, spread) in spreads.items():
        noise = np.random.default_rng([zlib.crc32(name.encode()), seed]).standard_normal(out[name].shape)
        drawn = base * np.exp(spread * noise) if base else spread * noise
        out[name] = jnp.asarray(drawn.astype(out[name].dtype))
    for name, factor in factors.items():
        out[name] = (out[name] * factor).astype(out[name].dtype)
    return out
```

```python
from contextlib import ExitStack

import concourse.bass as bass
from concourse import mybir

ALU = mybir.AluOpType
ACT = mybir.ActivationFunctionType
F32 = mybir.dt.float32
BF16 = mybir.dt.bfloat16
I32 = mybir.dt.int32
AX_X = mybir.AxisListType.X

P = 128
SRC_BITS = 14
LO_BITS = 7
BIG = float(2.0 ** 100)
LN_EPS = 1e-5
G_TAIL_LINKS = 36


def compact_stages(length):
    return [1 << b for b in range((length - 1).bit_length())]


def center(v, link, agg, bias, squares, col, blocks):
    _, _, width = agg.shape
    link(v.tensor_tensor(agg, agg, bias[:, :].unsqueeze(1).broadcast_to([P, blocks, width]), ALU.add))
    link(v.tensor_reduce(col[:, 0, :], agg, AX_X, ALU.add))
    link(v.tensor_scalar(col[:, 0, :], col[:, 0, :], 1.0 / width, None, ALU.mult))
    link(v.tensor_tensor(agg, agg, col[:, 0, :].unsqueeze(2).broadcast_to([P, blocks, width]), ALU.subtract))
    link(v.tensor_tensor(squares[:, :, :], agg, agg, ALU.mult))
    link(v.tensor_reduce(col[:, 1, :], squares[:, :, :], AX_X, ALU.add))
    return v.tensor_scalar(col[:, 2, :], col[:, 1, :], 1.0 / width, LN_EPS, ALU.mult, ALU.add)


def rank_scores(v, link, agg, gamma, beta, col, score, order, cmpb, blocks):
    width, exp = agg.shape[2], score.shape[2]
    heads = width // exp

    def wide(t):
        return t[:, :].unsqueeze(1).broadcast_to([P, blocks, width])

    link(v.reciprocal(col[:, 4, :], col[:, 3, :]))
    link(v.tensor_tensor(agg, agg, col[:, 4, :].unsqueeze(2).broadcast_to([P, blocks, width]), ALU.mult))
    link(v.tensor_tensor(agg, agg, wide(gamma), ALU.mult))
    link(v.tensor_tensor(agg, agg, wide(beta), ALU.add))
    link(v.tensor_reduce(score[:, :, :], agg.rearrange("p b (h k) -> p b k h", h=heads), AX_X, ALU.add))
    link(v.tensor_scalar(score[:, :, :], score[:, :, :], 1.0 / heads, None, ALU.mult))
    link(v.memset(order[:, :, :], 0.0))
    for j in range(exp):
        sj = score[:, :, j:j + 1]
        if j + 1 < exp:
            n = exp - 1 - j
            link(v.tensor_tensor(cmpb[:, :, 0:n], sj.broadcast_to([P, blocks, n]), score[:, :, j + 1:exp], ALU.is_ge))
            link(v.tensor_tensor(order[:, :, j + 1:exp], order[:, :, j + 1:exp], cmpb[:, :, 0:n], ALU.add))
        if j > 0:
            link(v.tensor_tensor(cmpb[:, :, 0:j], sj.broadcast_to([P, blocks, j]), score[:, :, 0:j], ALU.is_gt))
            link(v.tensor_tensor(order[:, :, 0:j], order[:, :, 0:j], cmpb[:, :, 0:j], ALU.add))
    link(v.tensor_reduce(col[:, 0, :], score[:, :, :], AX_X, ALU.max))
    return v.tensor_tensor(cmpb[:, :, :], score[:, :, :],
                           col[:, 0, :].unsqueeze(2).broadcast_to([P, blocks, exp]), ALU.subtract)


def share_gates(v, link, order, gexp, col, gate, blocks):
    exp = order.shape[2]
    link(v.scalar_tensor_tensor(out=gexp[:, :, :], in0=order[:, :, :], scalar=1.5, in1=gexp[:, :, :],
                                op0=ALU.is_lt, op1=ALU.mult))
    link(v.tensor_reduce(col[:, 1, :], gexp[:, :, :], AX_X, ALU.add))
    link(v.reciprocal(col[:, 5, :], col[:, 1, :]))
    return v.tensor_tensor(gate, gexp[:, :, :], col[:, 5, :].unsqueeze(2).broadcast_to([P, blocks, exp]), ALU.mult)


def adj_ffn_kernel(nc, x, adj, item_feat, W_item, b_item, W_user, b_user, W_gat, att_src, att_dst, b_gat,
                   ln_gamma, ln_beta, W1, b1, W2, b2, edge_index, out):
    N, D = x.shape
    NI = item_feat.shape[0]
    E = edge_index.shape[1]
    HEADS, EXP = att_src.shape
    HE = HEADS * EXP
    FF = W1.shape[2]
    ROW = HE + 2 * HEADS

    BATCH = 512
    NB = -(-N // BATCH)
    GR = BATCH // 32
    LAST_ROWS = N - (NB - 1) * BATCH
    KT = NI // P
    QW = KT * 32
    RES = NI - KT * P
    CHUNKS = [7] * 6 + [6] * 6
    assert sum(CHUNKS) == KT
    COFF = [sum(CHUNKS[:c]) for c in range(len(CHUNKS))]
    NCH = len(CHUNKS)
    CW = max(CHUNKS) * 32
    NRAW = 3
    NT = 2
    assert NCH % NRAW == 0 and NCH % NT == 0

    EC = E // P
    VC = 1408
    UC = 512
    NBLK = NB * BATCH // P
    TPB = 6
    CAP = TPB * P
    HG = 8
    OUT_OF_LIST = 131072
    EMPTY = 200 << SRC_BITS
    assert VC % (2 * HG) == 0

    lists = nc.dram_tensor("edge_lists", [NBLK * CAP, 1], I32).ap()
    lanes_dram = nc.dram_tensor("edge_lanes", [NBLK, CAP], BF16).ap()
    valid_dram = nc.dram_tensor("valid_edges", [P, EC], I32).ap()
    unclamped_dram = nc.dram_tensor("unclamped_edges", [P, VC], I32).ap()

    with ExitStack() as ctx:
        def sb(name, shape, dt=F32):
            return ctx.enter_context(nc.sbuf_tensor(name, shape, dt))

        def pb(name, shape, dt=F32):
            return ctx.enter_context(nc.psum_tensor(name, shape, dt))

        ident = sb("ident", [P, P])
        identb = sb("identb", [P, P], BF16)
        negident = sb("negident", [P, P], BF16)
        ones = sb("ones", [P, P])
        iota_lane = sb("iota_lane", [P, P, 24], BF16)
        lane_col = sb("lane_col", [P, 1])
        iota_blk = sb("iota_blk", [P, NBLK])
        clamp_count = sb("clamp_count", [P, NBLK])
        left_count = sb("left_count", [P, 1], I32)

        slot = sb("slot", [P, UC], I32)
        pay = sb("pay", [P, UC], I32)
        w_userT = sb("w_userT", [P, P])
        w_rows = sb("w_rows", [P, ROW])
        bias_user = sb("bias_user", [P, 1])
        h_items = sb("h_items", [P, KT, D])
        h_rest = sb("h_rest", [RES, D])

        prep = ExitStack()
        with prep:
            def psb(name, shape, dt=F32):
                return prep.enter_context(nc.sbuf_tensor(name, shape, dt))

            def sem(name):
                return prep.enter_context(nc.semaphore(name))

            src = psb("src", [P, EC], I32)
            code = psb("code", [P, EC], I32)
            bufA = psb("bufA", [P, EC], I32)
            bufB = psb("bufB", [P, EC], I32)
            bufC = psb("bufC", [P, EC], I32)
            codeB = psb("codeB", [P, VC], I32)
            iota_col = psb("iota_col", [P, VC])
            iota_tail = psb("iota_tail", [P, NBLK, HG], BF16)
            tri = psb("tri", [P, P])
            hot_lane = psb("hot_lane", [P, 2, P, HG], BF16)
            hot_blk = psb("hot_blk", [P, 2, NBLK, HG], BF16)
            lane_bf = psb("lane_bf", [P, VC], BF16)
            blk_bf = psb("blk_bf", [P, VC], BF16)
            nval = psb("nval", [P, 4])
            tot = psb("tot", [P, NBLK])
            base = psb("base", [P, NBLK])
            items = psb("items", [P, KT, D])
            items_rest = psb("items_rest", [RES, D])
            items_t = psb("items_t", [P, 2, 4, P])
            w_in = psb("w_in", [P, 2, D])
            w_itemT = psb("w_itemT", [P, P])
            bias_item = psb("bias_item", [1, 4, D])
            att = psb("att", [P, 2, HE])
            att_w = psb("att_w", [P, 2, HE])
            tr_ps = [prep.enter_context(nc.psum_tensor(f"items_tr{k}", [P, 4, P], F32)) for k in range(2)]
            h_ps = [prep.enter_context(nc.psum_tensor(f"items_h{k}", [P, 4, P], F32)) for k in range(2)]
            empties = psb("empties", [P, NBLK * TPB], I32)
            hist_ps = prep.enter_context(nc.psum_tensor("hist_ps", [P, NBLK], F32))
            base_ps = prep.enter_context(nc.psum_tensor("base_ps", [P, NBLK], F32))

            s_ld = sem("edges_loaded")
            s_const = sem("constants_ready")
            s_pool = sem("pool_step")
            s_dve = sem("vector_step")
            s_hot = sem("onehots_ready")
            s_hist = sem("onehots_used")
            s_z = sem("histogram_cleared")
            s_tot = sem("totals_ready")
            s_base = sem("bases_ready")
            s_left = sem("leftover_ready")
            s_leftp = sem("leftover_summed")
            s_empty = sem("lists_emptied")
            s_slot = sem("slots_ready")
            s_code = sem("codes_ready")
            s_scat = sem("edges_scattered")
            s_save = sem("codes_saved")
            s_w = sem("weights_loaded")
            s_items = sem("items_loaded")
            s_wt = sem("weights_transposed")
            s_wtc = sem("weights_copied")
            s_itr = sem("items_transposed")
            s_itc = sem("items_copied")
            s_hmm = sem("items_projected")
            s_hc = sem("h_copied")
            QUADS = [list(range(q, min(q + 4, KT))) for q in range(0, KT, 4)] + ["rest"]

            block = prep.enter_context(nc.Block())

            @block.sync
            def _(sp):
                e_v = edge_index.rearrange("a (p c) -> a p c", p=P)
                sp.dma_start(code[:, :], e_v[1]).then_inc(s_ld, 16)
                sp.dma_start(src[:, :], e_v[0]).then_inc(s_ld, 16)
                sp.dma_start(w_in[:, 0, :], W_item).then_inc(s_w, 16)
                sp.dma_start(w_in[:, 1, :], W_user).then_inc(s_w, 16)
                for k in range(4):
                    sp.dma_start(bias_item[0:1, k, :], b_item.unsqueeze(0)).then_inc(s_w, 16)
                sp.dma_start(bias_user[:, :], b_user.unsqueeze(1)).then_inc(s_w, 16)
                sp.dma_start(w_rows[:, 0:HE], W_gat).then_inc(s_w, 16)
                for k, a in enumerate((att_src, att_dst)):
                    sp.dma_start(att[:, k, :], a.rearrange("h k -> (h k)").partition_broadcast(P)).then_inc(s_w, 16)
                for q in range(4):
                    sp.dma_start(items[32 * q:32 * q + 32, :, :],
                                 item_feat[QW * q:QW * (q + 1), :].rearrange("(b c) f -> c b f", c=32)
                                 ).then_inc(s_items, 16)
                sp.dma_start(items_rest[:, :], item_feat[KT * P:NI, :]).then_inc(s_items, 16)
                sp.wait_ge(s_const, 1)
                sp.dma_start(lists.rearrange("(p c) a -> p (c a)", p=P), empties[:, :]).then_inc(s_empty, 16)
                sp.wait_ge(s_code, 1)
                sp.dma_start(valid_dram, code[:, :]).then_inc(s_save, 16)
                sp.wait_ge(s_code, 2)
                sp.dma_start(unclamped_dram, codeB[:, :]).then_inc(s_save, 16)
                sp.wait_ge(s_save, 32)

            @block.gpsimd
            def _(pool):
                nc.gpsimd.iota(empties[:, :], [[0, NBLK * TPB]], base=EMPTY, channel_multiplier=0).then_inc(s_pool, 1)
                nc.gpsimd.iota(iota_col[:, :], [[1, VC]], base=0, channel_multiplier=0,
                               allow_small_or_imprecise_dtypes=True).then_inc(s_pool, 1)
                nc.gpsimd.iota(iota_blk[:, :], [[1, NBLK]], base=P, channel_multiplier=0,
                               allow_small_or_imprecise_dtypes=True).then_inc(s_pool, 1)
                nc.gpsimd.iota(iota_tail[:, :, :], [[1, NBLK], [0, HG]], base=P, channel_multiplier=0,
                               allow_small_or_imprecise_dtypes=True).then_inc(s_pool, 1)
                nc.gpsimd.iota(iota_lane[:, :, :], [[1, P], [0, 24]], base=0, channel_multiplier=0,
                               allow_small_or_imprecise_dtypes=True).then_inc(s_pool, 1)
                nc.gpsimd.iota(lane_col[:, :], [[0, 1]], base=0, channel_multiplier=1,
                               allow_small_or_imprecise_dtypes=True).then_inc(s_pool, 1)
                nc.gpsimd.memset(ones[:, :], 1.0).then_inc(s_pool, 1)
                nc.gpsimd.memset(ident[:, :], 0.0).then_inc(s_pool, 1)
                nc.gpsimd.memset(identb[:, :], 0.0).then_inc(s_pool, 1)
                nc.gpsimd.memset(negident[:, :], 0.0).then_inc(s_pool, 1)
                pool.wait_ge(s_pool, 10)
                for m, v in ((ident, 1.0), (identb, 1.0), (negident, -BIG)):
                    nc.gpsimd.affine_select(out=m[:, :], in_=m[:, :], compare_op=ALU.not_equal, fill=v, base=0,
                                            pattern=[[-1, P]], channel_multiplier=1).then_inc(s_pool, 1)
                nc.gpsimd.affine_select(out=tri[:, :], in_=ones[:, :], compare_op=ALU.is_gt, fill=0.0, base=0,
                                        pattern=[[1, P]], channel_multiplier=-1).then_inc(s_pool, 1)
                pool.wait_ge(s_pool, 14)
                pool.nop().then_inc(s_const, 1)
                pool.wait_ge(s_empty, 16)

            @block.tensor
            def _(pe):
                pe.wait_ge(s_const, 1)
                pe.wait_ge(s_w, 16 * 10)
                for k in range(2):
                    nc.tensor.transpose(h_ps[0][:, k, :], w_in[:, k, :], ident[:, :]).then_inc(s_wt, 1)
                pe.wait_ge(s_items, 16 * 5)
                pe.wait_ge(s_wtc, 2)

                def turn(n):
                    if n >= 2:
                        pe.wait_ge(s_itc, n - 1)
                    if QUADS[n] == "rest":
                        mm = nc.tensor.transpose(tr_ps[n % 2][:, 0, 0:RES], items_rest[:, :], ident[0:RES, 0:RES])
                    else:
                        for k, b in enumerate(QUADS[n]):
                            mm = nc.tensor.transpose(tr_ps[n % 2][:, k, :], items[:, b, :], ident[:, :])
                    mm.then_inc(s_itr, 1)

                turn(0)
                for n, quad in enumerate(QUADS):
                    if n + 1 < len(QUADS):
                        turn(n + 1)
                    pe.wait_ge(s_itc, n + 1)
                    if n >= 2:
                        pe.wait_ge(s_hc, n - 1)
                    m = RES if quad == "rest" else P
                    nc.tensor.matmul(h_ps[n % 2][0:m, :, :], ones[0:1, 0:m], bias_item[0:1, :, :], start=True,
                                     stop=False, skip_group_check=True)
                    for k in range(1 if quad == "rest" else len(quad)):
                        mm = nc.tensor.matmul(h_ps[n % 2][0:m, k, :], items_t[:, n % 2, k, 0:m], w_itemT[:, :],
                                              start=False, stop=True, skip_group_check=True)
                    mm.then_inc(s_hmm, 1)
                pe.wait_ge(s_z, 1)
                nc.tensor.matmul(hist_ps[:, :], hot_lane[:, 0, :, 0], hot_blk[:, 0, :, 0], start=True, stop=False,
                                 skip_group_check=True).then_inc(s_hist, 1)
                with pe.Fori(0, VC // (2 * HG)) as g:
                    for half in range(2):
                        pe.wait_ge(s_hot, g * 2 + half + 1)
                        for j in range(HG):
                            mm = nc.tensor.matmul(hist_ps[:, :], hot_lane[:, half, :, j], hot_blk[:, half, :, j],
                                                  start=False, stop=False, skip_group_check=True)
                        mm.then_inc(s_hist, 1)
                pe.wait_ge(s_tot, 1)
                nc.tensor.matmul(base_ps[:, :], tri[:, :], tot[:, :], start=True, stop=True).then_inc(s_base, 1)
                pe.wait_ge(s_left, 1)
                nc.tensor.matmul(base_ps[:, 0:1], ones[:, :], nval[:, 3:4], start=True, stop=True).then_inc(s_leftp, 1)

            @block.scalar
            def _(act):
                act.wait_ge(s_wt, 2)
                nc.scalar.activation(w_itemT[:, :], h_ps[0][:, 0, :], ACT.Copy).then_inc(s_wtc, 1)
                nc.scalar.activation(w_userT[:, :], h_ps[0][:, 1, :], ACT.Copy).then_inc(s_wtc, 1)
                for n in range(len(QUADS) + 1):
                    if n < len(QUADS):
                        act.wait_ge(s_itr, n + 1)
                        if n >= 2:
                            act.wait_ge(s_hmm, n - 1)
                        if QUADS[n] == "rest":
                            nc.scalar.activation(items_t[:, n % 2, 0, 0:RES], tr_ps[n % 2][:, 0, 0:RES],
                                                 ACT.Copy).then_inc(s_itc, 1)
                        else:
                            w = len(QUADS[n])
                            nc.scalar.activation(items_t[:, n % 2, 0:w, :], tr_ps[n % 2][:, 0:w, :],
                                                 ACT.Copy).then_inc(s_itc, 1)
                    if n >= 1:
                        act.wait_ge(s_hmm, n)
                        quad = QUADS[n - 1]
                        if quad == "rest":
                            nc.scalar.activation(h_rest[:, :], h_ps[(n - 1) % 2][0:RES, 0, :],
                                                 ACT.Copy).then_inc(s_hc, 1)
                        else:
                            nc.scalar.activation(h_items[:, quad[0]:quad[0] + len(quad), :],
                                                 h_ps[(n - 1) % 2][:, 0:len(quad), :], ACT.Copy).then_inc(s_hc, 1)

            @block.vector
            def _(dve):
                n = [0]
                v = nc.vector

                def link(ins):
                    n[0] += 1
                    ins.then_inc(s_dve, 1)
                    dve.wait_ge(s_dve, n[0])

                def compact(key, shift, length, spare, marks):
                    for step in compact_stages(length):
                        m = length - step
                        link(v.tensor_scalar(marks, shift, step, None, ALU.bitwise_and))
                        link(v.scalar_tensor_tensor(out=spare, in0=marks, scalar=0.0, in1=shift,
                                                    op0=ALU.is_equal, op1=ALU.mult))
                        link(v.copy_predicated(spare[:, 0:m], marks[:, step:length], shift[:, step:length]))
                        link(v.copy_predicated(key[:, 0:m], marks[:, step:length], key[:, step:length]))
                        spare, shift = shift, spare

                dve.wait_ge(s_w, 16 * 10)
                for k in range(2):
                    link(v.tensor_tensor(att_w[:, k, :], w_rows[:, 0:HE], att[:, k, :], ALU.mult))
                    link(v.tensor_reduce(w_rows[:, HE + HEADS * k:HE + HEADS * (k + 1)],
                                         att_w[:, k, :].rearrange("p (h k) -> p h k", h=HEADS), AX_X, ALU.add))

                dve.wait_ge(s_ld, 32)
                holes = bufB[:, :].bitcast(F32)
                invalid = bufA[:, :].bitcast(F32)
                link(v.tensor_scalar(invalid, code[:, :], float(N), None, ALU.is_ge))
                link(v.tensor_tensor_scan(holes, invalid, invalid, 0.0, ALU.add, ALU.max))
                link(v.scalar_tensor_tensor(out=bufC[:, :], in0=invalid, scalar=0.0, in1=holes,
                                            op0=ALU.is_equal, op1=ALU.mult))
                link(v.tensor_scalar(nval[:, 0:1], holes[:, EC - 1:EC], -1.0, float(EC), ALU.mult, ALU.add))
                link(v.tensor_scalar(src[:, :], src[:, :], float(N - 1), None, ALU.min))
                link(v.tensor_scalar(code[:, :], code[:, :], SRC_BITS, None, ALU.logical_shift_left))
                link(v.tensor_tensor(code[:, :], code[:, :], src[:, :], ALU.bitwise_or))
                compact(code[:, :], bufC[:, :], EC, bufB[:, :], bufA[:, :])
                v.nop().then_inc(s_code, 1)

                dve.wait_ge(s_const, 1)
                third = [b[:, k * VC:(k + 1) * VC] for b in (bufA, bufB, bufC) for k in range(2)]
                kept = code[:, 0:VC]
                dst_i, src_i, lane_i, blk_i = third[0], third[1], third[2], third[3]
                live, clamped = third[4].bitcast(F32), third[5].bitcast(F32)
                loose = src[:, 0:VC].bitcast(F32)
                link(v.tensor_scalar(dst_i, kept, SRC_BITS, None, ALU.logical_shift_right))
                link(v.tensor_scalar(dst_i, dst_i, float(N), None, ALU.min))
                link(v.tensor_scalar(src_i, kept, (1 << SRC_BITS) - 1, None, ALU.bitwise_and))
                link(v.tensor_scalar(live, iota_col[:, :], nval[:, 0:1], None, ALU.is_lt))
                link(v.scalar_tensor_tensor(out=clamped, in0=src_i, scalar=float(N - 1), in1=live,
                                            op0=ALU.is_ge, op1=ALU.mult))
                link(v.scalar_tensor_tensor(out=loose, in0=src_i, scalar=float(N - 1), in1=live,
                                            op0=ALU.is_lt, op1=ALU.mult))
                link(v.tensor_scalar(lane_i, dst_i, P - 1, None, ALU.bitwise_and))
                link(v.tensor_scalar(blk_i, dst_i, LO_BITS, None, ALU.logical_shift_right))
                link(v.tensor_copy(lane_bf[:, :], lane_i))
                link(v.scalar_tensor_tensor(out=blk_bf[:, :], in0=clamped, scalar=float(P), in1=blk_i,
                                            op0=ALU.mult, op1=ALU.add))

                link(v.memset(hot_lane[:, 0, :, 0], 0.0))
                link(v.memset(hot_blk[:, 0, :, 0], 0.0))
                v.nop().then_inc(s_z, 1)
                with dve.Fori(0, VC // (2 * HG)) as g:
                    for half in range(2):
                        dve.wait_ge(s_hist, g * 2 + (half + 1 if half == 0 else 1))
                        at = (g * 2 + half) * HG
                        lanes = lane_bf[:, bass.ds(at, HG)].unsqueeze(1)
                        blks = blk_bf[:, bass.ds(at, HG)].unsqueeze(1)
                        v.tensor_tensor(hot_lane[:, half, :, :], lanes.broadcast_to([P, P, HG]),
                                        iota_lane[:, :, 0:HG], ALU.is_equal)
                        v.tensor_tensor(hot_blk[:, half, :, :], blks.broadcast_to([P, NBLK, HG]),
                                        iota_tail[:, :, :], ALU.is_equal).then_inc(s_hot, 1)
                dve.wait_ge(s_hist, 1 + VC // HG)
                link(v.tensor_copy(clamp_count[:, :], hist_ps[:, :]))

                fixed, holes2 = third[0].bitcast(F32), third[2].bitcast(F32)
                shift2, marks2 = third[4], third[1]
                link(v.tensor_scalar(fixed, loose, 0.0, None, ALU.is_equal))
                link(v.tensor_tensor_scan(holes2, fixed, fixed, 0.0, ALU.add, ALU.max))
                link(v.tensor_tensor(shift2, loose, holes2, ALU.mult))
                link(v.tensor_scalar(nval[:, 1:2], holes2[:, VC - 1:VC], -1.0, float(VC), ALU.mult, ALU.add))
                link(v.tensor_copy(codeB[:, :], kept))
                compact(codeB[:, :], shift2, VC, third[2], marks2)
                v.nop().then_inc(s_code, 1)

                c = [b[:, k * UC:(k + 1) * UC] for b in (bufA, bufB) for k in range(8)]
                blk_of, live2, same, count = (c[k].bitcast(F32) for k in range(4))
                rank, keep = c[4].bitcast(F32), c[5].bitcast(F32)
                short = codeB[:, 0:UC]
                link(v.tensor_scalar(pay[:, :], short, (1 << (SRC_BITS + LO_BITS)) - 1, None, ALU.bitwise_and))
                link(v.tensor_scalar(c[6], short, SRC_BITS + LO_BITS, None, ALU.logical_shift_right))
                link(v.tensor_scalar(c[6], c[6], float(NBLK - 1), None, ALU.min))
                link(v.tensor_scalar(live2, iota_col[:, 0:UC], nval[:, 1:2], None, ALU.is_lt))
                link(v.scalar_tensor_tensor(out=blk_of, in0=live2, scalar=float(P), in1=c[6],
                                            op0=ALU.mult, op1=ALU.add))
                link(v.memset(rank, 0.0))
                for b in range(NBLK):
                    link(v.tensor_scalar(same, blk_of, iota_blk[:, b:b + 1], None, ALU.is_equal, ALU.add,
                                         accum_out=tot[:, b:b + 1]))
                v.nop().then_inc(s_tot, 1)
                dve.wait_ge(s_base, 1)
                link(v.tensor_copy(base[:, :], base_ps[:, :]))
                for b in range(NBLK):
                    link(v.tensor_scalar(same, blk_of, iota_blk[:, b:b + 1], None, ALU.is_equal))
                    link(v.tensor_tensor_scan(count, same, same, base[:, b:b + 1], ALU.add, ALU.max))
                    link(v.copy_predicated(rank, same.bitcast(I32), count))
                link(v.scalar_tensor_tensor(out=keep, in0=rank, scalar=float(CAP), in1=live2,
                                            op0=ALU.is_le, op1=ALU.mult))
                link(v.tensor_tensor_scan(count, live2, keep, 0.0, ALU.add, ALU.subtract))
                link(v.scalar_tensor_tensor(out=same, in0=blk_of, scalar=float(CAP), in1=rank,
                                            op0=ALU.mult, op1=ALU.add))
                link(v.tensor_scalar(same, same, float(-(P * CAP + 1 + OUT_OF_LIST)), None, ALU.add))
                link(v.tensor_tensor(same, same, keep, ALU.mult))
                link(v.tensor_scalar(slot[:, :], same, float(OUT_OF_LIST), None, ALU.add))
                v.nop().then_inc(s_slot, 1)
                link(v.tensor_scalar(nval[:, 0:1], nval[:, 0:1], float(-VC), 0.0, ALU.add, ALU.max))
                link(v.tensor_scalar(nval[:, 1:2], nval[:, 1:2], float(-UC), 0.0, ALU.add, ALU.max))
                link(v.tensor_tensor(nval[:, 2:3], nval[:, 0:1], nval[:, 1:2], ALU.add))
                link(v.tensor_tensor(nval[:, 3:4], nval[:, 2:3], count[:, UC - 1:UC], ALU.add))
                v.nop().then_inc(s_left, 1)
                dve.wait_ge(s_leftp, 1)
                link(v.tensor_copy(left_count[:, :], base_ps[:, 0:1]))

        x1_dram = nc.dram_tensor("x1_rows", [NB * BATCH, D], F32).ap()
        yT_dram = nc.dram_tensor("normed_columns", [NB, P, BATCH], F32).ap()
        table = nc.dram_tensor("node_table", [NB * BATCH, ROW], F32).ap()
        one = ExitStack()
        with one:
            def osb(name, shape, dt=F32):
                return one.enter_context(nc.sbuf_tensor(name, shape, dt))

            def sem(name):
                return one.enter_context(nc.semaphore(name))

            raw = osb("raw", [P, NRAW, GR * CW])
            turned = osb("turned", [P, NT, GR * CW])
            raw_rest = osb("raw_rest", [32, GR, 32])
            turned_rest = osb("turned_rest", [32, GR, 32])
            xt = osb("xt", [P, 2, 4, D])
            u = osb("u", [P, 4, D])
            uT = osb("uT", [P, BATCH])
            rT = osb("rT", [P, BATCH])
            x1 = osb("x1", [P, 2, 4, D])
            y = osb("y", [P, 4, D])
            yT = osb("yT", [P, BATCH])
            rows = osb("rows", [P, 2, 4, ROW])
            stats = osb("stats", [P, 2, 4, 6])
            meanvar = osb("meanvar", [P, 2, 4, 2])
            dev = osb("dev", [P, 2, 4])
            rdev = osb("rdev", [P, 2, 4])
            acc = [one.enter_context(nc.psum_tensor(f"acc{k}", [P, BATCH], F32)) for k in range(2)]
            u_ps = one.enter_context(nc.psum_tensor("u_ps", [P, 4, P], F32))
            r_ps = one.enter_context(nc.psum_tensor("r_ps", [P, 4, P], F32))
            y_ps = one.enter_context(nc.psum_tensor("y_ps", [P, 4, P], F32))
            row_ps = one.enter_context(nc.psum_tensor("row_ps", [P, 4, ROW], F32))

            s_raw = [sem(f"adj_loaded{k}") for k in range(NRAW)]
            s_turn = sem("adj_turned")
            s_mm = sem("chunk_multiplied")
            s_rawr = sem("rest_loaded")
            s_turnr = sem("rest_turned")
            s_mmr = sem("rest_multiplied")
            s_x = [sem(f"x_loaded{k}") for k in range(2)]
            s_var = sem("variances_ready")
            s_dev = sem("deviations_ready")
            s_u = sem("u_ready")
            s_ut = sem("u_turned")
            s_utc = sem("uT_copied")
            s_wu = sem("batch_multiplied")
            s_relu = sem("relu_done")
            s_rt = sem("r_turned")
            s_x1 = sem("x1_ready")
            s_y = sem("y_ready")
            s_yt = sem("y_turned")
            s_ytc = sem("yT_copied")
            s_row = sem("rows_projected")
            s_rowc = sem("rows_copied")
            s_x1st = [sem(f"x1_stored{k}") for k in range(2)]
            s_ytst = sem("yT_stored")
            s_rowst = [sem(f"rows_stored{k}") for k in range(2)]
            s_dve = sem("vector_step")
            s_scat = sem("edges_scattered")
            s_zero = sem("rest_cleared")
            s_past = sem("waits_passed")

            def wait(eng, s, value):
                if not isinstance(value, int) or value > 0:
                    eng.wait_ge(s, value)

            def wait_alone(eng, s, value):
                wait(eng, s, value)
                if not isinstance(value, int):
                    eng.nop().then_inc(s_past, 1)

            def batches(eng, body, tail=None):
                for i in range(3):
                    body(i, i % 2)
                with eng.Fori(0, (NB - 4) // 2) as k:
                    body(k * 2 + 3, 1)
                    body(k * 2 + 4, 0)
                body(NB - 1, 1)
                if tail is not None:
                    tail(NB, 0)

            def half(i, par):
                return i // 2 if isinstance(i, int) else (i - par) // 2

            block = one.enter_context(nc.Block())

            @block.gpsimd
            def _(pool):
                for j in range(UC):
                    nc.gpsimd.indirect_dma_start(
                        lists, bass.IndirectOffsetOnAxis(ap=slot[:, j:j + 1], axis=0), pay[:, j:j + 1], None,
                        bounds_check=NBLK * CAP - 1, oob_is_err=False).then_inc(s_scat, 16)
                pool.wait_ge(s_scat, 16 * UC)


            @block.sync
            def _(sp):
                def body(i, par):
                    last = isinstance(i, int) and i == NB - 1
                    n_rows = LAST_ROWS if last else BATCH
                    whole, over = divmod(n_rows, 32)
                    u0 = i * BATCH

                    def load_rows(dst, cols, signal):
                        src = adj[bass.ds(u0, 32 * whole), cols] if not isinstance(u0, int) else adj[u0:u0 + 32 * whole, cols]
                        sp.dma_start(dst[:, 0:whole, :], src.rearrange("(g r) c -> r g c", r=32)).then_inc(signal, 16)
                        if over:
                            sp.dma_start(dst[0:over, whole, :], adj[u0 + 32 * whole:u0 + n_rows, cols]).then_inc(signal, 16)

                    def rows_of(t, n, i):
                        at = i * BATCH
                        return t[at:at + n, :] if isinstance(at, int) else t[bass.ds(at, n), :]

                    if isinstance(i, int) and i == 0:
                        sp.wait_ge(s_zero, 1)
                    wait_alone(sp, s_x1, i - 1)
                    whole_x, over_x = divmod(n_rows, P)
                    sp.dma_start(xt[:, par, 0:whole_x, :],
                                 rows_of(x, whole_x * P, i).rearrange("(t p) f -> p t f", p=P)).then_inc(s_x[par], 16)
                    if over_x:
                        sp.dma_start(xt[0:over_x, par, whole_x, :], x[u0 + whole_x * P:u0 + n_rows, :]
                                     ).then_inc(s_x[par], 16)
                    wait_alone(sp, s_turnr, i)
                    load_rows(raw_rest[:, :, 0:RES], slice(KT * P, NI), s_rawr)
                    for c, nb in enumerate(CHUNKS):
                        wait_alone(sp, s_turn, i * NCH + c - NRAW + 1)
                        for q in range(4):
                            c0 = QW * q + 32 * COFF[c]
                            load_rows(raw[32 * q:32 * q + 32, c % NRAW, 0:GR * 32 * nb].rearrange(
                                "p (g w) -> p g w", g=GR), slice(c0, c0 + 32 * nb), s_raw[c % NRAW])

                batches(sp, body)

            @block.tensor
            def _(pe):
                def turn_r(i):
                    pe.wait_ge(s_relu, i)
                    wait(pe, s_x1, i - 1)
                    for k in range(4):
                        mm = nc.tensor.transpose(r_ps[:, k, :], rT[:, k * P:(k + 1) * P], ident[:, :])
                    mm.then_inc(s_rt, 1)

                def turn_y(i):
                    pe.wait_ge(s_y, i)
                    wait(pe, s_ytc, i - 1)
                    for k in range(4):
                        mm = nc.tensor.transpose(y_ps[:, k, :], y[:, k, :], ident[:, :])
                    mm.then_inc(s_yt, 1)

                def project(i):
                    pe.wait_ge(s_ytc, i)
                    wait(pe, s_rowc, i - 1)
                    for k in range(4):
                        mm = nc.tensor.matmul(row_ps[:, k, :], yT[:, k * P:(k + 1) * P], w_rows[:, :],
                                              start=(k == 0), stop=True, skip_group_check=True)
                    mm.then_inc(s_row, 1)

                def body(i, par):
                    first = isinstance(i, int) and i == 0
                    wait(pe, s_relu, i - 1)
                    pe.wait_ge(s_turnr, i + 1)
                    nc.tensor.matmul(acc[par][:, :], h_rest[:, :], turned_rest[0:RES, :, :], start=True, stop=False,
                                     skip_group_check=True).then_inc(s_mmr, 1)
                    for c, nb in enumerate(CHUNKS):
                        pe.wait_ge(s_turn, i * NCH + c + 1)
                        t = turned[:, c % NT, 0:GR * 32 * nb].rearrange("p (g b r) -> p g b r", g=GR, b=nb)
                        for b in range(nb):
                            mm = nc.tensor.matmul(acc[par][:, :], h_items[:, COFF[c] + b, :], t[:, :, b, :],
                                                  start=False, stop=False, skip_group_check=True)
                        mm.then_inc(s_mm, 1)
                        if c == 1 and not first:
                            turn_r(i)
                        if c == 4:
                            pe.wait_ge(s_u, i + 1)
                            wait(pe, s_utc, i)
                            for k in range(4):
                                mm = nc.tensor.transpose(u_ps[:, k, :], u[:, k, :], ident[:, :])
                            mm.then_inc(s_ut, 1)
                        if c == 7 and not first:
                            turn_y(i)
                        if c == 9 and not first:
                            project(i)
                    pe.wait_ge(s_utc, i + 1)
                    nc.tensor.matmul(acc[par][:, :], w_userT[:, :], uT[:, :], start=False, stop=True,
                                     skip_group_check=True).then_inc(s_wu, 1)

                def tail(i, par):
                    turn_r(i)
                    turn_y(i)
                    project(i)

                batches(pe, body, tail)

            @block.scalar
            def _(act):
                def relu(i, par):
                    act.wait_ge(s_wu, i)
                    wait(act, s_rt, i - 1)
                    nc.scalar.activation(rT[:, :], acc[par][:, :], ACT.Relu, bias=bias_user[:, 0:1]).then_inc(s_relu, 1)

                def root(which, value):
                    act.wait_ge(s_var, value)
                    nc.scalar.activation(dev[:, which, :], meanvar[:, which, :, 1], ACT.Sqrt).then_inc(s_dev, 1)

                def finish(i, par):
                    act.wait_ge(s_yt, i)
                    wait(act, s_row, i - 1)
                    wait(act, s_ytst, (i - 1) * 16)
                    nc.scalar.activation(yT[:, :], y_ps[:, :, :], ACT.Copy).then_inc(s_ytc, 1)
                    act.wait_ge(s_ytc, i)
                    act.dma_start(yT_dram[i - 1] if isinstance(i, int) else
                                  yT_dram[bass.ds(i - 1, 1)].rearrange("a p c -> p (a c)"), yT[:, :]).then_inc(s_ytst, 16)
                    act.wait_ge(s_row, i)
                    wait(act, s_rowst[par], half(i - 1, par) * 16)
                    nc.scalar.activation(rows[:, par, :, :], row_ps[:, :, :], ACT.Copy).then_inc(s_rowc, 1)
                    act.wait_ge(s_rowc, i)
                    act.dma_start(dram_rows(table, i), rows[:, par, :, :]).then_inc(s_rowst[par], 16)

                def dram_rows(t, i):
                    at = (i - 1) * BATCH
                    r = t[at:at + BATCH, :] if isinstance(at, int) else t[bass.ds(at, BATCH), :]
                    return r.rearrange("(t p) f -> p t f", p=P)

                def body(i, par):
                    first = isinstance(i, int) and i == 0
                    if not first:
                        relu(i, 1 - par)
                    root(0, i * 2 + (1 if first else 0) if first else i * 2)
                    act.wait_ge(s_ut, i + 1)
                    wait(act, s_wu, i)
                    nc.scalar.activation(uT[:, :], u_ps[:, :, :], ACT.Copy).then_inc(s_utc, 1)
                    if not first:
                        root(1, i * 2 + 1)
                        act.wait_ge(s_x1, i)
                        act.dma_start(dram_rows(x1_dram, i), x1[:, 1 - par, :, :]).then_inc(s_x1st[1 - par], 16)
                        finish(i, 1 - par)

                def tail(i, par):
                    relu(i, 1)
                    root(1, i * 2)
                    act.wait_ge(s_x1, i)
                    act.dma_start(dram_rows(x1_dram, i), x1[:, 1, :, :]).then_inc(s_x1st[1], 16)
                    finish(i, 1)
                    for k in range(2):
                        act.wait_ge(s_x1st[k], NB // 2 * 16)
                        act.wait_ge(s_rowst[k], NB // 2 * 16)
                    act.wait_ge(s_ytst, NB * 16)

                batches(act, body, tail)

            @block.vector
            def _(dve):
                v = nc.vector
                LINKS = 13
                at = [0, 0]

                def link(ins):
                    at[1] += 1
                    ins.then_inc(s_dve, 1)
                    dve.wait_ge(s_dve, at[0] + at[1])

                def spread(src, which):
                    for k in range(4):
                        ins = v.bn_stats(stats[:, which, k, :], src[:, k, :])
                    at[1] += 1
                    ins.then_inc(s_dve, 1)
                    wait_alone(dve, s_dve, at[0] + at[1])
                    for k in range(4):
                        ins = v.bn_aggr(meanvar[:, which, k, :], stats[:, which, k, :])
                    link(ins)
                    v.tensor_scalar(meanvar[:, which, :, 1], meanvar[:, which, :, 1], LN_EPS, None,
                                    ALU.add).then_inc(s_var, 1)

                def normalize(dst, src, which, value):
                    dve.wait_ge(s_dev, value)
                    link(v.reciprocal(rdev[:, which, :], dev[:, which, :]))
                    for k in range(4):
                        ins = v.tensor_scalar(dst[:, k, :], src[:, k, :], meanvar[:, which, k, 0:1],
                                              rdev[:, which, k:k + 1], ALU.subtract, ALU.mult)
                    return ins

                def x1_stats(i, par):
                    dve.wait_ge(s_rt, i)
                    wait(dve, s_x1st[par], half(i - 1, par) * 16)
                    ins = v.tensor_tensor(x1[:, par, :, :], r_ps[:, :, :], xt[:, par, :, :], ALU.add)
                    ins.then_inc(s_x1, 1)
                    dve.wait_ge(s_x1, i)
                    spread(x1[:, par, :, :], 1)

                def y_norm(i, par, value):
                    wait(dve, s_yt, i - 1)
                    normalize(y, x1[:, par, :, :], 1, value).then_inc(s_y, 1)

                def body(i, par):
                    first = isinstance(i, int) and i == 0
                    at[0], at[1] = (0, 0) if first else ((i - 1) * 6 + 3, 0)
                    last = isinstance(i, int) and i == NB - 1
                    if first:
                        v.memset(xt[:, :, :, :], 0.0)
                        v.memset(raw_rest[:, :, :], 0.0).then_inc(s_zero, 1)
                    wait(dve, s_mmr, i)
                    dve.wait_ge(s_rawr, 32 * 0 + (i + 1) * 16 + (16 if last else 0))
                    v.transpose(turned_rest[:, :, :].rearrange("p g r -> p (g r)"),
                                raw_rest[:, :, :].rearrange("p g r -> p (g r)")).then_inc(s_turnr, 1)
                    for c, nb in enumerate(CHUNKS):
                        n = GR * 32 * nb
                        wait(dve, s_mm, i * NCH + c - NT + 1)
                        extra = 64 * (c // NRAW + 1) if last else 0
                        dve.wait_ge(s_raw[c % NRAW], (i * (NCH // NRAW) + c // NRAW + 1) * 64 + extra)
                        v.transpose(turned[:, c % NT, 0:n], raw[:, c % NRAW, 0:n]).then_inc(s_turn, 1)
                        if c == 1:
                            dve.wait_ge(s_x[par], half(i, par) * 16 + 16 + (16 if last else 0))
                            spread(xt[:, par, :, :], 0)
                        if c == 2:
                            wait(dve, s_ut, i)
                            normalize(u, xt[:, par, :, :], 0, 1 if first else i * 2).then_inc(s_u, 1)
                        if c == 4 and not first:
                            x1_stats(i, 1 - par)
                        if c == 5 and not first:
                            y_norm(i, 1 - par, i * 2 + 1)

                def tail(i, par):
                    at[0], at[1] = (NB - 1) * 6 + 3, 0
                    x1_stats(i, 1)
                    y_norm(i, 1, i * 2)

                batches(dve, body, tail)

        UB = BATCH // P
        UT = UB * TPB
        TRI = 3
        NTRI = UT // TRI
        PARTS = 3
        HALVES = FF // P
        NF = EXP * HALVES
        TP8 = 8
        two = ExitStack()
        with two:
            def tsb(name, shape, dt=F32):
                return two.enter_context(nc.sbuf_tensor(name, shape, dt))

            def sem(name):
                return two.enter_context(nc.semaphore(name))

            entry = tsb("entry", [P, NBLK, TPB], I32)
            source = tsb("source", [P, NBLK * TPB], I32)
            source_now = tsb("source_now", [P, 2, UT], I32)
            lane_i = tsb("lane_i", [P, NBLK * TPB], I32)
            lane_e = tsb("lane_e", [P, NBLK * TPB], BF16)
            list_rows = tsb("list_rows", [NBLK, CAP], I32)
            lane_rows = tsb("lane_rows", [NBLK, CAP], BF16)
            nodes = tsb("nodes", [P, NBLK, ROW])
            last_row = tsb("last_row", [P, ROW])
            no_clamp = tsb("no_clamp", [P, NBLK])
            floor_max = tsb("floor_max", [P, NBLK, HEADS])
            e_self = tsb("e_self", [P, NBLK, 2, HEADS])
            part_sel = tsb("part_sel", [PARTS * HEADS, HEADS, P], BF16)
            b2_row = tsb("b2_row", [1, EXP * D])
            b2_res = tsb("b2_res", [1, EXP * D])
            b2_cut = tsb("b2_cut", [1, PARTS, EXP * D], BF16)
            b2_parts = tsb("b2_parts", [PARTS, EXP * D], BF16)
            onesb = tsb("onesb", [PARTS, P], BF16)
            w1_sb = tsb("w1_sb", [P, EXP, FF])
            w2_sb = tsb("w2_sb", [P, EXP, HALVES, D])
            b1_sb = tsb("b1_sb", [P, EXP, HALVES])
            bg = tsb("bg", [P, HE])
            gamma = tsb("gamma", [P, HE])
            beta = tsb("beta", [P, HE])

            gath = tsb("gath", [P, 2, UT, ROW])
            lane_bc = tsb("lane_bc", [P, 2, UB * CAP], BF16)
            yTu = tsb("yTu", [P, 2, BATCH])
            x1u = tsb("x1u", [P, 2, UB, D])
            as_cut = tsb("as_cut", [P, UT, PARTS, HEADS], BF16)
            as_res = tsb("as_res", [P, UT, HEADS])
            asT = tsb("asT", [PARTS * HEADS, UT * P], BF16)
            maskT = tsb("maskT", [P, UT, P], BF16)
            hotT = tsb("hotT", [P, UT, P], BF16)
            hot = tsb("hot", [P, P, UT], BF16)
            junk = tsb("junk", [P, 2, TRI * P], BF16)
            mx = tsb("mx", [P, UB, 2, HEADS])
            am = tsb("am", [P, UB, 2 * HEADS])
            tmp4 = tsb("tmp4", [P, UB, HEADS])
            am_cut = tsb("am_cut", [P, UB, PARTS, 2 * HEADS], BF16)
            am_res = tsb("am_res", [P, UB, 2 * HEADS])
            am_e = tsb("am_e", [P, UT, 2 * HEADS])
            logit = tsb("logit", [P, UT + 2 * UB, HEADS])
            weight = tsb("weight", [P, UT + 2 * UB, HEADS])
            pay_e = tsb("pay_e", [P, UT, HE + HEADS])
            pay_cut = tsb("pay_cut", [P, UT, PARTS, HE + HEADS], BF16)
            pay_res = tsb("pay_res", [P, UT, HE + HEADS])
            nd = tsb("nd", [P, UB, HE + HEADS])
            tmp16 = tsb("tmp16", [P, UB, HE])
            tmp16b = tsb("tmp16b", [P, UB, HE])
            col = tsb("col", [P, 6, UB])
            score = tsb("score", [P, UB, EXP])
            cmpb = tsb("cmpb", [P, UB, EXP])
            order = tsb("order", [P, UB, EXP])
            gexp = tsb("gexp", [P, UB, EXP])
            gate = tsb("gate", [P, 2, UB, EXP])
            hidden = tsb("hidden", [P, NF, BATCH])

            hid_ps = [two.enter_context(nc.psum_tensor(f"hid{k}", [P, BATCH], F32)) for k in range(2)]
            out_ps = [two.enter_context(nc.psum_tensor(f"experts{k}", [P, EXP, D], F32)) for k in range(2)]
            as_ps = [two.enter_context(nc.psum_tensor(f"as_rows{k}", [P, TRI * P], F32)) for k in range(2)]
            misc_ps = two.enter_context(nc.psum_tensor("misc", [P, 512], F32))
            agg_ps = two.enter_context(nc.psum_tensor("agg", [P, UB, PARTS, HE + HEADS], F32))

            s_in = sem("setup_loaded")
            s_rows2 = sem("lane_rows_ready")
            s_lanes = sem("lane_rows_stored")
            s_b2 = sem("b2_parts_ready")
            s_b2m = sem("b2_parts_moved")
            s_src = sem("sources_ready")
            s_sel = sem("selectors_ready")
            s_past = sem("waits_passed")
            s_idx = sem("indices_copied")
            s_gath = [sem(f"rows_gathered{k}") for k in range(2)]
            s_bc = [sem(f"lanes_spread{k}") for k in range(2)]
            s_y2 = [sem(f"y_loaded{k}") for k in range(2)]
            s_x2 = [sem(f"x1_loaded{k}") for k in range(2)]
            s_ast = sem("as_cut_ready")
            s_tp = sem("as_turned")
            s_tpc = sem("as_copied")
            s_as = sem("as_spread")
            s_mx = sem("maxima_taken")
            s_am = sem("am_ready")
            s_ame = sem("am_spread")
            s_amr = sem("am_read")
            s_log = sem("logits_ready")
            s_exp = sem("weights_ready")
            s_pay = sem("payload_ready")
            s_agg = sem("payload_summed")
            s_sq = sem("score_variance_ready")
            s_sqd = sem("score_deviation_ready")
            s_ge = sem("gate_logits_ready")
            s_ged = sem("gate_exponentials_ready")
            s_gate = sem("gates_ready")
            s_hid = sem("hidden_multiplied")
            s_gelu = sem("hidden_activated")
            s_ex = sem("experts_multiplied")
            s_comb = sem("experts_combined")
            s_outst = [sem(f"out_stored{k}") for k in range(2)]
            s_dve = sem("vector_step")
            SETUP_LOADS = 4 + 4 + 3

            def slots(eng, body, tail=None):
                for i in range(3):
                    body(i, i % 2)
                with eng.Fori(0, (NB - 4) // 2) as k:
                    body(k * 2 + 3, 1)
                    body(k * 2 + 4, 0)
                body(NB - 1, 1)
                if tail is not None:
                    tail(NB, 0)

            def wait_alone(eng, s, value):
                eng.wait_ge(s, value)
                if not isinstance(value, int):
                    eng.nop().then_inc(s_past, 1)

            def seen(i, par):
                return i // 2 if isinstance(i, int) else (i - par) // 2

            block = two.enter_context(nc.Block())

            @block.sync
            def _(sp):
                sp.dma_start(entry[:, :, :], lists.rearrange("(b p t) a -> p b (t a)", b=NBLK, p=P)).then_inc(s_in, 16)
                sp.dma_start(list_rows[:, :], lists.rearrange("(b c) a -> b (c a)", b=NBLK)).then_inc(s_in, 16)
                sp.dma_start(nodes[:, :, :], table.rearrange("(b p) c -> p b c", p=P)).then_inc(s_in, 16)
                sp.dma_start(last_row[:, :], table[N - 1, :].partition_broadcast(P)).then_inc(s_in, 16)
                sp.dma_start(w1_sb[:, :, :], W1.rearrange("e f c -> f e c")).then_inc(s_in, 16)
                sp.dma_start(w2_sb[:, :, :, :], W2.rearrange("e (k f) c -> f e k c", f=P)).then_inc(s_in, 16)
                with nc.allow_non_contiguous_dma(reason="1024 biases, once"):
                    sp.dma_start(b1_sb[:, :, :], b1.rearrange("e (k f) -> f e k", f=P)).then_inc(s_in, 16)
                sp.dma_start(b2_row[:, :], b2.rearrange("e f -> (e f)").unsqueeze(0)).then_inc(s_in, 16)
                for t, a in ((bg, b_gat), (gamma, ln_gamma), (beta, ln_beta)):
                    sp.dma_start(t[:, :], a.partition_broadcast(P)).then_inc(s_in, 16)
                sp.wait_ge(s_rows2, 1)
                sp.dma_start(lanes_dram, lane_rows[:, :]).then_inc(s_lanes, 16)
                sp.wait_ge(s_b2, 1)
                for k in range(PARTS):
                    sp.dma_start(b2_parts[k:k + 1, :], b2_cut[0:1, k, :]).then_inc(s_b2m, 16)
                sp.wait_ge(s_lanes, 16)

                def body(i, par):
                    if not isinstance(i, int) or i >= 2:
                        wait_alone(sp, s_am, i - 1)
                    lanes = lanes_dram[i * UB:(i + 1) * UB, :] if isinstance(i, int) else lanes_dram[bass.ds(i * UB, UB), :]
                    sp.dma_start(lane_bc[:, par, :], lanes.rearrange("b c -> (b c)").partition_broadcast(P)
                                 ).then_inc(s_bc[par], 16)
                    if not isinstance(i, int) or i >= 2:
                        wait_alone(sp, s_hid, (i - 1) * NF)
                    sp.dma_start(yTu[:, par, :], yT_dram[i] if isinstance(i, int) else
                                 yT_dram[bass.ds(i, 1)].rearrange("a p c -> p (a c)")).then_inc(s_y2[par], 16)
                    if not isinstance(i, int) or i >= 2:
                        wait_alone(sp, s_comb, (i - 1) * UB)
                        sp.wait_ge(s_outst[par], seen(i, par) * 16)
                    rows_i = x1_dram[i * BATCH:(i + 1) * BATCH, :] if isinstance(i, int) else \
                        x1_dram[bass.ds(i * BATCH, BATCH), :]
                    sp.dma_start(x1u[:, par, :, :], rows_i.rearrange("(t p) f -> p t f", p=P)).then_inc(s_x2[par], 16)

                slots(sp, body)

            @block.gpsimd
            def _(pool):
                nc.gpsimd.memset(part_sel[:, :, :], 0.0).then_inc(s_sel, 1)
                nc.gpsimd.memset(onesb[:, :], 1.0).then_inc(s_sel, 1)
                for k in range(PARTS):
                    pool.wait_ge(s_sel, 2 + k)
                    nc.gpsimd.affine_select(out=part_sel[:, :, :], in_=part_sel[:, :, :], compare_op=ALU.not_equal,
                                            fill=1.0, base=-HEADS * k, pattern=[[-1, HEADS], [0, P]],
                                            channel_multiplier=1).then_inc(s_sel, 1)
                pool.wait_ge(s_src, 1)

                def body(i, par):
                    if not isinstance(i, int) or i >= 2:
                        wait_alone(pool, s_pay, i - 1)
                        pool.wait_ge(s_gath[par], seen(i, par) * 16 * UT)
                    at = i * UT
                    nc.gpsimd.tensor_copy(source_now[:, par, :], source[:, at:at + UT] if isinstance(at, int) else
                                          source[:, bass.ds(at, UT)]).then_inc(s_idx, 1)
                    wait_alone(pool, s_idx, i + 1)
                    for t in range(UT):
                        nc.gpsimd.indirect_dma_start(
                            gath[:, par, t, :], None, table,
                            bass.IndirectOffsetOnAxis(ap=source_now[:, par, t:t + 1], axis=0),
                            bounds_check=N - 1, oob_is_err=False).then_inc(s_gath[par], 16)

                slots(pool, body)

            @block.tensor
            def _(pe):
                def turn_as(i, k):
                    if k == 0:
                        pe.wait_ge(s_ast, i + 1)
                        if not isinstance(i, int) or i >= 1:
                            pe.wait_ge(s_amr, i * 2)
                    else:
                        pe.wait_ge(s_tpc, i * 3 + k)
                    piece = misc_ps[0:PARTS * HEADS, :].bitcast(BF16)
                    for t in range(TP8):
                        mm = nc.tensor.transpose(piece[:, t * P:(t + 1) * P],
                                                 as_cut[:, k * TP8 + t, :, :].rearrange("p a h -> p (a h)"), identb[:, :])
                    mm.then_inc(s_tp, 1)

                def spread_as(i, tri):
                    if tri == 0:
                        pe.wait_ge(s_tpc, (i + 1) * 3)
                    for h in range(HEADS):
                        n = tri * HEADS + h
                        if not isinstance(i, int) or i > 0 or n >= 2:
                            pe.wait_ge(s_mx, i * (NTRI * HEADS) + n - 1)
                        nc.tensor.matmul(as_ps[n % 2][:, :], part_sel[:, h, :], asT[:, tri * TRI * P:(tri + 1) * TRI * P],
                                         start=True, stop=True).then_inc(s_as, 1)

                def spread_am(i, k):
                    if k == 0:
                        pe.wait_ge(s_am, i + 1)
                    else:
                        pe.wait_ge(s_amr, i * 2 + 1)
                    for t in range(UT // 2):
                        n = k * (UT // 2) + t
                        w = PARTS * 2 * HEADS
                        mm = nc.tensor.matmul(misc_ps[:, t * w:(t + 1) * w], hotT[:, n, :],
                                              am_cut[:, n // TPB, :, :], start=(t == 0), stop=True, skip_group_check=True)
                    mm.then_inc(s_ame, 1)

                def gather_sum(i):
                    pe.wait_ge(s_pay, i + 1)
                    for t in range(UT):
                        mm = nc.tensor.matmul(agg_ps[:, t // TPB, :, :], hot[:, :, t], pay_cut[:, t, :, :],
                                              start=(t == 0), stop=(t % TPB == TPB - 1), skip_group_check=True)
                    mm.then_inc(s_agg, 1)

                def layer1(i, par, f):
                    if f == 0:
                        pe.wait_ge(s_y2[par], seen(i - 1, par) * 16 + 16)
                    n = (i - 1) * NF + f
                    if not isinstance(n, int) or n >= 2:
                        pe.wait_ge(s_gelu, n - 1)
                    e, k = divmod(f, HALVES)
                    nc.tensor.matmul(hid_ps[f % 2][:, :], w1_sb[:, e, k * P:(k + 1) * P], yTu[:, par, :],
                                     start=True, stop=True).then_inc(s_hid, 1)

                def layer2(i, par, b):
                    if b == 0:
                        pe.wait_ge(s_gelu, i * NF)
                    n = (i - 1) * UB + b
                    if not isinstance(n, int) or n >= 2:
                        pe.wait_ge(s_comb, n - 1)
                    nc.tensor.matmul(out_ps[b % 2][:, :, :], onesb[:, :], b2_parts[:, :], start=True, stop=False,
                                     skip_group_check=True)
                    for e in range(EXP):
                        for k in range(HALVES):
                            mm = nc.tensor.matmul(out_ps[b % 2][:, e, :], hidden[:, e * HALVES + k, b * P:(b + 1) * P],
                                                  w2_sb[:, e, k, :], start=False, stop=(k == HALVES - 1),
                                                  skip_group_check=True)
                    mm.then_inc(s_ex, 1)

                pe.wait_ge(s_in, 16 * SETUP_LOADS)
                pe.wait_ge(s_b2m, 16 * PARTS)
                pe.wait_ge(s_sel, 2 + PARTS)

                def body(i, par):
                    experts = not isinstance(i, int) or i >= 1
                    for k in range(3):
                        turn_as(i, k)
                        if experts:
                            layer1(i, 1 - par, k)
                    for tri in range(NTRI):
                        spread_as(i, tri)
                        if experts and tri in (1, 3, 5):
                            layer1(i, 1 - par, 3 + tri // 2)
                    if experts:
                        layer1(i, 1 - par, 6)
                        layer1(i, 1 - par, 7)
                    spread_am(i, 0)
                    if experts:
                        layer2(i, 1 - par, 0)
                        layer2(i, 1 - par, 1)
                    spread_am(i, 1)
                    if experts:
                        layer2(i, 1 - par, 2)
                        layer2(i, 1 - par, 3)
                    gather_sum(i)

                def tail(i, par):
                    for f in range(NF):
                        layer1(i, 1 - par, f)
                    for b in range(UB):
                        layer2(i, 1 - par, b)

                slots(pe, body, tail)

            @block.scalar
            def _(act):
                act.wait_ge(s_in, 16 * SETUP_LOADS)

                def gelu(i, f):
                    act.wait_ge(s_hid, (i - 1) * NF + f + 1)
                    if f == 0 and (not isinstance(i, int) or i >= 2):
                        act.wait_ge(s_ex, (i - 1) * UB)
                    e, k = divmod(f, HALVES)
                    nc.scalar.activation(hidden[:, f, :], hid_ps[f % 2][:, :], ACT.Gelu, bias=b1_sb[:, e, k:k + 1]
                                         ).then_inc(s_gelu, 1)

                def store(i, par):
                    act.wait_ge(s_comb, i * UB)
                    last = isinstance(i, int) and i == NB
                    at = (i - 1) * BATCH
                    rows_n = LAST_ROWS if last else BATCH
                    whole, over = divmod(rows_n, P)
                    o = out[at:at + whole * P, :] if isinstance(at, int) else out[bass.ds(at, whole * P), :]
                    act.dma_start(o.rearrange("(t p) f -> p t f", p=P), x1u[:, par, 0:whole, :]).then_inc(s_outst[par], 16)
                    if over:
                        act.dma_start(out[at + whole * P:at + rows_n, :], x1u[0:over, par, whole, :]
                                      ).then_inc(s_outst[par], 16)

                def body(i, par):
                    experts = not isinstance(i, int) or i >= 1
                    for k in range(3):
                        act.wait_ge(s_tp, i * 3 + k + 1)
                        if k == 0 and (not isinstance(i, int) or i >= 1):
                            act.wait_ge(s_as, i * NTRI * HEADS)
                        nc.scalar.activation(asT[:, k * TP8 * P:(k + 1) * TP8 * P],
                                             misc_ps[0:PARTS * HEADS, :].bitcast(BF16), ACT.Copy).then_inc(s_tpc, 1)
                        if experts:
                            gelu(i, k)
                    if experts:
                        for f in range(3, NF):
                            gelu(i, f)
                    act.wait_ge(s_log, i + 1)
                    nc.scalar.activation(weight[:, :, :], logit[:, :, :], ACT.Exp).then_inc(s_exp, 1)
                    if experts:
                        store(i, 1 - par)
                    act.wait_ge(s_sq, i + 1)
                    nc.scalar.activation(col[:, 3, :], col[:, 2, :], ACT.Sqrt).then_inc(s_sqd, 1)
                    act.wait_ge(s_ge, i + 1)
                    nc.scalar.activation(gexp[:, :, :], cmpb[:, :, :], ACT.Exp).then_inc(s_ged, 1)

                def tail(i, par):
                    for f in range(NF):
                        gelu(i, f)
                    store(i, 1 - par)
                    act.wait_ge(s_outst[0], NB // 2 * 16)
                    act.wait_ge(s_outst[1], NB // 2 * 16 + 16)

                slots(act, body, tail)

            @block.vector
            def _(dve):
                v = nc.vector
                at = [0, 0]
                LINKS = [0]

                def link(ins):
                    at[1] += 1
                    ins.then_inc(s_dve, 1)
                    dve.wait_ge(s_dve, at[0] + at[1])

                def cut(parts, value, residue):
                    link(v.tensor_copy(parts(0), value))
                    link(v.tensor_tensor(residue, value, parts(0), ALU.subtract))
                    link(v.tensor_copy(parts(1), residue))
                    link(v.tensor_tensor(residue, residue, parts(1), ALU.subtract))
                    return v.tensor_copy(parts(2), residue)

                def leaky(t):
                    link(v.scalar_tensor_tensor(out=t, in0=t, scalar=0.2, in1=t, op0=ALU.mult, op1=ALU.max))

                dve.wait_ge(s_in, 16 * SETUP_LOADS)
                link(v.tensor_scalar(source[:, :], entry[:, :, :].rearrange("p b t -> p (b t)"), (1 << SRC_BITS) - 1, None,
                                     ALU.bitwise_and))
                v.nop().then_inc(s_src, 1)
                link(v.tensor_scalar(list_rows[:, :], list_rows[:, :], SRC_BITS, None, ALU.logical_shift_right))
                v.tensor_copy(lane_rows[:, :], list_rows[:, :]).then_inc(s_rows2, 1)
                link(v.tensor_scalar(lane_i[:, :], entry[:, :, :].rearrange("p b t -> p (b t)"), SRC_BITS, None,
                                     ALU.logical_shift_right))
                link(v.tensor_copy(lane_e[:, :], lane_i[:, :]))
                cut(lambda k: b2_cut[:, k, :], b2_row[:, :], b2_res[:, :]).then_inc(s_b2, 1)
                a_src, a_dst = nodes[:, :, HE:HE + HEADS], nodes[:, :, HE + HEADS:ROW]
                last_as = last_row[:, HE:HE + HEADS].unsqueeze(1).broadcast_to([P, NBLK, HEADS])
                link(v.tensor_scalar(no_clamp[:, :], clamp_count[:, :], 0.0, -BIG, ALU.is_equal, ALU.mult))
                link(v.tensor_tensor(floor_max[:, :, :], last_as,
                                     no_clamp[:, :].unsqueeze(2).broadcast_to([P, NBLK, HEADS]), ALU.add))
                link(v.tensor_tensor(floor_max[:, :, :], floor_max[:, :, :], a_src, ALU.max))
                link(v.tensor_tensor(e_self[:, :, 0, :], a_src, a_dst, ALU.add))
                link(v.tensor_tensor(e_self[:, :, 1, :], last_as, a_dst, ALU.add))
                leaky(e_self[:, :, :, :])
                SETUP_LINKS = at[1]

                def blk(t, i, *rest):
                    b0 = i * UB
                    key = slice(b0, b0 + UB) if isinstance(i, int) else bass.ds(b0, UB)
                    return t[(slice(None), key) + rest]

                def combine(i, par, b):
                    dve.wait_ge(s_ex, (i - 1) * UB + b + 1)
                    if b == 0:
                        dve.wait_ge(s_x2[par], seen(i - 1, par) * 16 + 16)
                    for e in range(EXP):
                        ins = v.scalar_tensor_tensor(out=x1u[:, par, b, :], in0=out_ps[b % 2][:, e, :],
                                                     scalar=gate[:, par, b, e:e + 1], in1=x1u[:, par, b, :],
                                                     op0=ALU.mult, op1=ALU.add)
                        if e < EXP - 1:
                            link(ins)
                        else:
                            ins.then_inc(s_comb, 1)

                def body(i, par):
                    first = isinstance(i, int) and i == 0
                    at[0], at[1] = (SETUP_LINKS, 0) if first else \
                        (SETUP_LINKS + LINKS[0] + (i - 1) * LINKS[-1], 0) if not (isinstance(i, int) and i == 1) else \
                        (SETUP_LINKS + LINKS[0], 0)
                    dve.wait_ge(s_gath[par], (seen(i, par) + 1) * 16 * UT)
                    if not first:
                        dve.wait_ge(s_tp, i * 3)
                    g_as = gath[:, par, :, HE:HE + HEADS]
                    cut(lambda k: as_cut[:, :, k, :], g_as, as_res[:, :, :]).then_inc(s_ast, 1)
                    dve.wait_ge(s_bc[par], (seen(i, par) + 1) * 16)
                    lanes = lane_bc[:, par, :].rearrange("q (b p t) -> q b t p", b=UB, p=P)
                    hv = hotT[:, :, :].rearrange("q (b t) p -> q b t p", b=UB)
                    mv = maskT[:, :, :].rearrange("q (b t) p -> q b t p", b=UB)
                    for b in range(UB):
                        v.tensor_scalar(mv[:, b], lanes[:, b], lane_col[:, 0:1], -BIG, ALU.not_equal, ALU.mult)
                        ins = v.tensor_scalar(hv[:, b], lanes[:, b], lane_col[:, 0:1], None, ALU.is_equal)
                    link(ins)
                    le = lane_e[:, i * UT:(i + 1) * UT] if isinstance(i, int) else lane_e[:, bass.ds(i * UT, UT)]
                    if not first:
                        dve.wait_ge(s_agg, i)
                    link(v.tensor_tensor(hot[:, :, :], le.unsqueeze(1).broadcast_to([P, P, UT]), iota_lane[:, :, :],
                                         ALU.is_equal))
                    for tri in range(NTRI):
                        for h in range(HEADS):
                            n = tri * HEADS + h
                            wait_alone(dve, s_as, i * (NTRI * HEADS) + n + 1)
                            ins = v.tensor_tensor_reduce(
                                out=junk[:, n % 2, :], in0=as_ps[n % 2][:, :],
                                in1=maskT[:, tri * TRI:(tri + 1) * TRI, :].rearrange("q t p -> q (t p)"),
                                scale=1.0, scalar=-BIG, op0=ALU.add, op1=ALU.max,
                                accum_out=mx[:, tri // 2, tri % 2, h:h + 1])
                            ins.then_inc(s_mx, 1)
                    dve.wait_ge(s_mx, (i + 1) * NTRI * HEADS)
                    m = am[:, :, HEADS:2 * HEADS]
                    link(v.tensor_tensor(m, mx[:, :, 0, :], mx[:, :, 1, :], ALU.max))
                    link(v.tensor_tensor(m, m, blk(floor_max, i, slice(None)), ALU.max))
                    link(v.tensor_copy(am[:, :, 0:HEADS], blk(nodes, i, slice(HE + HEADS, ROW))))
                    link(v.tensor_tensor(m, m, am[:, :, 0:HEADS], ALU.add))
                    leaky(m)
                    cut(lambda k: am_cut[:, :, k, :], am[:, :, :], am_res[:, :, :]).then_inc(s_am, 1)
                    sl = logit[:, UT:UT + 2 * UB, :].rearrange("p (b s) h -> p b s h", s=2)
                    link(v.tensor_tensor(sl, blk(e_self, i, slice(None), slice(None)),
                                         m.unsqueeze(2).broadcast_to([P, UB, 2, HEADS]), ALU.subtract))
                    link(v.tensor_scalar(logit[:, UT:UT + 2 * UB, :], logit[:, UT:UT + 2 * UB, :], 0.0, None, ALU.min))
                    if not first:
                        combine(i, 1 - par, 0)
                    for k in range(2):
                        half_t = UT // 2
                        dve.wait_ge(s_ame, i * 2 + k + 1)
                        w = PARTS * 2 * HEADS
                        ins = v.tensor_reduce(am_e[:, k * half_t:(k + 1) * half_t, :],
                                              misc_ps[:, 0:half_t * w].rearrange("p (t a c) -> p t c a", t=half_t, a=PARTS),
                                              AX_X, ALU.add)
                        ins.then_inc(s_amr, 1)
                        if k == 0 and not first:
                            combine(i, 1 - par, 1)
                    dve.wait_ge(s_amr, i * 2 + 2)
                    lg = logit[:, 0:UT, :]
                    link(v.tensor_tensor(lg, g_as, am_e[:, :, 0:HEADS], ALU.add))
                    leaky(lg)
                    v.tensor_tensor(lg, lg, am_e[:, :, HEADS:2 * HEADS], ALU.subtract).then_inc(s_log, 1)
                    if not first:
                        combine(i, 1 - par, 2)
                        combine(i, 1 - par, 3)
                    dve.wait_ge(s_exp, i + 1)
                    wt = weight[:, 0:UT, :]
                    link(v.tensor_copy(pay_e[:, :, HE:HE + HEADS], wt))
                    link(v.tensor_tensor(pay_e[:, :, 0:HE].rearrange("p t (h k) -> p t h k", h=HEADS),
                                         gath[:, par, :, 0:HE].rearrange("p t (h k) -> p t h k", h=HEADS),
                                         wt.unsqueeze(3).broadcast_to([P, UT, HEADS, EXP]), ALU.mult))
                    cut(lambda k: pay_cut[:, :, k, :], pay_e[:, :, :], pay_res[:, :, :]).then_inc(s_pay, 1)
                    sw = weight[:, UT:UT + 2 * UB, :].rearrange("p (b s) h -> p b s h", s=2)
                    w_self, w_last = sw[:, :, 0, :], sw[:, :, 1, :]
                    link(v.tensor_tensor(w_last, w_last, blk(clamp_count, i).unsqueeze(2).broadcast_to([P, UB, HEADS]),
                                         ALU.mult))
                    h4 = "p b (h k) -> p b h k"
                    link(v.tensor_tensor(tmp16[:, :, :].rearrange(h4, h=HEADS),
                                         blk(nodes, i, slice(0, HE)).rearrange(h4, h=HEADS),
                                         w_self.unsqueeze(3).broadcast_to([P, UB, HEADS, EXP]), ALU.mult))
                    link(v.tensor_tensor(tmp16b[:, :, :].rearrange(h4, h=HEADS),
                                         last_row[:, 0:HE].unsqueeze(1).broadcast_to([P, UB, HE]).rearrange(h4, h=HEADS),
                                         w_last.unsqueeze(3).broadcast_to([P, UB, HEADS, EXP]), ALU.mult))
                    link(v.tensor_tensor(tmp16[:, :, :], tmp16[:, :, :], tmp16b[:, :, :], ALU.add))
                    link(v.tensor_tensor(tmp4[:, :, :], w_self, w_last, ALU.add))
                    dve.wait_ge(s_agg, i + 1)
                    link(v.tensor_reduce(nd[:, :, :], agg_ps[:, :, :, :].rearrange("p b a c -> p b c a"), AX_X, ALU.add))
                    link(v.tensor_tensor(nd[:, :, 0:HE], nd[:, :, 0:HE], tmp16[:, :, :], ALU.add))
                    link(v.tensor_tensor(nd[:, :, HE:HE + HEADS], nd[:, :, HE:HE + HEADS], tmp4[:, :, :], ALU.add))
                    link(v.tensor_scalar(tmp4[:, :, :], nd[:, :, HE:HE + HEADS], 1e-16, None, ALU.add))
                    link(v.reciprocal(tmp4[:, :, :], tmp4[:, :, :]))
                    agg = tmp16[:, :, :]
                    link(v.tensor_tensor(agg.rearrange(h4, h=HEADS), nd[:, :, 0:HE].rearrange(h4, h=HEADS),
                                         tmp4[:, :, :].unsqueeze(3).broadcast_to([P, UB, HEADS, EXP]), ALU.mult))

                    center(v, link, agg, bg, tmp16b, col, UB).then_inc(s_sq, 1)
                    dve.wait_ge(s_sqd, i + 1)
                    rank_scores(v, link, agg, gamma, beta, col, score, order, cmpb, UB).then_inc(s_ge, 1)
                    dve.wait_ge(s_ged, i + 1)
                    link(share_gates(v, link, order, gexp, col, gate[:, par, :, :], UB))
                    if first or (isinstance(i, int) and i == 1):
                        LINKS.append(at[1])
                        if first:
                            LINKS[0] = at[1]
                    assert at[1] == (LINKS[0] if first else LINKS[-1])

                def tail(i, par):
                    at[0], at[1] = SETUP_LINKS + LINKS[0] + (i - 1) * LINKS[-1], 0
                    for b in range(UB):
                        combine(i, 1 - par, b)

                slots(dve, body, tail)

        ALL_COLS = EC
        ND = HE + HEADS
        FULL = N // P
        OVER = N - FULL * P
        HALF_FF = FF // P
        every = ExitStack()
        with every:
            def gsb(name, shape, dt=F32):
                return every.enter_context(nc.sbuf_tensor(name, shape, dt))

            def gps(name, shape):
                return every.enter_context(nc.psum_tensor(name, shape, F32))

            def sem(name):
                return every.enter_context(nc.semaphore(name))

            all_src = gsb("all_src", [P, EC], I32)
            all_dst = gsb("all_dst", [P, EC], I32)
            col_src = gsb("col_src", [P, 1], I32)
            col_dst = gsb("col_dst", [P, 1])
            table_lanes = gsb("table_lanes", [P, NBLK, ROW])
            node_id = gsb("node_id", [P, NBLK])
            edge_rows = gsb("edge_rows", [P, ROW])
            diag = gsb("diag", [P, HEADS + 1, P])
            as_all = gsb("as_all", [P, HEADS, P])
            dst_all = gsb("dst_all", [P, P])
            off = gsb("off", [P, P])
            z = gsb("z", [P, HEADS, P + 1])
            wz = gsb("wz", [P, HEADS, P + 1])
            wzT = gsb("wzT", [P, HEADS, P])
            run_max = gsb("run_max", [P, NBLK, HEADS])
            run_sum = gsb("run_sum", [P, NBLK, ND])
            new_max = gsb("new_max", [P, HEADS])
            part = gsb("part", [P, ND])
            gw1 = gsb("gw1", [P, EXP, FF])
            gw2 = gsb("gw2", [P, EXP, HALF_FF, D])
            gb1 = gsb("gb1", [P, EXP, HALF_FF])
            gb2 = gsb("gb2", [1, EXP * D])
            gbg, ggamma, gbeta = gsb("gbg", [P, HE]), gsb("ggamma", [P, HE]), gsb("gbeta", [P, HE])
            gy = gsb("gy", [P, P])
            gx1 = gsb("gx1", [P, D])
            ghid = gsb("ghid", [P, EXP * HALF_FF, P])
            gagg = gsb("gagg", [P, 1, HE])
            gsq = gsb("gsq", [P, 1, HE])
            gcol = gsb("gcol", [P, 6, 1])
            gscore, gcmp, gorder, gexps, ggate = (gsb(n, [P, 1, EXP]) for n in
                                                  ("gscore", "gcmp", "gorder", "gexps", "ggate"))
            wide_ps = gps("wide_ps", [P, HEADS, P])
            dst_ps = gps("dst_ps", [P, P])
            wzT_ps = gps("wzT_ps", [P, HEADS, P])
            num_ps = gps("num_ps", [P, HE])
            ghid_ps = [gps(f"ghid_ps{k}", [P, 4, P]) for k in range(2)]
            gout_ps = gps("gout_ps", [P, EXP, D])

            s_past = sem("waits_passed")
            s_gin = sem("general_loaded")
            s_gid = sem("node_ids_ready")
            s_gidx = sem("column_sources_ready")
            s_grow = sem("column_rows_gathered")
            s_gdiag = sem("diagonals_ready")
            s_gwide = sem("column_spread")
            s_gz = sem("column_logits_ready")
            s_gwz = sem("column_weights_ready")
            s_gwt = sem("column_weights_turned")
            s_gwc = sem("column_weights_copied")
            s_gnum = sem("column_summed")
            s_gcols = sem("columns_done")
            s_gfree = sem("block_buffers_free")
            s_gyx = sem("block_loaded")
            s_ghm = sem("block_hidden_multiplied")
            s_gha = sem("block_hidden_activated")
            s_gex = sem("block_experts_multiplied")
            s_gsq = sem("block_variance_ready")
            s_gsd = sem("block_deviation_ready")
            s_gge = sem("block_gate_logits_ready")
            s_ggd = sem("block_gate_exponentials_ready")
            s_gout = sem("block_stored")
            s_dve = sem("vector_step")
            G_LOADS = 3 + 4 + 3

            def wait_alone(eng, s, value):
                eng.wait_ge(s, value)
                eng.nop().then_inc(s_past, 1)

            def each_block(eng, body):
                with eng.Fori(0, FULL) as b:
                    body(b, P)
                body(FULL, OVER)

            def lanes_of(t, b, n):
                return t[b * P:b * P + n, :] if isinstance(b, int) else t[bass.ds(b * P, n), :]

            block = every.enter_context(nc.Block())

            @block.sync
            def _(sp):
                left = sp.value_load(left_count[0:1, 0:1], min_val=0, max_val=E)
                with sp.If(left > 0):
                    e_v = edge_index.rearrange("a (p c) -> a p c", p=P)
                    sp.dma_start(all_src[:, :], e_v[0]).then_inc(s_gin, 16)
                    sp.dma_start(all_dst[:, :], e_v[1]).then_inc(s_gin, 16)
                    sp.dma_start(table_lanes[:, :, :], table.rearrange("(b p) c -> p b c", p=P)).then_inc(s_gin, 16)
                    sp.dma_start(gw1[:, :, :], W1.rearrange("e f c -> f e c")).then_inc(s_gin, 16)
                    sp.dma_start(gw2[:, :, :, :], W2.rearrange("e (k f) c -> f e k c", f=P)).then_inc(s_gin, 16)
                    with nc.allow_non_contiguous_dma(reason="1024 biases, once"):
                        sp.dma_start(gb1[:, :, :], b1.rearrange("e (k f) -> f e k", f=P)).then_inc(s_gin, 16)
                    sp.dma_start(gb2[:, :], b2.rearrange("e f -> (e f)").unsqueeze(0)).then_inc(s_gin, 16)
                    for t, a in ((gbg, b_gat), (ggamma, ln_gamma), (gbeta, ln_beta)):
                        sp.dma_start(t[:, :], a.partition_broadcast(P)).then_inc(s_gin, 16)

                    def body(b, n):
                        sp.wait_ge(s_gfree, b + 1)
                        yb = yT_dram[b // 4] if isinstance(b, int) else yT_dram[bass.ds(b // 4, 1)].rearrange(
                            "a p c -> p (a c)")
                        at = (b % 4) * P
                        yb = yb[:, at:at + P] if isinstance(b, int) else yb[:, bass.ds(at, P)]
                        sp.dma_start(gy[:, :], yb).then_inc(s_gyx, 16)
                        sp.dma_start(gx1[0:n, :], lanes_of(x1_dram, b, n)).then_inc(s_gyx, 16)

                    each_block(sp, body)

            @block.gpsimd
            def _(pool):
                left = pool.value_load(left_count[0:1, 0:1], min_val=0, max_val=E)
                with pool.If(left > 0):
                    nc.gpsimd.iota(node_id[:, :], [[P, NBLK]], base=0, channel_multiplier=1,
                                   allow_small_or_imprecise_dtypes=True).then_inc(s_gid, 1)
                    with pool.Fori(0, ALL_COLS) as k:
                        wait_alone(pool, s_gidx, k + 1)
                        nc.gpsimd.indirect_dma_start(
                            edge_rows[:, :], None, table, bass.IndirectOffsetOnAxis(ap=col_src[:, 0:1], axis=0),
                            bounds_check=N - 1, oob_is_err=False).then_inc(s_grow, 16)

            @block.tensor
            def _(pe):
                left = pe.value_load(left_count[0:1, 0:1], min_val=0, max_val=E)
                with pe.If(left > 0):
                    with pe.Fori(0, ALL_COLS) as k:
                        pe.wait_ge(s_gdiag, k + 1)
                        nc.tensor.matmul(wide_ps[:, :, :], ones[:, :], diag[:, 0:HEADS, :], start=True, stop=True)
                        nc.tensor.matmul(dst_ps[:, :], ones[:, :], diag[:, HEADS, :], start=True, stop=True
                                         ).then_inc(s_gwide, 1)
                        with pe.Fori(0, NBLK) as b:
                            n = k * NBLK + b + 1
                            pe.wait_ge(s_gwz, n)
                            for h in range(HEADS):
                                mm = nc.tensor.transpose(wzT_ps[:, h, :], wz[:, h, 0:P], ident[:, :])
                            mm.then_inc(s_gwt, 1)
                            pe.wait_ge(s_gwc, n)
                            for h in range(HEADS):
                                mm = nc.tensor.matmul(num_ps[:, h * EXP:(h + 1) * EXP], wzT[:, h, :],
                                                      edge_rows[:, h * EXP:(h + 1) * EXP], start=(h == 0), stop=True,
                                                      skip_group_check=True)
                            mm.then_inc(s_gnum, 1)
                    pe.wait_ge(s_gin, 16 * G_LOADS)

                    def body(b, n):
                        pe.wait_ge(s_gyx, (b + 1) * 32)
                        for f in range(EXP * HALF_FF):
                            e, k = divmod(f, HALF_FF)
                            mm = nc.tensor.matmul(ghid_ps[f // 4][:, f % 4, :], gw1[:, e, k * P:(k + 1) * P], gy[:, :],
                                                  start=(f % 4 == 0), stop=True, skip_group_check=True)
                        mm.then_inc(s_ghm, 1)
                        pe.wait_ge(s_gha, b + 1)
                        nc.tensor.matmul(gout_ps[:, :, :], ones[0:1, :], gb2[:, :], start=True, stop=False,
                                         skip_group_check=True)
                        for e in range(EXP):
                            for k in range(HALF_FF):
                                mm = nc.tensor.matmul(gout_ps[:, e, :], ghid[:, e * HALF_FF + k, :], gw2[:, e, k, :],
                                                      start=False, stop=(k == HALF_FF - 1), skip_group_check=True)
                        mm.then_inc(s_gex, 1)

                    each_block(pe, body)

            @block.scalar
            def _(act):
                left = act.value_load(left_count[0:1, 0:1], min_val=0, max_val=E)
                with act.If(left > 0):
                    with act.Fori(0, ALL_COLS) as k:
                        with act.Fori(0, NBLK) as b:
                            n = k * NBLK + b + 1
                            act.wait_ge(s_gz, n)
                            nc.scalar.activation(wz[:, :, :], z[:, :, :], ACT.Exp).then_inc(s_gwz, 1)
                            act.wait_ge(s_gwt, n)
                            nc.scalar.activation(wzT[:, :, :], wzT_ps[:, :, :], ACT.Copy).then_inc(s_gwc, 1)
                    act.wait_ge(s_gin, 16 * G_LOADS)

                    def body(b, n):
                        act.wait_ge(s_ghm, b + 1)
                        for f in range(EXP * HALF_FF):
                            e, k = divmod(f, HALF_FF)
                            ins = nc.scalar.activation(ghid[:, f, :], ghid_ps[f // 4][:, f % 4, :], ACT.Gelu,
                                                       bias=gb1[:, e, k:k + 1])
                        ins.then_inc(s_gha, 1)
                        act.wait_ge(s_gsq, b + 1)
                        nc.scalar.activation(gcol[:, 3, :], gcol[:, 2, :], ACT.Sqrt).then_inc(s_gsd, 1)
                        act.wait_ge(s_gge, b + 1)
                        nc.scalar.activation(gexps[:, :, :], gcmp[:, :, :], ACT.Exp).then_inc(s_ggd, 1)
                        act.wait_ge(s_gcols, b + 1)
                        act.dma_start(lanes_of(out, b, n), gx1[0:n, :]).then_inc(s_gout, 16)

                    each_block(act, body)
                    act.wait_ge(s_gout, (FULL + 1) * 16)

            @block.vector
            def _(dve):
                v = nc.vector
                at = [0, 0]

                def link(ins):
                    at[1] += 1
                    ins.then_inc(s_dve, 1)
                    dve.wait_ge(s_dve, at[0] + at[1])

                left = dve.value_load(left_count[0:1, 0:1], min_val=0, max_val=E)
                with dve.If(left > 0):
                    dve.wait_ge(s_gin, 16 * G_LOADS)
                    dve.wait_ge(s_gid, 1)
                    link(v.tensor_scalar(all_src[:, :], all_src[:, :], float(N - 1), None, ALU.min))
                    a_src, a_dst = table_lanes[:, :, HE:HE + HEADS], table_lanes[:, :, HE + HEADS:ROW]
                    link(v.tensor_tensor(run_max[:, :, :], a_src, a_dst, ALU.add))
                    link(v.scalar_tensor_tensor(out=run_max[:, :, :], in0=run_max[:, :, :], scalar=0.2,
                                                in1=run_max[:, :, :], op0=ALU.mult, op1=ALU.max))
                    link(v.tensor_copy(run_sum[:, :, 0:HE], table_lanes[:, :, 0:HE]))
                    link(v.memset(run_sum[:, :, HE:ND], 1.0))
                    SETUP = at[1]
                    COL_LINKS, BLK_LINKS = 4, 11
                    with dve.Fori(0, ALL_COLS) as k:
                        at[0], at[1] = k * (COL_LINKS + NBLK * BLK_LINKS) + SETUP, 0
                        v.tensor_copy(col_src[:, :], all_src[:, bass.ds(k, 1)]).then_inc(s_gidx, 1)
                        link(v.tensor_copy(col_dst[:, :], all_dst[:, bass.ds(k, 1)]))
                        dve.wait_ge(s_grow, (k + 1) * 16)
                        for h in range(HEADS):
                            v.tensor_scalar(diag[:, h, :], ident[:, :], edge_rows[:, HE + h:HE + h + 1], None, ALU.mult)
                        link(v.tensor_scalar(diag[:, HEADS, :], ident[:, :], col_dst[:, 0:1], None, ALU.mult))
                        v.nop().then_inc(s_gdiag, 1)
                        dve.wait_ge(s_gwide, k + 1)
                        link(v.tensor_copy(as_all[:, :, :], wide_ps[:, :, :]))
                        link(v.tensor_copy(dst_all[:, :], dst_ps[:, :]))
                        v.nop().then_inc(s_past, 1)
                        assert at[1] == COL_LINKS
                        with dve.Fori(0, NBLK) as b:
                            at[0], at[1] = k * (COL_LINKS + NBLK * BLK_LINKS) + b * BLK_LINKS + (SETUP + COL_LINKS), 0
                            n = k * NBLK + b + 1
                            mine, ad = run_max[:, bass.ds(b, 1), :], table_lanes[:, bass.ds(b, 1), HE + HEADS:ROW]
                            zz = z[:, :, 0:P]
                            link(v.tensor_scalar(off[:, :], dst_all[:, :], node_id[:, bass.ds(b, 1)], -BIG,
                                                 ALU.not_equal, ALU.mult))
                            link(v.tensor_tensor(zz, as_all[:, :, :], ad.rearrange("p a h -> p (a h)").unsqueeze(2)
                                                 .broadcast_to([P, HEADS, P]), ALU.add))
                            link(v.scalar_tensor_tensor(out=zz, in0=zz, scalar=0.2, in1=zz, op0=ALU.mult, op1=ALU.max))
                            link(v.tensor_tensor(zz, zz, off[:, :].unsqueeze(1).broadcast_to([P, HEADS, P]), ALU.add))
                            link(v.tensor_reduce(new_max[:, :], zz, AX_X, ALU.max))
                            mine = mine.rearrange("p a h -> p (a h)")
                            link(v.tensor_tensor(new_max[:, :], new_max[:, :], mine, ALU.max))
                            v.tensor_tensor(z[:, :, P], mine, new_max[:, :], ALU.subtract)
                            v.tensor_tensor(zz, zz, new_max[:, :].unsqueeze(2).broadcast_to([P, HEADS, P]),
                                            ALU.subtract).then_inc(s_gz, 1)
                            wait_alone(dve, s_gz, n)
                            link(v.tensor_copy(mine, new_max[:, :]))
                            dve.wait_ge(s_gwz, n)
                            link(v.tensor_reduce(part[:, HE:ND], wz[:, :, 0:P], AX_X, ALU.add))
                            dve.wait_ge(s_gnum, n)
                            link(v.tensor_copy(part[:, 0:HE], num_ps[:, :]))
                            mysum = run_sum[:, bass.ds(b, 1), :].rearrange("p a c -> p (a c)")
                            num, den = mysum[:, 0:HE].rearrange("p (h k) -> p h k", h=HEADS), mysum[:, HE:ND]
                            v.tensor_tensor(num, num, wz[:, :, P:P + 1].broadcast_to([P, HEADS, EXP]), ALU.mult)
                            link(v.tensor_tensor(den, den, wz[:, :, P], ALU.mult))
                            link(v.tensor_tensor(mysum, mysum, part[:, :], ALU.add))
                            GOT = at[1]
                    assert GOT == BLK_LINKS, GOT
                    AFTER = ALL_COLS * (COL_LINKS + NBLK * BLK_LINKS) + SETUP
                    TAIL = [0]
                    v.memset(gx1[:, :], 0.0).then_inc(s_gfree, 1)

                    def body(b, n):
                        at[0], at[1] = b * TAIL[0] + AFTER, 0
                        sums = run_sum[:, b:b + 1, :] if isinstance(b, int) else run_sum[:, bass.ds(b, 1), :]
                        link(v.tensor_scalar(gexps[:, :, :], sums[:, :, HE:ND], 1e-16, None, ALU.add))
                        link(v.reciprocal(gexps[:, :, :], gexps[:, :, :]))
                        h4 = "p b (h k) -> p b h k"
                        link(v.tensor_tensor(gagg[:, :, :].rearrange(h4, h=HEADS), sums[:, :, 0:HE].rearrange(h4, h=HEADS),
                                             gexps[:, :, :].unsqueeze(3).broadcast_to([P, 1, HEADS, EXP]), ALU.mult))
                        center(v, link, gagg[:, :, :], gbg, gsq, gcol, 1).then_inc(s_gsq, 1)
                        dve.wait_ge(s_gsd, b + 1)
                        rank_scores(v, link, gagg[:, :, :], ggamma, gbeta, gcol, gscore, gorder, gcmp, 1
                                    ).then_inc(s_gge, 1)
                        dve.wait_ge(s_ggd, b + 1)
                        link(share_gates(v, link, gorder, gexps, gcol, ggate[:, :, :], 1))
                        dve.wait_ge(s_gyx, (b + 1) * 32)
                        dve.wait_ge(s_gex, b + 1)
                        for e in range(EXP):
                            ins = v.scalar_tensor_tensor(out=gx1[:, :], in0=gout_ps[:, e, :], scalar=ggate[:, 0, e:e + 1],
                                                         in1=gx1[:, :], op0=ALU.mult, op1=ALU.add)
                            if e < EXP - 1:
                                link(ins)
                            else:
                                ins.then_inc(s_gcols, 1)
                        dve.wait_ge(s_gout, (b + 1) * 16)
                        v.nop().then_inc(s_gfree, 1)

                    TAIL[0] = G_TAIL_LINKS
                    each_block(dve, body)
                    assert at[1] == G_TAIL_LINKS, at[1]


_INS = ["x", "adj", "L0_gnn_item_feat", "L0_gnn_W_item", "L0_gnn_b_item", "L0_gnn_W_user", "L0_gnn_b_user",
        "L0_ffn_W_gat", "L0_ffn_att_src", "L0_ffn_att_dst", "L0_ffn_b_gat", "L0_ffn_ln_gamma", "L0_ffn_ln_beta",
        "L0_ffn_W1", "L0_ffn_b1", "L0_ffn_W2", "L0_ffn_b2", "L0_ffn_edge_index"]


def kernel(**inputs):
    import numpy as _np
    import concourse.bacc as _bacc
    from concourse import mybir as _mybir
    from concourse.bass_utils import run_bass_kernel_spmd as _run

    nc = _bacc.Bacc("TRN2", target_bir_lowering=False, num_devices=1)
    arrays, args = {}, []
    for name in _INS:
        a = _np.ascontiguousarray(inputs[name])
        arrays[f"in_{name}_dram"] = a
        args.append(nc.dram_tensor(f"in_{name}_dram", a.shape, _mybir.dt.from_np(a.dtype), kind="ExternalInput").ap())
    out = nc.dram_tensor("out_0_dram", (10000, 128), _mybir.dt.from_np(_np.dtype("float32")), kind="ExternalOutput").ap()
    adj_ffn_kernel(nc, *args, out)
    r = _run(nc, [arrays], core_ids=[0])
    return r.results[0]["out_0_dram"]
```

```python
from contextlib import ExitStack

import concourse.bass as bass
from concourse import mybir

ALU = mybir.AluOpType
ACT = mybir.ActivationFunctionType
F32 = mybir.dt.float32
BF16 = mybir.dt.bfloat16
I32 = mybir.dt.int32
AX_X = mybir.AxisListType.X

P = 128
SRC_BITS = 14
LO_BITS = 7
BIG = float(2.0 ** 100)
LN_EPS = 1e-5
G_TAIL_LINKS = 36


def compact_stages(length):
    return [1 << b for b in range((length - 1).bit_length())]


def center(v, link, agg, bias, squares, col, blocks):
    _, _, width = agg.shape
    link(v.tensor_tensor(agg, agg, bias[:, :].unsqueeze(1).broadcast_to([P, blocks, width]), ALU.add))
    link(v.tensor_reduce(col[:, 0, :], agg, AX_X, ALU.add))
    link(v.tensor_scalar(col[:, 0, :], col[:, 0, :], 1.0 / width, None, ALU.mult))
    link(v.tensor_tensor(agg, agg, col[:, 0, :].unsqueeze(2).broadcast_to([P, blocks, width]), ALU.subtract))
    link(v.tensor_tensor(squares[:, :, :], agg, agg, ALU.mult))
    link(v.tensor_reduce(col[:, 1, :], squares[:, :, :], AX_X, ALU.add))
    return v.tensor_scalar(col[:, 2, :], col[:, 1, :], 1.0 / width, LN_EPS, ALU.mult, ALU.add)


def rank_scores(v, link, agg, gamma, beta, col, score, order, cmpb, blocks):
    width, exp = agg.shape[2], score.shape[2]
    heads = width // exp

    def wide(t):
        return t[:, :].unsqueeze(1).broadcast_to([P, blocks, width])

    link(v.reciprocal(col[:, 4, :], col[:, 3, :]))
    link(v.tensor_tensor(agg, agg, col[:, 4, :].unsqueeze(2).broadcast_to([P, blocks, width]), ALU.mult))
    link(v.tensor_tensor(agg, agg, wide(gamma), ALU.mult))
    link(v.tensor_tensor(agg, agg, wide(beta), ALU.add))
    link(v.tensor_reduce(score[:, :, :], agg.rearrange("p b (h k) -> p b k h", h=heads), AX_X, ALU.add))
    link(v.tensor_scalar(score[:, :, :], score[:, :, :], 1.0 / heads, None, ALU.mult))
    link(v.memset(order[:, :, :], 0.0))
    for j in range(exp):
        sj = score[:, :, j:j + 1]
        if j + 1 < exp:
            n = exp - 1 - j
            link(v.tensor_tensor(cmpb[:, :, 0:n], sj.broadcast_to([P, blocks, n]), score[:, :, j + 1:exp], ALU.is_ge))
            link(v.tensor_tensor(order[:, :, j + 1:exp], order[:, :, j + 1:exp], cmpb[:, :, 0:n], ALU.add))
        if j > 0:
            link(v.tensor_tensor(cmpb[:, :, 0:j], sj.broadcast_to([P, blocks, j]), score[:, :, 0:j], ALU.is_gt))
            link(v.tensor_tensor(order[:, :, 0:j], order[:, :, 0:j], cmpb[:, :, 0:j], ALU.add))
    link(v.tensor_reduce(col[:, 0, :], score[:, :, :], AX_X, ALU.max))
    return v.tensor_tensor(cmpb[:, :, :], score[:, :, :],
                           col[:, 0, :].unsqueeze(2).broadcast_to([P, blocks, exp]), ALU.subtract)


def share_gates(v, link, order, gexp, col, gate, blocks):
    exp = order.shape[2]
    link(v.scalar_tensor_tensor(out=gexp[:, :, :], in0=order[:, :, :], scalar=1.5, in1=gexp[:, :, :],
                                op0=ALU.is_lt, op1=ALU.mult))
    link(v.tensor_reduce(col[:, 1, :], gexp[:, :, :], AX_X, ALU.add))
    link(v.reciprocal(col[:, 5, :], col[:, 1, :]))
    return v.tensor_tensor(gate, gexp[:, :, :], col[:, 5, :].unsqueeze(2).broadcast_to([P, blocks, exp]), ALU.mult)


def adj_ffn_kernel(nc, x, adj, item_feat, W_item, b_item, W_user, b_user, W_gat, att_src, att_dst, b_gat,
                   ln_gamma, ln_beta, W1, b1, W2, b2, edge_index, out):
    N, D = x.shape
    NI = item_feat.shape[0]
    E = edge_index.shape[1]
    HEADS, EXP = att_src.shape
    HE = HEADS * EXP
    FF = W1.shape[2]
    ROW = HE + 2 * HEADS

    BATCH = 512
    NB = -(-N // BATCH)
    GR = BATCH // 32
    LAST_ROWS = N - (NB - 1) * BATCH
    KT = NI // P
    QW = KT * 32
    RES = NI - KT * P
    CHUNKS = [7] * 6 + [6] * 6
    assert sum(CHUNKS) == KT
    COFF = [sum(CHUNKS[:c]) for c in range(len(CHUNKS))]
    NCH = len(CHUNKS)
    CW = max(CHUNKS) * 32
    NRAW = 3
    NT = 2
    assert NCH % NRAW == 0 and NCH % NT == 0

    EC = E // P
    VC = 1408
    UC = 512
    NBLK = NB * BATCH // P
    TPB = 6
    CAP = TPB * P
    HG = 8
    OUT_OF_LIST = 131072
    EMPTY = 200 << SRC_BITS
    assert VC % (2 * HG) == 0

    lists = nc.dram_tensor("edge_lists", [NBLK * CAP, 1], I32).ap()
    lanes_dram = nc.dram_tensor("edge_lanes", [NBLK, CAP], BF16).ap()
    valid_dram = nc.dram_tensor("valid_edges", [P, EC], I32).ap()
    unclamped_dram = nc.dram_tensor("unclamped_edges", [P, VC], I32).ap()

    with ExitStack() as ctx:
        def sb(name, shape, dt=F32):
            return ctx.enter_context(nc.sbuf_tensor(name, shape, dt))

        def pb(name, shape, dt=F32):
            return ctx.enter_context(nc.psum_tensor(name, shape, dt))

        ident = sb("ident", [P, P])
        identb = sb("identb", [P, P], BF16)
        negident = sb("negident", [P, P], BF16)
        ones = sb("ones", [P, P])
        iota_lane = sb("iota_lane", [P, P, 24], BF16)
        lane_col = sb("lane_col", [P, 1])
        iota_blk = sb("iota_blk", [P, NBLK])
        clamp_count = sb("clamp_count", [P, NBLK])
        left_count = sb("left_count", [P, 1], I32)

        slot = sb("slot", [P, UC], I32)
        pay = sb("pay", [P, UC], I32)
        w_userT = sb("w_userT", [P, P])
        w_rows = sb("w_rows", [P, ROW])
        bias_user = sb("bias_user", [P, 1])
        h_items = sb("h_items", [P, KT, D])
        h_rest = sb("h_rest", [RES, D])

        prep = ExitStack()
        with prep:
            def psb(name, shape, dt=F32):
                return prep.enter_context(nc.sbuf_tensor(name, shape, dt))

            def sem(name):
                return prep.enter_context(nc.semaphore(name))

            src = psb("src", [P, EC], I32)
            code = psb("code", [P, EC], I32)
            bufA = psb("bufA", [P, EC], I32)
            bufB = psb("bufB", [P, EC], I32)
            bufC = psb("bufC", [P, EC], I32)
            codeB = psb("codeB", [P, VC], I32)
            iota_col = psb("iota_col", [P, VC])
            iota_tail = psb("iota_tail", [P, NBLK, HG], BF16)
            tri = psb("tri", [P, P])
            hot_lane = psb("hot_lane", [P, 2, P, HG], BF16)
            hot_blk = psb("hot_blk", [P, 2, NBLK, HG], BF16)
            lane_bf = psb("lane_bf", [P, VC], BF16)
            blk_bf = psb("blk_bf", [P, VC], BF16)
            nval = psb("nval", [P, 4])
            tot = psb("tot", [P, NBLK])
            base = psb("base", [P, NBLK])
            items = psb("items", [P, KT, D])
            items_rest = psb("items_rest", [RES, D])
            items_t = psb("items_t", [P, 2, 4, P])
            w_in = psb("w_in", [P, 2, D])
            w_itemT = psb("w_itemT", [P, P])
            bias_item = psb("bias_item", [1, 4, D])
            att = psb("att", [P, 2, HE])
            att_w = psb("att_w", [P, 2, HE])
            tr_ps = [prep.enter_context(nc.psum_tensor(f"items_tr{k}", [P, 4, P], F32)) for k in range(2)]
            h_ps = [prep.enter_context(nc.psum_tensor(f"items_h{k}", [P, 4, P], F32)) for k in range(2)]
            empties = psb("empties", [P, NBLK * TPB], I32)
            hist_ps = prep.enter_context(nc.psum_tensor("hist_ps", [P, NBLK], F32))
            base_ps = prep.enter_context(nc.psum_tensor("base_ps", [P, NBLK], F32))

            s_ld = sem("edges_loaded")
            s_const = sem("constants_ready")
            s_pool = sem("pool_step")
            s_dve = sem("vector_step")
            s_hot = sem("onehots_ready")
            s_hist = sem("onehots_used")
            s_z = sem("histogram_cleared")
            s_tot = sem("totals_ready")
            s_base = sem("bases_ready")
            s_left = sem("leftover_ready")
            s_leftp = sem("leftover_summed")
            s_empty = sem("lists_emptied")
            s_slot = sem("slots_ready")
            s_code = sem("codes_ready")
            s_scat = sem("edges_scattered")
            s_save = sem("codes_saved")
            s_w = sem("weights_loaded")
            s_items = sem("items_loaded")
            s_wt = sem("weights_transposed")
            s_wtc = sem("weights_copied")
            s_itr = sem("items_transposed")
            s_itc = sem("items_copied")
            s_hmm = sem("items_projected")
            s_hc = sem("h_copied")
            QUADS = [list(range(q, min(q + 4, KT))) for q in range(0, KT, 4)] + ["rest"]

            block = prep.enter_context(nc.Block())

            @block.sync
            def _(sp):
                e_v = edge_index.rearrange("a (p c) -> a p c", p=P)
                sp.dma_start(code[:, :], e_v[1]).then_inc(s_ld, 16)
                sp.dma_start(src[:, :], e_v[0]).then_inc(s_ld, 16)
                sp.dma_start(w_in[:, 0, :], W_item).then_inc(s_w, 16)
                sp.dma_start(w_in[:, 1, :], W_user).then_inc(s_w, 16)
                for k in range(4):
                    sp.dma_start(bias_item[0:1, k, :], b_item.unsqueeze(0)).then_inc(s_w, 16)
                sp.dma_start(bias_user[:, :], b_user.unsqueeze(1)).then_inc(s_w, 16)
                sp.dma_start(w_rows[:, 0:HE], W_gat).then_inc(s_w, 16)
                for k, a in enumerate((att_src, att_dst)):
                    sp.dma_start(att[:, k, :], a.rearrange("h k -> (h k)").partition_broadcast(P)).then_inc(s_w, 16)
                for q in range(4):
                    sp.dma_start(items[32 * q:32 * q + 32, :, :],
                                 item_feat[QW * q:QW * (q + 1), :].rearrange("(b c) f -> c b f", c=32)
                                 ).then_inc(s_items, 16)
                sp.dma_start(items_rest[:, :], item_feat[KT * P:NI, :]).then_inc(s_items, 16)
                sp.wait_ge(s_const, 1)
                sp.dma_start(lists.rearrange("(p c) a -> p (c a)", p=P), empties[:, :]).then_inc(s_empty, 16)
                sp.wait_ge(s_code, 1)
                sp.dma_start(valid_dram, code[:, :]).then_inc(s_save, 16)
                sp.wait_ge(s_code, 2)
                sp.dma_start(unclamped_dram, codeB[:, :]).then_inc(s_save, 16)
                sp.wait_ge(s_save, 32)

            @block.gpsimd
            def _(pool):
                nc.gpsimd.iota(empties[:, :], [[0, NBLK * TPB]], base=EMPTY, channel_multiplier=0).then_inc(s_pool, 1)
                nc.gpsimd.iota(iota_col[:, :], [[1, VC]], base=0, channel_multiplier=0,
                               allow_small_or_imprecise_dtypes=True).then_inc(s_pool, 1)
                nc.gpsimd.iota(iota_blk[:, :], [[1, NBLK]], base=P, channel_multiplier=0,
                               allow_small_or_imprecise_dtypes=True).then_inc(s_pool, 1)
                nc.gpsimd.iota(iota_tail[:, :, :], [[1, NBLK], [0, HG]], base=P, channel_multiplier=0,
                               allow_small_or_imprecise_dtypes=True).then_inc(s_pool, 1)
                nc.gpsimd.iota(iota_lane[:, :, :], [[1, P], [0, 24]], base=0, channel_multiplier=0,
                               allow_small_or_imprecise_dtypes=True).then_inc(s_pool, 1)
                nc.gpsimd.iota(lane_col[:, :], [[0, 1]], base=0, channel_multiplier=1,
                               allow_small_or_imprecise_dtypes=True).then_inc(s_pool, 1)
                nc.gpsimd.memset(ones[:, :], 1.0).then_inc(s_pool, 1)
                nc.gpsimd.memset(ident[:, :], 0.0).then_inc(s_pool, 1)
                nc.gpsimd.memset(identb[:, :], 0.0).then_inc(s_pool, 1)
                nc.gpsimd.memset(negident[:, :], 0.0).then_inc(s_pool, 1)
                pool.wait_ge(s_pool, 10)
                for m, v in ((ident, 1.0), (identb, 1.0), (negident, -BIG)):
                    nc.gpsimd.affine_select(out=m[:, :], in_=m[:, :], compare_op=ALU.not_equal, fill=v, base=0,
                                            pattern=[[-1, P]], channel_multiplier=1).then_inc(s_pool, 1)
                nc.gpsimd.affine_select(out=tri[:, :], in_=ones[:, :], compare_op=ALU.is_gt, fill=0.0, base=0,
                                        pattern=[[1, P]], channel_multiplier=-1).then_inc(s_pool, 1)
                pool.wait_ge(s_pool, 14)
                pool.nop().then_inc(s_const, 1)
                pool.wait_ge(s_empty, 16)

            @block.tensor
            def _(pe):
                pe.wait_ge(s_const, 1)
                pe.wait_ge(s_w, 16 * 10)
                for k in range(2):
                    nc.tensor.transpose(h_ps[0][:, k, :], w_in[:, k, :], ident[:, :]).then_inc(s_wt, 1)
                pe.wait_ge(s_items, 16 * 5)
                pe.wait_ge(s_wtc, 2)

                def turn(n):
                    if n >= 2:
                        pe.wait_ge(s_itc, n - 1)
                    if QUADS[n] == "rest":
                        mm = nc.tensor.transpose(tr_ps[n % 2][:, 0, 0:RES], items_rest[:, :], ident[0:RES, 0:RES])
                    else:
                        for k, b in enumerate(QUADS[n]):
                            mm = nc.tensor.transpose(tr_ps[n % 2][:, k, :], items[:, b, :], ident[:, :])
                    mm.then_inc(s_itr, 1)

                turn(0)
                for n, quad in enumerate(QUADS):
                    if n + 1 < len(QUADS):
                        turn(n + 1)
                    pe.wait_ge(s_itc, n + 1)
                    if n >= 2:
                        pe.wait_ge(s_hc, n - 1)
                    m = RES if quad == "rest" else P
                    nc.tensor.matmul(h_ps[n % 2][0:m, :, :], ones[0:1, 0:m], bias_item[0:1, :, :], start=True,
                                     stop=False, skip_group_check=True)
                    for k in range(1 if quad == "rest" else len(quad)):
                        mm = nc.tensor.matmul(h_ps[n % 2][0:m, k, :], items_t[:, n % 2, k, 0:m], w_itemT[:, :],
                                              start=False, stop=True, skip_group_check=True)
                    mm.then_inc(s_hmm, 1)
                pe.wait_ge(s_z, 1)
                nc.tensor.matmul(hist_ps[:, :], hot_lane[:, 0, :, 0], hot_blk[:, 0, :, 0], start=True, stop=False,
                                 skip_group_check=True).then_inc(s_hist, 1)
                with pe.Fori(0, VC // (2 * HG)) as g:
                    for half in range(2):
                        pe.wait_ge(s_hot, g * 2 + half + 1)
                        for j in range(HG):
                            mm = nc.tensor.matmul(hist_ps[:, :], hot_lane[:, half, :, j], hot_blk[:, half, :, j],
                                                  start=False, stop=False, skip_group_check=True)
                        mm.then_inc(s_hist, 1)
                pe.wait_ge(s_tot, 1)
                nc.tensor.matmul(base_ps[:, :], tri[:, :], tot[:, :], start=True, stop=True).then_inc(s_base, 1)
                pe.wait_ge(s_left, 1)
                nc.tensor.matmul(base_ps[:, 0:1], ones[:, :], nval[:, 3:4], start=True, stop=True).then_inc(s_leftp, 1)

            @block.scalar
            def _(act):
                act.wait_ge(s_wt, 2)
                nc.scalar.activation(w_itemT[:, :], h_ps[0][:, 0, :], ACT.Copy).then_inc(s_wtc, 1)
                nc.scalar.activation(w_userT[:, :], h_ps[0][:, 1, :], ACT.Copy).then_inc(s_wtc, 1)
                for n in range(len(QUADS) + 1):
                    if n < len(QUADS):
                        act.wait_ge(s_itr, n + 1)
                        if n >= 2:
                            act.wait_ge(s_hmm, n - 1)
                        if QUADS[n] == "rest":
                            nc.scalar.activation(items_t[:, n % 2, 0, 0:RES], tr_ps[n % 2][:, 0, 0:RES],
                                                 ACT.Copy).then_inc(s_itc, 1)
                        else:
                            w = len(QUADS[n])
                            nc.scalar.activation(items_t[:, n % 2, 0:w, :], tr_ps[n % 2][:, 0:w, :],
                                                 ACT.Copy).then_inc(s_itc, 1)
                    if n >= 1:
                        act.wait_ge(s_hmm, n)
                        quad = QUADS[n - 1]
                        if quad == "rest":
                            nc.scalar.activation(h_rest[:, :], h_ps[(n - 1) % 2][0:RES, 0, :],
                                                 ACT.Copy).then_inc(s_hc, 1)
                        else:
                            nc.scalar.activation(h_items[:, quad[0]:quad[0] + len(quad), :],
                                                 h_ps[(n - 1) % 2][:, 0:len(quad), :], ACT.Copy).then_inc(s_hc, 1)

            @block.vector
            def _(dve):
                n = [0]
                v = nc.vector

                def link(ins):
                    n[0] += 1
                    ins.then_inc(s_dve, 1)
                    dve.wait_ge(s_dve, n[0])

                def compact(key, shift, length, spare, marks):
                    for step in compact_stages(length):
                        m = length - step
                        link(v.tensor_scalar(marks, shift, step, None, ALU.bitwise_and))
                        link(v.scalar_tensor_tensor(out=spare, in0=marks, scalar=0.0, in1=shift,
                                                    op0=ALU.is_equal, op1=ALU.mult))
                        link(v.copy_predicated(spare[:, 0:m], marks[:, step:length], shift[:, step:length]))
                        link(v.copy_predicated(key[:, 0:m], marks[:, step:length], key[:, step:length]))
                        spare, shift = shift, spare

                dve.wait_ge(s_w, 16 * 10)
                for k in range(2):
                    link(v.tensor_tensor(att_w[:, k, :], w_rows[:, 0:HE], att[:, k, :], ALU.mult))
                    link(v.tensor_reduce(w_rows[:, HE + HEADS * k:HE + HEADS * (k + 1)],
                                         att_w[:, k, :].rearrange("p (h k) -> p h k", h=HEADS), AX_X, ALU.add))

                dve.wait_ge(s_ld, 32)
                holes = bufB[:, :].bitcast(F32)
                invalid = bufA[:, :].bitcast(F32)
                link(v.tensor_scalar(invalid, code[:, :], float(N), None, ALU.is_ge))
                link(v.tensor_tensor_scan(holes, invalid, invalid, 0.0, ALU.add, ALU.max))
                link(v.scalar_tensor_tensor(out=bufC[:, :], in0=invalid, scalar=0.0, in1=holes,
                                            op0=ALU.is_equal, op1=ALU.mult))
                link(v.tensor_scalar(nval[:, 0:1], holes[:, EC - 1:EC], -1.0, float(EC), ALU.mult, ALU.add))
                link(v.tensor_scalar(src[:, :], src[:, :], float(N - 1), None, ALU.min))
                link(v.tensor_scalar(code[:, :], code[:, :], SRC_BITS, None, ALU.logical_shift_left))
                link(v.tensor_tensor(code[:, :], code[:, :], src[:, :], ALU.bitwise_or))
                compact(code[:, :], bufC[:, :], EC, bufB[:, :], bufA[:, :])
                v.nop().then_inc(s_code, 1)

                dve.wait_ge(s_const, 1)
                third = [b[:, k * VC:(k + 1) * VC] for b in (bufA, bufB, bufC) for k in range(2)]
                kept = code[:, 0:VC]
                dst_i, src_i, lane_i, blk_i = third[0], third[1], third[2], third[3]
                live, clamped = third[4].bitcast(F32), third[5].bitcast(F32)
                loose = src[:, 0:VC].bitcast(F32)
                link(v.tensor_scalar(dst_i, kept, SRC_BITS, None, ALU.logical_shift_right))
                link(v.tensor_scalar(dst_i, dst_i, float(N), None, ALU.min))
                link(v.tensor_scalar(src_i, kept, (1 << SRC_BITS) - 1, None, ALU.bitwise_and))
                link(v.tensor_scalar(live, iota_col[:, :], nval[:, 0:1], None, ALU.is_lt))
                link(v.scalar_tensor_tensor(out=clamped, in0=src_i, scalar=float(N - 1), in1=live,
                                            op0=ALU.is_ge, op1=ALU.mult))
                link(v.scalar_tensor_tensor(out=loose, in0=src_i, scalar=float(N - 1), in1=live,
                                            op0=ALU.is_lt, op1=ALU.mult))
                link(v.tensor_scalar(lane_i, dst_i, P - 1, None, ALU.bitwise_and))
                link(v.tensor_scalar(blk_i, dst_i, LO_BITS, None, ALU.logical_shift_right))
                link(v.tensor_copy(lane_bf[:, :], lane_i))
                link(v.scalar_tensor_tensor(out=blk_bf[:, :], in0=clamped, scalar=float(P), in1=blk_i,
                                            op0=ALU.mult, op1=ALU.add))

                link(v.memset(hot_lane[:, 0, :, 0], 0.0))
                link(v.memset(hot_blk[:, 0, :, 0], 0.0))
                v.nop().then_inc(s_z, 1)
                with dve.Fori(0, VC // (2 * HG)) as g:
                    for half in range(2):
                        dve.wait_ge(s_hist, g * 2 + (half + 1 if half == 0 else 1))
                        at = (g * 2 + half) * HG
                        lanes = lane_bf[:, bass.ds(at, HG)].unsqueeze(1)
                        blks = blk_bf[:, bass.ds(at, HG)].unsqueeze(1)
                        v.tensor_tensor(hot_lane[:, half, :, :], lanes.broadcast_to([P, P, HG]),
                                        iota_lane[:, :, 0:HG], ALU.is_equal)
                        v.tensor_tensor(hot_blk[:, half, :, :], blks.broadcast_to([P, NBLK, HG]),
                                        iota_tail[:, :, :], ALU.is_equal).then_inc(s_hot, 1)
                dve.wait_ge(s_hist, 1 + VC // HG)
                link(v.tensor_copy(clamp_count[:, :], hist_ps[:, :]))

                fixed, holes2 = third[0].bitcast(F32), third[2].bitcast(F32)
                shift2, marks2 = third[4], third[1]
                link(v.tensor_scalar(fixed, loose, 0.0, None, ALU.is_equal))
                link(v.tensor_tensor_scan(holes2, fixed, fixed, 0.0, ALU.add, ALU.max))
                link(v.tensor_tensor(shift2, loose, holes2, ALU.mult))
                link(v.tensor_scalar(nval[:, 1:2], holes2[:, VC - 1:VC], -1.0, float(VC), ALU.mult, ALU.add))
                link(v.tensor_copy(codeB[:, :], kept))
                compact(codeB[:, :], shift2, VC, third[2], marks2)
                v.nop().then_inc(s_code, 1)

                c = [b[:, k * UC:(k + 1) * UC] for b in (bufA, bufB) for k in range(8)]
                blk_of, live2, same, count = (c[k].bitcast(F32) for k in range(4))
                rank, keep = c[4].bitcast(F32), c[5].bitcast(F32)
                short = codeB[:, 0:UC]
                link(v.tensor_scalar(pay[:, :], short, (1 << (SRC_BITS + LO_BITS)) - 1, None, ALU.bitwise_and))
                link(v.tensor_scalar(c[6], short, SRC_BITS + LO_BITS, None, ALU.logical_shift_right))
                link(v.tensor_scalar(c[6], c[6], float(NBLK - 1), None, ALU.min))
                link(v.tensor_scalar(live2, iota_col[:, 0:UC], nval[:, 1:2], None, ALU.is_lt))
                link(v.scalar_tensor_tensor(out=blk_of, in0=live2, scalar=float(P), in1=c[6],
                                            op0=ALU.mult, op1=ALU.add))
                link(v.memset(rank, 0.0))
                for b in range(NBLK):
                    link(v.tensor_scalar(same, blk_of, iota_blk[:, b:b + 1], None, ALU.is_equal, ALU.add,
                                         accum_out=tot[:, b:b + 1]))
                v.nop().then_inc(s_tot, 1)
                dve.wait_ge(s_base, 1)
                link(v.tensor_copy(base[:, :], base_ps[:, :]))
                for b in range(NBLK):
                    link(v.tensor_scalar(same, blk_of, iota_blk[:, b:b + 1], None, ALU.is_equal))
                    link(v.tensor_tensor_scan(count, same, same, base[:, b:b + 1], ALU.add, ALU.max))
                    link(v.copy_predicated(rank, same.bitcast(I32), count))
                link(v.scalar_tensor_tensor(out=keep, in0=rank, scalar=float(CAP), in1=live2,
                                            op0=ALU.is_le, op1=ALU.mult))
                link(v.tensor_tensor_scan(count, live2, keep, 0.0, ALU.add, ALU.subtract))
                link(v.scalar_tensor_tensor(out=same, in0=blk_of, scalar=float(CAP), in1=rank,
                                            op0=ALU.mult, op1=ALU.add))
                link(v.tensor_scalar(same, same, float(-(P * CAP + 1 + OUT_OF_LIST)), None, ALU.add))
                link(v.tensor_tensor(same, same, keep, ALU.mult))
                link(v.tensor_scalar(slot[:, :], same, float(OUT_OF_LIST), None, ALU.add))
                v.nop().then_inc(s_slot, 1)
                link(v.tensor_scalar(nval[:, 0:1], nval[:, 0:1], float(-VC), 0.0, ALU.add, ALU.max))
                link(v.tensor_scalar(nval[:, 1:2], nval[:, 1:2], float(-UC), 0.0, ALU.add, ALU.max))
                link(v.tensor_tensor(nval[:, 2:3], nval[:, 0:1], nval[:, 1:2], ALU.add))
                link(v.tensor_tensor(nval[:, 3:4], nval[:, 2:3], count[:, UC - 1:UC], ALU.add))
                v.nop().then_inc(s_left, 1)
                dve.wait_ge(s_leftp, 1)
                link(v.tensor_copy(left_count[:, :], base_ps[:, 0:1]))

        x1_dram = nc.dram_tensor("x1_rows", [NB * BATCH, D], F32).ap()
        yT_dram = nc.dram_tensor("normed_columns", [NB, P, BATCH], F32).ap()
        table = nc.dram_tensor("node_table", [NB * BATCH, ROW], F32).ap()
        one = ExitStack()
        with one:
            def osb(name, shape, dt=F32):
                return one.enter_context(nc.sbuf_tensor(name, shape, dt))

            def sem(name):
                return one.enter_context(nc.semaphore(name))

            raw = osb("raw", [P, NRAW, GR * CW])
            turned = osb("turned", [P, NT, GR * CW])
            raw_rest = osb("raw_rest", [32, GR, 32])
            turned_rest = osb("turned_rest", [32, GR, 32])
            xt = osb("xt", [P, 2, 4, D])
            u = osb("u", [P, 4, D])
            uT = osb("uT", [P, BATCH])
            rT = osb("rT", [P, BATCH])
            x1 = osb("x1", [P, 2, 4, D])
            y = osb("y", [P, 4, D])
            yT = osb("yT", [P, BATCH])
            rows = osb("rows", [P, 2, 4, ROW])
            stats = osb("stats", [P, 2, 4, 6])
            meanvar = osb("meanvar", [P, 2, 4, 2])
            dev = osb("dev", [P, 2, 4])
            rdev = osb("rdev", [P, 2, 4])
            acc = [one.enter_context(nc.psum_tensor(f"acc{k}", [P, BATCH], F32)) for k in range(2)]
            u_ps = one.enter_context(nc.psum_tensor("u_ps", [P, 4, P], F32))
            r_ps = one.enter_context(nc.psum_tensor("r_ps", [P, 4, P], F32))
            y_ps = one.enter_context(nc.psum_tensor("y_ps", [P, 4, P], F32))
            row_ps = one.enter_context(nc.psum_tensor("row_ps", [P, 4, ROW], F32))

            s_raw = [sem(f"adj_loaded{k}") for k in range(NRAW)]
            s_turn = sem("adj_turned")
            s_mm = sem("chunk_multiplied")
            s_rawr = sem("rest_loaded")
            s_turnr = sem("rest_turned")
            s_mmr = sem("rest_multiplied")
            s_x = [sem(f"x_loaded{k}") for k in range(2)]
            s_var = sem("variances_ready")
            s_dev = sem("deviations_ready")
            s_u = sem("u_ready")
            s_ut = sem("u_turned")
            s_utc = sem("uT_copied")
            s_wu = sem("batch_multiplied")
            s_relu = sem("relu_done")
            s_rt = sem("r_turned")
            s_x1 = sem("x1_ready")
            s_y = sem("y_ready")
            s_yt = sem("y_turned")
            s_ytc = sem("yT_copied")
            s_row = sem("rows_projected")
            s_rowc = sem("rows_copied")
            s_x1st = [sem(f"x1_stored{k}") for k in range(2)]
            s_ytst = sem("yT_stored")
            s_rowst = [sem(f"rows_stored{k}") for k in range(2)]
            s_dve = sem("vector_step")
            s_scat = sem("edges_scattered")
            s_zero = sem("rest_cleared")
            s_past = sem("waits_passed")

            def wait(eng, s, value):
                if not isinstance(value, int) or value > 0:
                    eng.wait_ge(s, value)

            def wait_alone(eng, s, value):
                wait(eng, s, value)
                if not isinstance(value, int):
                    eng.nop().then_inc(s_past, 1)

            def batches(eng, body, tail=None):
                for i in range(3):
                    body(i, i % 2)
                with eng.Fori(0, (NB - 4) // 2) as k:
                    body(k * 2 + 3, 1)
                    body(k * 2 + 4, 0)
                body(NB - 1, 1)
                if tail is not None:
                    tail(NB, 0)

            def half(i, par):
                return i // 2 if isinstance(i, int) else (i - par) // 2

            block = one.enter_context(nc.Block())

            @block.gpsimd
            def _(pool):
                for j in range(UC):
                    nc.gpsimd.indirect_dma_start(
                        lists, bass.IndirectOffsetOnAxis(ap=slot[:, j:j + 1], axis=0), pay[:, j:j + 1], None,
                        bounds_check=NBLK * CAP - 1, oob_is_err=False).then_inc(s_scat, 16)
                pool.wait_ge(s_scat, 16 * UC)


            @block.sync
            def _(sp):
                def body(i, par):
                    last = isinstance(i, int) and i == NB - 1
                    n_rows = LAST_ROWS if last else BATCH
                    whole, over = divmod(n_rows, 32)
                    u0 = i * BATCH

                    def load_rows(dst, cols, signal):
                        src = adj[bass.ds(u0, 32 * whole), cols] if not isinstance(u0, int) else adj[u0:u0 + 32 * whole, cols]
                        sp.dma_start(dst[:, 0:whole, :], src.rearrange("(g r) c -> r g c", r=32)).then_inc(signal, 16)
                        if over:
                            sp.dma_start(dst[0:over, whole, :], adj[u0 + 32 * whole:u0 + n_rows, cols]).then_inc(signal, 16)

                    def rows_of(t, n, i):
                        at = i * BATCH
                        return t[at:at + n, :] if isinstance(at, int) else t[bass.ds(at, n), :]

                    if isinstance(i, int) and i == 0:
                        sp.wait_ge(s_zero, 1)
                    wait_alone(sp, s_x1, i - 1)
                    whole_x, over_x = divmod(n_rows, P)
                    sp.dma_start(xt[:, par, 0:whole_x, :],
                                 rows_of(x, whole_x * P, i).rearrange("(t p) f -> p t f", p=P)).then_inc(s_x[par], 16)
                    if over_x:
                        sp.dma_start(xt[0:over_x, par, whole_x, :], x[u0 + whole_x * P:u0 + n_rows, :]
                                     ).then_inc(s_x[par], 16)
                    wait_alone(sp, s_turnr, i)
                    load_rows(raw_rest[:, :, 0:RES], slice(KT * P, NI), s_rawr)
                    for c, nb in enumerate(CHUNKS):
                        wait_alone(sp, s_turn, i * NCH + c - NRAW + 1)
                        for q in range(4):
                            c0 = QW * q + 32 * COFF[c]
                            load_rows(raw[32 * q:32 * q + 32, c % NRAW, 0:GR * 32 * nb].rearrange(
                                "p (g w) -> p g w", g=GR), slice(c0, c0 + 32 * nb), s_raw[c % NRAW])

                batches(sp, body)

            @block.tensor
            def _(pe):
                def turn_r(i):
                    pe.wait_ge(s_relu, i)
                    wait(pe, s_x1, i - 1)
                    for k in range(4):
                        mm = nc.tensor.transpose(r_ps[:, k, :], rT[:, k * P:(k + 1) * P], ident[:, :])
                    mm.then_inc(s_rt, 1)

                def turn_y(i):
                    pe.wait_ge(s_y, i)
                    wait(pe, s_ytc, i - 1)
                    for k in range(4):
                        mm = nc.tensor.transpose(y_ps[:, k, :], y[:, k, :], ident[:, :])
                    mm.then_inc(s_yt, 1)

                def project(i):
                    pe.wait_ge(s_ytc, i)
                    wait(pe, s_rowc, i - 1)
                    for k in range(4):
                        mm = nc.tensor.matmul(row_ps[:, k, :], yT[:, k * P:(k + 1) * P], w_rows[:, :],
                                              start=(k == 0), stop=True, skip_group_check=True)
                    mm.then_inc(s_row, 1)

                def body(i, par):
                    first = isinstance(i, int) and i == 0
                    wait(pe, s_relu, i - 1)
                    pe.wait_ge(s_turnr, i + 1)
                    nc.tensor.matmul(acc[par][:, :], h_rest[:, :], turned_rest[0:RES, :, :], start=True, stop=False,
                                     skip_group_check=True).then_inc(s_mmr, 1)
                    for c, nb in enumerate(CHUNKS):
                        pe.wait_ge(s_turn, i * NCH + c + 1)
                        t = turned[:, c % NT, 0:GR * 32 * nb].rearrange("p (g b r) -> p g b r", g=GR, b=nb)
                        for b in range(nb):
                            mm = nc.tensor.matmul(acc[par][:, :], h_items[:, COFF[c] + b, :], t[:, :, b, :],
                                                  start=False, stop=False, skip_group_check=True)
                        mm.then_inc(s_mm, 1)
                        if c == 1 and not first:
                            turn_r(i)
                        if c == 4:
                            pe.wait_ge(s_u, i + 1)
                            wait(pe, s_utc, i)
                            for k in range(4):
                                mm = nc.tensor.transpose(u_ps[:, k, :], u[:, k, :], ident[:, :])
                            mm.then_inc(s_ut, 1)
                        if c == 7 and not first:
                            turn_y(i)
                        if c == 9 and not first:
                            project(i)
                    pe.wait_ge(s_utc, i + 1)
                    nc.tensor.matmul(acc[par][:, :], w_userT[:, :], uT[:, :], start=False, stop=True,
                                     skip_group_check=True).then_inc(s_wu, 1)

                def tail(i, par):
                    turn_r(i)
                    turn_y(i)
                    project(i)

                batches(pe, body, tail)

            @block.scalar
            def _(act):
                def relu(i, par):
                    act.wait_ge(s_wu, i)
                    wait(act, s_rt, i - 1)
                    nc.scalar.activation(rT[:, :], acc[par][:, :], ACT.Relu, bias=bias_user[:, 0:1]).then_inc(s_relu, 1)

                def root(which, value):
                    act.wait_ge(s_var, value)
                    nc.scalar.activation(dev[:, which, :], meanvar[:, which, :, 1], ACT.Sqrt).then_inc(s_dev, 1)

                def finish(i, par):
                    act.wait_ge(s_yt, i)
                    wait(act, s_row, i - 1)
                    wait(act, s_ytst, (i - 1) * 16)
                    nc.scalar.activation(yT[:, :], y_ps[:, :, :], ACT.Copy).then_inc(s_ytc, 1)
                    act.wait_ge(s_ytc, i)
                    act.dma_start(yT_dram[i - 1] if isinstance(i, int) else
                                  yT_dram[bass.ds(i - 1, 1)].rearrange("a p c -> p (a c)"), yT[:, :]).then_inc(s_ytst, 16)
                    act.wait_ge(s_row, i)
                    wait(act, s_rowst[par], half(i - 1, par) * 16)
                    nc.scalar.activation(rows[:, par, :, :], row_ps[:, :, :], ACT.Copy).then_inc(s_rowc, 1)
                    act.wait_ge(s_rowc, i)
                    act.dma_start(dram_rows(table, i), rows[:, par, :, :]).then_inc(s_rowst[par], 16)

                def dram_rows(t, i):
                    at = (i - 1) * BATCH
                    r = t[at:at + BATCH, :] if isinstance(at, int) else t[bass.ds(at, BATCH), :]
                    return r.rearrange("(t p) f -> p t f", p=P)

                def body(i, par):
                    first = isinstance(i, int) and i == 0
                    if not first:
                        relu(i, 1 - par)
                    root(0, i * 2 + (1 if first else 0) if first else i * 2)
                    act.wait_ge(s_ut, i + 1)
                    wait(act, s_wu, i)
                    nc.scalar.activation(uT[:, :], u_ps[:, :, :], ACT.Copy).then_inc(s_utc, 1)
                    if not first:
                        root(1, i * 2 + 1)
                        act.wait_ge(s_x1, i)
                        act.dma_start(dram_rows(x1_dram, i), x1[:, 1 - par, :, :]).then_inc(s_x1st[1 - par], 16)
                        finish(i, 1 - par)

                def tail(i, par):
                    relu(i, 1)
                    root(1, i * 2)
                    act.wait_ge(s_x1, i)
                    act.dma_start(dram_rows(x1_dram, i), x1[:, 1, :, :]).then_inc(s_x1st[1], 16)
                    finish(i, 1)
                    for k in range(2):
                        act.wait_ge(s_x1st[k], NB // 2 * 16)
                        act.wait_ge(s_rowst[k], NB // 2 * 16)
                    act.wait_ge(s_ytst, NB * 16)

                batches(act, body, tail)

            @block.vector
            def _(dve):
                v = nc.vector
                LINKS = 13
                at = [0, 0]

                def link(ins):
                    at[1] += 1
                    ins.then_inc(s_dve, 1)
                    dve.wait_ge(s_dve, at[0] + at[1])

                def spread(src, which):
                    for k in range(4):
                        ins = v.bn_stats(stats[:, which, k, :], src[:, k, :])
                    at[1] += 1
                    ins.then_inc(s_dve, 1)
                    wait_alone(dve, s_dve, at[0] + at[1])
                    for k in range(4):
                        ins = v.bn_aggr(meanvar[:, which, k, :], stats[:, which, k, :])
                    link(ins)
                    v.tensor_scalar(meanvar[:, which, :, 1], meanvar[:, which, :, 1], LN_EPS, None,
                                    ALU.add).then_inc(s_var, 1)

                def normalize(dst, src, which, value):
                    dve.wait_ge(s_dev, value)
                    link(v.reciprocal(rdev[:, which, :], dev[:, which, :]))
                    for k in range(4):
                        ins = v.tensor_scalar(dst[:, k, :], src[:, k, :], meanvar[:, which, k, 0:1],
                                              rdev[:, which, k:k + 1], ALU.subtract, ALU.mult)
                    return ins

                def x1_stats(i, par):
                    dve.wait_ge(s_rt, i)
                    wait(dve, s_x1st[par], half(i - 1, par) * 16)
                    ins = v.tensor_tensor(x1[:, par, :, :], r_ps[:, :, :], xt[:, par, :, :], ALU.add)
                    ins.then_inc(s_x1, 1)
                    dve.wait_ge(s_x1, i)
                    spread(x1[:, par, :, :], 1)

                def y_norm(i, par, value):
                    wait(dve, s_yt, i - 1)
                    normalize(y, x1[:, par, :, :], 1, value).then_inc(s_y, 1)

                def body(i, par):
                    first = isinstance(i, int) and i == 0
                    at[0], at[1] = (0, 0) if first else ((i - 1) * 6 + 3, 0)
                    last = isinstance(i, int) and i == NB - 1
                    if first:
                        v.memset(xt[:, :, :, :], 0.0)
                        v.memset(raw_rest[:, :, :], 0.0).then_inc(s_zero, 1)
                    wait(dve, s_mmr, i)
                    dve.wait_ge(s_rawr, 32 * 0 + (i + 1) * 16 + (16 if last else 0))
                    v.transpose(turned_rest[:, :, :].rearrange("p g r -> p (g r)"),
                                raw_rest[:, :, :].rearrange("p g r -> p (g r)")).then_inc(s_turnr, 1)
                    for c, nb in enumerate(CHUNKS):
                        n = GR * 32 * nb
                        wait(dve, s_mm, i * NCH + c - NT + 1)
                        extra = 64 * (c // NRAW + 1) if last else 0
                        dve.wait_ge(s_raw[c % NRAW], (i * (NCH // NRAW) + c // NRAW + 1) * 64 + extra)
                        v.transpose(turned[:, c % NT, 0:n], raw[:, c % NRAW, 0:n]).then_inc(s_turn, 1)
                        if c == 1:
                            dve.wait_ge(s_x[par], half(i, par) * 16 + 16 + (16 if last else 0))
                            spread(xt[:, par, :, :], 0)
                        if c == 2:
                            wait(dve, s_ut, i)
                            normalize(u, xt[:, par, :, :], 0, 1 if first else i * 2).then_inc(s_u, 1)
                        if c == 4 and not first:
                            x1_stats(i, 1 - par)
                        if c == 5 and not first:
                            y_norm(i, 1 - par, i * 2 + 1)

                def tail(i, par):
                    at[0], at[1] = (NB - 1) * 6 + 3, 0
                    x1_stats(i, 1)
                    y_norm(i, 1, i * 2)

                batches(dve, body, tail)

        UB = BATCH // P
        UT = UB * TPB
        TRI = 3
        NTRI = UT // TRI
        PARTS = 3
        HALVES = FF // P
        NF = EXP * HALVES
        TP8 = 8
        NTP = UT // TP8
        MX = NTRI * HEADS
        ND = HE + HEADS

        def slots(eng, body, tail=None):
            for i in range(3):
                body(i, i % 2)
            with eng.Fori(0, (NB - 4) // 2) as k:
                body(k * 2 + 3, 1)
                body(k * 2 + 4, 0)
            body(NB - 1, 1)
            if tail is not None:
                tail(NB, 0)

        def seen(i, par):
            return i // 2 if isinstance(i, int) else (i - par) // 2

        def from_(i, least):
            return not isinstance(i, int) or i >= least

        gate = sb("gate", [P, NBLK, EXP])

        two = ExitStack()
        with two:
            def tsb(name, shape, dt=F32):
                return two.enter_context(nc.sbuf_tensor(name, shape, dt))

            def sem(name):
                return two.enter_context(nc.semaphore(name))

            entry = tsb("entry", [P, NBLK, TPB], I32)
            source = tsb("source", [P, NBLK * TPB], I32)
            source_now = tsb("source_now", [P, 2, UT], I32)
            lane_i = tsb("lane_i", [P, NBLK * TPB], I32)
            lane_e = tsb("lane_e", [P, NBLK * TPB], BF16)
            list_rows = tsb("list_rows", [NBLK, CAP], I32)
            lane_rows = tsb("lane_rows", [NBLK, CAP], BF16)
            nodes = tsb("nodes", [P, NBLK, ROW])
            last_row = tsb("last_row", [P, ROW])
            no_clamp = tsb("no_clamp", [P, NBLK])
            floor_max = tsb("floor_max", [P, NBLK, HEADS])
            e_self = tsb("e_self", [P, NBLK, 2, HEADS])
            part_sel = tsb("part_sel", [PARTS * HEADS, HEADS, P], BF16)
            bg = tsb("bg", [P, HE])
            gamma = tsb("gamma", [P, HE])
            beta = tsb("beta", [P, HE])

            gath = tsb("gath", [P, 2, UT, ROW])
            held = tsb("held", [P, 2, UT, ROW])
            lane_bc = tsb("lane_bc", [P, 2, UB * CAP], BF16)
            as_cut = tsb("as_cut", [P, UT, PARTS, HEADS], BF16)
            as_res = tsb("as_res", [P, UT, HEADS])
            asT = tsb("asT", [PARTS * HEADS, UT * P], BF16)
            maskT = tsb("maskT", [P, UT, P], BF16)
            hotT = tsb("hotT", [P, 2, UT, P], BF16)
            hot = tsb("hot", [P, 2, P, UT], BF16)
            junk = tsb("junk", [P, 4, TRI * P], BF16)
            mx = tsb("mx", [P, UB, 2, HEADS])
            am = tsb("am", [P, UB, 2 * HEADS])
            tmp4 = tsb("tmp4", [P, UB, HEADS])
            am_cut = tsb("am_cut", [P, UB, PARTS, 2 * HEADS], BF16)
            am_res = tsb("am_res", [P, UB, 2 * HEADS])
            am_e = tsb("am_e", [P, UT, 2 * HEADS])
            logit = tsb("logit", [P, UT + 2 * UB, HEADS])
            weight = tsb("weight", [P, UT + 2 * UB, HEADS])
            pay_e = tsb("pay_e", [P, UT, ND])
            pay_cut = tsb("pay_cut", [P, UT, PARTS, ND], BF16)
            pay_res = tsb("pay_res", [P, UT, ND])
            own = tsb("own", [P, UB, ND])
            own_b = tsb("own_b", [P, UB, HE])
            nd = tsb("nd", [P, UB, ND])
            nd_all = tsb("nd_all", [P, NBLK, ND])
            tmp16 = tsb("tmp16", [P, NBLK, HE])
            tmp16b = tsb("tmp16b", [P, NBLK, HE])
            inv = tsb("inv", [P, NBLK, HEADS])
            col = tsb("col", [P, 6, NBLK])
            score = tsb("score", [P, NBLK, EXP])
            cmpb = tsb("cmpb", [P, NBLK, EXP])
            order = tsb("order", [P, NBLK, EXP])
            gexp = tsb("gexp", [P, NBLK, EXP])

            as_ps = [two.enter_context(nc.psum_tensor(f"as_rows{k}", [P, TRI * P], F32)) for k in range(HEADS)]
            am_ps = [two.enter_context(nc.psum_tensor(f"am_rows{k}", [P, UT // 2 * PARTS * 2 * HEADS], F32))
                     for k in range(2)]
            turn_ps = two.enter_context(nc.psum_tensor("as_turned_ps", [PARTS * HEADS, TP8 * P], BF16))
            agg_ps = two.enter_context(nc.psum_tensor("agg", [P, UB, PARTS, ND], F32))

            s_in = sem("setup_loaded")
            s_rows2 = sem("lane_rows_ready")
            s_lanes = sem("lane_rows_stored")
            s_src = sem("sources_ready")
            s_sel = sem("selectors_ready")
            s_past = sem("waits_passed")
            s_idx = sem("indices_copied")
            s_gath = [sem(f"rows_gathered{k}") for k in range(2)]
            s_held = sem("rows_held")
            s_bc = [sem(f"lanes_spread{k}") for k in range(2)]
            s_ast = sem("as_cut_ready")
            s_tp = sem("as_turned")
            s_tpc = sem("as_copied")
            s_hotT = sem("lane_onehots_ready")
            s_mask = sem("masks_ready")
            s_as = sem("as_spread")
            s_mx = sem("maxima_taken")
            s_am = sem("am_ready")
            s_ame = sem("am_spread")
            s_amr = sem("am_read")
            s_log = sem("logits_ready")
            s_exp = sem("weights_ready")
            s_pay = sem("payload_ready")
            s_agg = sem("payload_summed")
            s_nd = sem("sums_read")
            s_sq = sem("score_variance_ready")
            s_sqd = sem("score_deviation_ready")
            s_ge = sem("gate_logits_ready")
            s_ged = sem("gate_exponentials_ready")
            s_dve = sem("vector_step")
            SETUP_LOADS = 4 + 3

            def wait_alone(eng, s, value):
                eng.wait_ge(s, value)
                if not isinstance(value, int):
                    eng.nop().then_inc(s_past, 1)

            block = two.enter_context(nc.Block())

            @block.sync
            def _(sp):
                sp.dma_start(entry[:, :, :], lists.rearrange("(b p t) a -> p b (t a)", b=NBLK, p=P)).then_inc(s_in, 16)
                sp.dma_start(list_rows[:, :], lists.rearrange("(b c) a -> b (c a)", b=NBLK)).then_inc(s_in, 16)
                sp.dma_start(nodes[:, :, :], table.rearrange("(b p) c -> p b c", p=P)).then_inc(s_in, 16)
                sp.dma_start(last_row[:, :], table[N - 1, :].partition_broadcast(P)).then_inc(s_in, 16)
                for t, a in ((bg, b_gat), (gamma, ln_gamma), (beta, ln_beta)):
                    sp.dma_start(t[:, :], a.partition_broadcast(P)).then_inc(s_in, 16)
                sp.wait_ge(s_rows2, 1)
                sp.dma_start(lanes_dram, lane_rows[:, :]).then_inc(s_lanes, 16)
                sp.wait_ge(s_lanes, 16)

                def body(i, par):
                    if from_(i, 2):
                        wait_alone(sp, s_hotT, i - 1)
                    lanes = lanes_dram[i * UB:(i + 1) * UB, :] if isinstance(i, int) else lanes_dram[bass.ds(i * UB, UB), :]
                    sp.dma_start(lane_bc[:, par, :], lanes.rearrange("b c -> (b c)").partition_broadcast(P)
                                 ).then_inc(s_bc[par], 16)

                slots(sp, body)

            @block.gpsimd
            def _(pool):
                nc.gpsimd.memset(part_sel[:, :, :], 0.0).then_inc(s_sel, 1)
                for k in range(PARTS):
                    pool.wait_ge(s_sel, 1 + k)
                    nc.gpsimd.affine_select(out=part_sel[:, :, :], in_=part_sel[:, :, :], compare_op=ALU.not_equal,
                                            fill=1.0, base=-HEADS * k, pattern=[[-1, HEADS], [0, P]],
                                            channel_multiplier=1).then_inc(s_sel, 1)
                pool.wait_ge(s_src, 1)

                def body(i, par):
                    if from_(i, 2):
                        wait_alone(pool, s_held, i - 1)
                        pool.wait_ge(s_gath[par], seen(i, par) * 16 * UT)
                    at = i * UT
                    nc.gpsimd.tensor_copy(source_now[:, par, :], source[:, at:at + UT] if isinstance(at, int) else
                                          source[:, bass.ds(at, UT)]).then_inc(s_idx, 1)
                    wait_alone(pool, s_idx, i + 1)
                    for t in range(UT):
                        nc.gpsimd.indirect_dma_start(
                            gath[:, par, t, :], None, table,
                            bass.IndirectOffsetOnAxis(ap=source_now[:, par, t:t + 1], axis=0),
                            bounds_check=N - 1, oob_is_err=False).then_inc(s_gath[par], 16)

                slots(pool, body)

            @block.tensor
            def _(pe):
                def turn_as(i, k):
                    if k == 0:
                        pe.wait_ge(s_ast, i + 1)
                    else:
                        pe.wait_ge(s_tpc, i * NTP + k)
                    for t in range(TP8):
                        mm = nc.tensor.transpose(turn_ps[:, t * P:(t + 1) * P],
                                                 as_cut[:, k * TP8 + t, :, :].rearrange("p a h -> p (a h)"), identb[:, :])
                    mm.then_inc(s_tp, 1)

                def spread_as(i, tri):
                    pe.wait_ge(s_tpc, i * NTP + (tri * TRI + TRI - 1) // TP8 + 1)
                    for h in range(HEADS):
                        if from_(i, 1) or tri >= 1:
                            pe.wait_ge(s_mx, i * MX + (tri - 1) * HEADS + h + 1)
                        nc.tensor.matmul(as_ps[h][:, :], part_sel[:, h, :], asT[:, tri * TRI * P:(tri + 1) * TRI * P],
                                         start=True, stop=True).then_inc(s_as, 1)

                def spread_am(i, par):
                    pe.wait_ge(s_am, i + 1)
                    if from_(i, 1):
                        pe.wait_ge(s_amr, i * 2)
                    for k in range(2):
                        for t in range(UT // 2):
                            n = k * (UT // 2) + t
                            w = PARTS * 2 * HEADS
                            mm = nc.tensor.matmul(am_ps[k][:, t * w:(t + 1) * w], hotT[:, par, n, :],
                                                  am_cut[:, n // TPB, :, :], start=(t == 0), stop=True,
                                                  skip_group_check=True)
                        mm.then_inc(s_ame, 1)

                def gather_sum(i, par):
                    pe.wait_ge(s_pay, i)
                    if from_(i, 2):
                        pe.wait_ge(s_nd, i - 1)
                    for t in range(UT):
                        mm = nc.tensor.matmul(agg_ps[:, t // TPB, :, :], hot[:, par, :, t], pay_cut[:, t, :, :],
                                              start=(t == 0), stop=(t % TPB == TPB - 1), skip_group_check=True)
                    mm.then_inc(s_agg, 1)

                pe.wait_ge(s_sel, 1 + PARTS)

                def body(i, par):
                    turn_as(i, 0)
                    turn_as(i, 1)
                    spread_as(i, 0)
                    spread_as(i, 1)
                    turn_as(i, 2)
                    for tri in range(2, NTRI):
                        spread_as(i, tri)
                    if from_(i, 1):
                        gather_sum(i, 1 - par)
                    spread_am(i, par)

                def tail(i, par):
                    gather_sum(i, 1 - par)

                slots(pe, body, tail)

            @block.scalar
            def _(act):
                def weights(i):
                    act.wait_ge(s_log, i)
                    nc.scalar.activation(weight[:, :, :], logit[:, :, :], ACT.Exp).then_inc(s_exp, 1)

                def copy_turned(i, k):
                    act.wait_ge(s_tp, i * NTP + k + 1)
                    if k == 0 and from_(i, 1):
                        act.wait_ge(s_as, i * MX)
                    nc.scalar.activation(asT[:, k * TP8 * P:(k + 1) * TP8 * P], turn_ps[:, :], ACT.Copy
                                         ).then_inc(s_tpc, 1)

                def body(i, par):
                    act.wait_ge(s_gath[par], (seen(i, par) + 1) * 16 * UT)
                    if from_(i, 2):
                        act.wait_ge(s_pay, i - 1)
                    nc.scalar.activation(held[:, par, :, :], gath[:, par, :, :], ACT.Copy).then_inc(s_held, 1)
                    if from_(i, 1):
                        weights(i)
                    copy_turned(i, 0)
                    copy_turned(i, 1)
                    act.wait_ge(s_hotT, i + 1)
                    if from_(i, 1):
                        act.wait_ge(s_mx, i * MX)
                    nc.scalar.activation(maskT[:, :, :], hotT[:, par, :, :], ACT.Copy, bias=-BIG, scale=BIG
                                         ).then_inc(s_mask, 1)
                    copy_turned(i, 2)

                def tail(i, par):
                    weights(i)
                    act.wait_ge(s_sq, 1)
                    nc.scalar.activation(col[:, 3, :], col[:, 2, :], ACT.Sqrt).then_inc(s_sqd, 1)
                    act.wait_ge(s_ge, 1)
                    nc.scalar.activation(gexp[:, :, :], cmpb[:, :, :], ACT.Exp).then_inc(s_ged, 1)

                slots(act, body, tail)

            @block.vector
            def _(dve):
                v = nc.vector
                at = [0, 0]
                LINKS = [0]

                def link(ins):
                    at[1] += 1
                    ins.then_inc(s_dve, 1)
                    dve.wait_ge(s_dve, at[0] + at[1])

                def cut(parts, value, residue):
                    link(v.tensor_copy(parts(0), value))
                    link(v.tensor_tensor(residue, value, parts(0), ALU.subtract))
                    link(v.tensor_copy(parts(1), residue))
                    link(v.tensor_tensor(residue, residue, parts(1), ALU.subtract))
                    return v.tensor_copy(parts(2), residue)

                def leaky(t):
                    link(v.scalar_tensor_tensor(out=t, in0=t, scalar=0.2, in1=t, op0=ALU.mult, op1=ALU.max))

                dve.wait_ge(s_in, 16 * SETUP_LOADS)
                link(v.tensor_scalar(source[:, :], entry[:, :, :].rearrange("p b t -> p (b t)"), (1 << SRC_BITS) - 1, None,
                                     ALU.bitwise_and))
                v.nop().then_inc(s_src, 1)
                link(v.tensor_scalar(list_rows[:, :], list_rows[:, :], SRC_BITS, None, ALU.logical_shift_right))
                v.tensor_copy(lane_rows[:, :], list_rows[:, :]).then_inc(s_rows2, 1)
                link(v.tensor_scalar(lane_i[:, :], entry[:, :, :].rearrange("p b t -> p (b t)"), SRC_BITS, None,
                                     ALU.logical_shift_right))
                link(v.tensor_copy(lane_e[:, :], lane_i[:, :]))
                a_src, a_dst = nodes[:, :, HE:HE + HEADS], nodes[:, :, HE + HEADS:ROW]
                last_as = last_row[:, HE:HE + HEADS].unsqueeze(1).broadcast_to([P, NBLK, HEADS])
                link(v.tensor_scalar(no_clamp[:, :], clamp_count[:, :], 0.0, -BIG, ALU.is_equal, ALU.mult))
                link(v.tensor_tensor(floor_max[:, :, :], last_as,
                                     no_clamp[:, :].unsqueeze(2).broadcast_to([P, NBLK, HEADS]), ALU.add))
                link(v.tensor_tensor(floor_max[:, :, :], floor_max[:, :, :], a_src, ALU.max))
                link(v.tensor_tensor(e_self[:, :, 0, :], a_src, a_dst, ALU.add))
                link(v.tensor_tensor(e_self[:, :, 1, :], last_as, a_dst, ALU.add))
                leaky(e_self[:, :, :, :])
                SETUP_LINKS = at[1]

                def blk(t, i, *rest):
                    b0 = i * UB
                    key = slice(b0, b0 + UB) if isinstance(i, int) else bass.ds(b0, UB)
                    return t[(slice(None), key) + rest]

                h4 = "p b (h k) -> p b h k"

                def logits(i, par):
                    half_t = UT // 2
                    w = PARTS * 2 * HEADS
                    for k in range(2):
                        dve.wait_ge(s_ame, i * 2 + k - 1)
                        v.tensor_reduce(am_e[:, k * half_t:(k + 1) * half_t, :],
                                        am_ps[k][:, 0:half_t * w].rearrange("p (t a c) -> p t c a", t=half_t, a=PARTS),
                                        AX_X, ALU.add).then_inc(s_amr, 1)
                    dve.wait_ge(s_amr, i * 2)
                    lg = logit[:, 0:UT, :]
                    link(v.tensor_tensor(lg, held[:, par, :, HE:HE + HEADS], am_e[:, :, 0:HEADS], ALU.add))
                    leaky(lg)
                    v.tensor_tensor(lg, lg, am_e[:, :, HEADS:2 * HEADS], ALU.subtract).then_inc(s_log, 1)

                def payload(i, par):
                    dve.wait_ge(s_exp, i)
                    wt = weight[:, 0:UT, :]
                    v.tensor_copy(pay_e[:, :, HE:ND], wt)
                    link(v.tensor_tensor(pay_e[:, :, 0:HE].rearrange("p t (h k) -> p t h k", h=HEADS),
                                         held[:, par, :, 0:HE].rearrange("p t (h k) -> p t h k", h=HEADS),
                                         wt.unsqueeze(3).broadcast_to([P, UT, HEADS, EXP]), ALU.mult))
                    cut(lambda k: pay_cut[:, :, k, :], pay_e[:, :, :], pay_res[:, :, :]).then_inc(s_pay, 1)
                    sw = weight[:, UT:UT + 2 * UB, :].rearrange("p (b s) h -> p b s h", s=2)
                    w_self, w_last = sw[:, :, 0, :], sw[:, :, 1, :]
                    v.tensor_tensor(own[:, :, 0:HE].rearrange(h4, h=HEADS),
                                    blk(nodes, i - 1, slice(0, HE)).rearrange(h4, h=HEADS),
                                    w_self.unsqueeze(3).broadcast_to([P, UB, HEADS, EXP]), ALU.mult)
                    link(v.tensor_tensor(w_last, w_last, blk(clamp_count, i - 1).unsqueeze(2).broadcast_to([P, UB, HEADS]),
                                         ALU.mult))
                    v.tensor_tensor(own[:, :, HE:ND], w_self, w_last, ALU.add)
                    link(v.tensor_tensor(own_b[:, :, :].rearrange(h4, h=HEADS),
                                         last_row[:, 0:HE].unsqueeze(1).broadcast_to([P, UB, HE]).rearrange(h4, h=HEADS),
                                         w_last.unsqueeze(3).broadcast_to([P, UB, HEADS, EXP]), ALU.mult))
                    link(v.tensor_tensor(own[:, :, 0:HE], own[:, :, 0:HE], own_b[:, :, :], ALU.add))

                def sums(i):
                    dve.wait_ge(s_agg, i)
                    link(v.tensor_reduce(nd[:, :, :], agg_ps[:, :, :, :].rearrange("p b a c -> p b c a"), AX_X, ALU.add))
                    v.tensor_tensor(blk(nd_all, i - 1, slice(None)), nd[:, :, :], own[:, :, :], ALU.add
                                    ).then_inc(s_nd, 1)

                def body(i, par):
                    first = isinstance(i, int) and i == 0
                    at[0], at[1] = (SETUP_LINKS, 0) if first else \
                        (SETUP_LINKS + LINKS[0] + (i - 1) * LINKS[-1], 0) if not (isinstance(i, int) and i == 1) else \
                        (SETUP_LINKS + LINKS[0], 0)
                    if not first:
                        logits(i, 1 - par)
                    dve.wait_ge(s_held, i + 1)
                    if not first:
                        dve.wait_ge(s_tp, i * NTP)
                    g_as = held[:, par, :, HE:HE + HEADS]
                    cut(lambda k: as_cut[:, :, k, :], g_as, as_res[:, :, :]).then_inc(s_ast, 1)
                    dve.wait_ge(s_bc[par], (seen(i, par) + 1) * 16)
                    lanes = lane_bc[:, par, :].rearrange("q (b p t) -> q b t p", b=UB, p=P)
                    hv = hotT[:, par, :, :].rearrange("q (b t) p -> q b t p", b=UB)
                    for b in range(UB):
                        ins = v.tensor_scalar(hv[:, b], lanes[:, b], lane_col[:, 0:1], None, ALU.is_equal)
                    ins.then_inc(s_hotT, 1)
                    le = lane_e[:, i * UT:(i + 1) * UT] if isinstance(i, int) else lane_e[:, bass.ds(i * UT, UT)]
                    v.tensor_tensor(hot[:, par, :, :], le.unsqueeze(1).broadcast_to([P, P, UT]), iota_lane[:, :, :],
                                    ALU.is_equal)
                    if not first:
                        payload(i, 1 - par)
                    wait_alone(dve, s_mask, i + 1)
                    for tri in range(NTRI):
                        for h in range(HEADS):
                            n = tri * HEADS + h
                            wait_alone(dve, s_as, i * MX + n + 1)
                            v.tensor_tensor_reduce(
                                out=junk[:, h, :], in0=as_ps[h][:, :],
                                in1=maskT[:, tri * TRI:(tri + 1) * TRI, :].rearrange("q t p -> q (t p)"),
                                scale=1.0, scalar=-BIG, op0=ALU.add, op1=ALU.max,
                                accum_out=mx[:, tri // 2, tri % 2, h:h + 1]).then_inc(s_mx, 1)
                    v.tensor_copy(am[:, :, 0:HEADS], blk(nodes, i, slice(HE + HEADS, ROW)))
                    dve.wait_ge(s_mx, (i + 1) * MX)
                    m = am[:, :, HEADS:2 * HEADS]
                    link(v.tensor_tensor(m, mx[:, :, 0, :], mx[:, :, 1, :], ALU.max))
                    link(v.tensor_tensor(m, m, blk(floor_max, i, slice(None)), ALU.max))
                    link(v.tensor_tensor(m, m, am[:, :, 0:HEADS], ALU.add))
                    leaky(m)
                    cut(lambda k: am_cut[:, :, k, :], am[:, :, :], am_res[:, :, :]).then_inc(s_am, 1)
                    sl = logit[:, UT:UT + 2 * UB, :].rearrange("p (b s) h -> p b s h", s=2)
                    link(v.tensor_tensor(sl, blk(e_self, i, slice(None), slice(None)),
                                         m.unsqueeze(2).broadcast_to([P, UB, 2, HEADS]), ALU.subtract))
                    link(v.tensor_scalar(logit[:, UT:UT + 2 * UB, :], logit[:, UT:UT + 2 * UB, :], 0.0, None, ALU.min))
                    if not first:
                        sums(i)
                    if first or (isinstance(i, int) and i == 1):
                        LINKS.append(at[1])
                        if first:
                            LINKS[0] = at[1]
                    assert at[1] == (LINKS[0] if first else LINKS[-1])

                def tail(i, par):
                    at[0], at[1] = SETUP_LINKS + LINKS[0] + (i - 1) * LINKS[-1], 0
                    logits(i, 1 - par)
                    payload(i, 1 - par)
                    sums(i)
                    dve.wait_ge(s_nd, NB)
                    link(v.tensor_scalar(inv[:, :, :], nd_all[:, :, HE:ND], 1e-16, None, ALU.add))
                    link(v.reciprocal(inv[:, :, :], inv[:, :, :]))
                    link(v.tensor_tensor(tmp16[:, :, :].rearrange(h4, h=HEADS),
                                         nd_all[:, :, 0:HE].rearrange(h4, h=HEADS),
                                         inv[:, :, :].unsqueeze(3).broadcast_to([P, NBLK, HEADS, EXP]), ALU.mult))
                    center(v, link, tmp16[:, :, :], bg, tmp16b, col, NBLK).then_inc(s_sq, 1)
                    dve.wait_ge(s_sqd, 1)
                    rank_scores(v, link, tmp16[:, :, :], gamma, beta, col, score, order, cmpb, NBLK).then_inc(s_ge, 1)
                    dve.wait_ge(s_ged, 1)
                    link(share_gates(v, link, order, gexp, col, gate[:, :, :], NBLK))

                slots(dve, body, tail)

        three = ExitStack()
        with three:
            def tsb(name, shape, dt=F32):
                return three.enter_context(nc.sbuf_tensor(name, shape, dt))

            def sem(name):
                return three.enter_context(nc.semaphore(name))

            NHID, NOUT = 4, 4
            w1_sb = tsb("w1_sb", [P, EXP, FF])
            w2_sb = tsb("w2_sb", [P, EXP, HALVES, D])
            b1_sb = tsb("b1_sb", [P, EXP, HALVES])
            b2_row = tsb("b2_row", [1, EXP * D])
            b2_res = tsb("b2_res", [1, EXP * D])
            b2_cut = tsb("b2_cut", [1, PARTS, EXP * D], BF16)
            b2_parts = tsb("b2_parts", [PARTS, EXP * D], BF16)
            onesb = tsb("onesb", [PARTS, P], BF16)
            yTu = tsb("yTu", [P, 2, BATCH])
            x1u = tsb("x1u", [P, 2, UB, D])
            gate_now = tsb("gate_now", [P, 2, UB, EXP])
            hidden = tsb("hidden", [P, 2, NF, BATCH])
            hid_ps = [three.enter_context(nc.psum_tensor(f"hid{k}", [P, BATCH], F32)) for k in range(NHID)]
            out_ps = [three.enter_context(nc.psum_tensor(f"experts{k}", [P, EXP, D], F32)) for k in range(NOUT)]

            s_in = sem("experts_loaded")
            s_b2 = sem("b2_parts_ready")
            s_b2m = sem("b2_parts_moved")
            s_sel = sem("ones_ready")
            s_past = sem("waits_passed")
            s_y2 = [sem(f"y_loaded{k}") for k in range(2)]
            s_x2 = [sem(f"x1_loaded{k}") for k in range(2)]
            s_hid = sem("hidden_multiplied")
            s_gelu = sem("hidden_activated")
            s_ex = sem("experts_multiplied")
            s_comb = sem("experts_combined")
            s_outst = [sem(f"out_stored{k}") for k in range(2)]
            s_dve = sem("vector_step")
            SETUP_LOADS = 4

            def wait_alone(eng, s, value):
                eng.wait_ge(s, value)
                if not isinstance(value, int):
                    eng.nop().then_inc(s_past, 1)

            block = three.enter_context(nc.Block())

            @block.sync
            def _(sp):
                sp.dma_start(w1_sb[:, :, :], W1.rearrange("e f c -> f e c")).then_inc(s_in, 16)
                sp.dma_start(w2_sb[:, :, :, :], W2.rearrange("e (k f) c -> f e k c", f=P)).then_inc(s_in, 16)
                with nc.allow_non_contiguous_dma(reason="1024 biases, once"):
                    sp.dma_start(b1_sb[:, :, :], b1.rearrange("e (k f) -> f e k", f=P)).then_inc(s_in, 16)
                sp.dma_start(b2_row[:, :], b2.rearrange("e f -> (e f)").unsqueeze(0)).then_inc(s_in, 16)

                def body(i, par):
                    if from_(i, 2):
                        wait_alone(sp, s_hid, (i - 1) * NF)
                    sp.dma_start(yTu[:, par, :], yT_dram[i] if isinstance(i, int) else
                                 yT_dram[bass.ds(i, 1)].rearrange("a p c -> p (a c)")).then_inc(s_y2[par], 16)
                    if from_(i, 2):
                        wait_alone(sp, s_outst[par], seen(i, par) * 16)
                    rows_i = x1_dram[i * BATCH:(i + 1) * BATCH, :] if isinstance(i, int) else \
                        x1_dram[bass.ds(i * BATCH, BATCH), :]
                    sp.dma_start(x1u[:, par, :, :], rows_i.rearrange("(t p) f -> p t f", p=P)).then_inc(s_x2[par], 16)
                    if isinstance(i, int) and i == 0:
                        sp.wait_ge(s_b2, 1)
                        for k in range(PARTS):
                            sp.dma_start(b2_parts[k:k + 1, :], b2_cut[0:1, k, :]).then_inc(s_b2m, 16)

                slots(sp, body)

            @block.gpsimd
            def _(pool):
                nc.gpsimd.memset(onesb[:, :], 1.0).then_inc(s_sel, 1)

            @block.tensor
            def _(pe):
                def layer1(i, par, f):
                    n = i * NF + f
                    if from_(n, NHID):
                        pe.wait_ge(s_gelu, n - NHID + 1)
                    e, k = divmod(f, HALVES)
                    nc.tensor.matmul(hid_ps[f % NHID][:, :], w1_sb[:, e, k * P:(k + 1) * P], yTu[:, par, :],
                                     start=True, stop=True).then_inc(s_hid, 1)

                def layer2(i, par, b):
                    if b == 0:
                        pe.wait_ge(s_gelu, i * NF)
                    n = (i - 1) * UB + b
                    if from_(n, NOUT):
                        pe.wait_ge(s_comb, n - NOUT + 1)
                    nc.tensor.matmul(out_ps[b % NOUT][:, :, :], onesb[:, :], b2_parts[:, :], start=True, stop=False,
                                     skip_group_check=True)
                    for e in range(EXP):
                        for k in range(HALVES):
                            mm = nc.tensor.matmul(out_ps[b % NOUT][:, e, :],
                                                  hidden[:, par, e * HALVES + k, b * P:(b + 1) * P],
                                                  w2_sb[:, e, k, :], start=False, stop=(k == HALVES - 1),
                                                  skip_group_check=True)
                    mm.then_inc(s_ex, 1)

                pe.wait_ge(s_in, 16 * SETUP_LOADS)

                def body(i, par):
                    pe.wait_ge(s_y2[par], seen(i, par) * 16 + 16)
                    for f in range(NF):
                        layer1(i, par, f)
                        if f % 2 == 1 and from_(i, 1):
                            if isinstance(i, int) and i == 1 and f == 1:
                                pe.wait_ge(s_b2m, 16 * PARTS)
                                pe.wait_ge(s_sel, 1)
                            layer2(i, 1 - par, f // 2)

                def tail(i, par):
                    for b in range(UB):
                        layer2(i, 1 - par, b)

                slots(pe, body, tail)

            @block.scalar
            def _(act):
                act.wait_ge(s_in, 16 * SETUP_LOADS)

                def gelu(i, par, f):
                    act.wait_ge(s_hid, i * NF + f + 1)
                    if f == 0 and from_(i, 2):
                        act.wait_ge(s_ex, (i - 1) * UB)
                    e, k = divmod(f, HALVES)
                    nc.scalar.activation(hidden[:, par, f, :], hid_ps[f % NHID][:, :], ACT.Gelu,
                                         bias=b1_sb[:, e, k:k + 1]).then_inc(s_gelu, 1)

                def store(i, par):
                    act.wait_ge(s_comb, i * UB)
                    last = isinstance(i, int) and i == NB
                    at = (i - 1) * BATCH
                    rows_n = LAST_ROWS if last else BATCH
                    whole, over = divmod(rows_n, P)
                    o = out[at:at + whole * P, :] if isinstance(at, int) else out[bass.ds(at, whole * P), :]
                    act.dma_start(o.rearrange("(t p) f -> p t f", p=P), x1u[:, par, 0:whole, :]).then_inc(s_outst[par], 16)
                    if over:
                        act.dma_start(out[at + whole * P:at + rows_n, :], x1u[0:over, par, whole, :]
                                      ).then_inc(s_outst[par], 16)

                def body(i, par):
                    for f in range(NF):
                        gelu(i, par, f)
                    if from_(i, 1):
                        store(i, 1 - par)

                def tail(i, par):
                    store(i, 1 - par)
                    act.wait_ge(s_outst[0], NB // 2 * 16)
                    act.wait_ge(s_outst[1], NB // 2 * 16 + 16)

                slots(act, body, tail)

            @block.vector
            def _(dve):
                v = nc.vector
                at = [0, 0]

                def link(ins):
                    at[1] += 1
                    ins.then_inc(s_dve, 1)
                    dve.wait_ge(s_dve, at[0] + at[1])

                dve.wait_ge(s_in, 16 * SETUP_LOADS)
                link(v.tensor_copy(b2_cut[:, 0, :], b2_row[:, :]))
                link(v.tensor_tensor(b2_res[:, :], b2_row[:, :], b2_cut[:, 0, :], ALU.subtract))
                link(v.tensor_copy(b2_cut[:, 1, :], b2_res[:, :]))
                link(v.tensor_tensor(b2_res[:, :], b2_res[:, :], b2_cut[:, 1, :], ALU.subtract))
                v.tensor_copy(b2_cut[:, 2, :], b2_res[:, :]).then_inc(s_b2, 1)
                SETUP_LINKS = at[1]
                UNIT_LINKS = UB * (EXP - 1) + 1

                def combine(i, par, b):
                    dve.wait_ge(s_ex, (i - 1) * UB + b + 1)
                    for e in range(EXP):
                        ins = v.scalar_tensor_tensor(out=x1u[:, par, b, :], in0=out_ps[b % NOUT][:, e, :],
                                                     scalar=gate_now[:, par, b, e:e + 1], in1=x1u[:, par, b, :],
                                                     op0=ALU.mult, op1=ALU.add)
                        if e < EXP - 1:
                            link(ins)
                        else:
                            ins.then_inc(s_comb, 1)

                def body(i, par):
                    if not from_(i, 1):
                        return
                    at[0], at[1] = SETUP_LINKS + (i - 1) * UNIT_LINKS, 0
                    at_b = (i - 1) * UB
                    g = gate[:, at_b:at_b + UB, :] if isinstance(i, int) else gate[:, bass.ds(at_b, UB), :]
                    link(v.tensor_copy(gate_now[:, 1 - par, :, :], g))
                    dve.wait_ge(s_x2[1 - par], seen(i - 1, 1 - par) * 16 + 16)
                    for b in range(UB):
                        combine(i, 1 - par, b)
                    assert at[1] == UNIT_LINKS

                slots(dve, body, body)

        ALL_COLS = EC
        FULL = N // P
        OVER = N - FULL * P
        HALF_FF = FF // P
        every = ExitStack()
        with every:
            def gsb(name, shape, dt=F32):
                return every.enter_context(nc.sbuf_tensor(name, shape, dt))

            def gps(name, shape):
                return every.enter_context(nc.psum_tensor(name, shape, F32))

            def sem(name):
                return every.enter_context(nc.semaphore(name))

            all_src = gsb("all_src", [P, EC], I32)
            all_dst = gsb("all_dst", [P, EC], I32)
            col_src = gsb("col_src", [P, 1], I32)
            col_dst = gsb("col_dst", [P, 1])
            table_lanes = gsb("table_lanes", [P, NBLK, ROW])
            node_id = gsb("node_id", [P, NBLK])
            edge_rows = gsb("edge_rows", [P, ROW])
            diag = gsb("diag", [P, HEADS + 1, P])
            as_all = gsb("as_all", [P, HEADS, P])
            dst_all = gsb("dst_all", [P, P])
            off = gsb("off", [P, P])
            z = gsb("z", [P, HEADS, P + 1])
            wz = gsb("wz", [P, HEADS, P + 1])
            wzT = gsb("wzT", [P, HEADS, P])
            run_max = gsb("run_max", [P, NBLK, HEADS])
            run_sum = gsb("run_sum", [P, NBLK, ND])
            new_max = gsb("new_max", [P, HEADS])
            part = gsb("part", [P, ND])
            gw1 = gsb("gw1", [P, EXP, FF])
            gw2 = gsb("gw2", [P, EXP, HALF_FF, D])
            gb1 = gsb("gb1", [P, EXP, HALF_FF])
            gb2 = gsb("gb2", [1, EXP * D])
            gbg, ggamma, gbeta = gsb("gbg", [P, HE]), gsb("ggamma", [P, HE]), gsb("gbeta", [P, HE])
            gy = gsb("gy", [P, P])
            gx1 = gsb("gx1", [P, D])
            ghid = gsb("ghid", [P, EXP * HALF_FF, P])
            gagg = gsb("gagg", [P, 1, HE])
            gsq = gsb("gsq", [P, 1, HE])
            gcol = gsb("gcol", [P, 6, 1])
            gscore, gcmp, gorder, gexps, ggate = (gsb(n, [P, 1, EXP]) for n in
                                                  ("gscore", "gcmp", "gorder", "gexps", "ggate"))
            wide_ps = gps("wide_ps", [P, HEADS, P])
            dst_ps = gps("dst_ps", [P, P])
            wzT_ps = gps("wzT_ps", [P, HEADS, P])
            num_ps = gps("num_ps", [P, HE])
            ghid_ps = [gps(f"ghid_ps{k}", [P, 4, P]) for k in range(2)]
            gout_ps = gps("gout_ps", [P, EXP, D])

            s_past = sem("waits_passed")
            s_gin = sem("general_loaded")
            s_gid = sem("node_ids_ready")
            s_gidx = sem("column_sources_ready")
            s_grow = sem("column_rows_gathered")
            s_gdiag = sem("diagonals_ready")
            s_gwide = sem("column_spread")
            s_gz = sem("column_logits_ready")
            s_gwz = sem("column_weights_ready")
            s_gwt = sem("column_weights_turned")
            s_gwc = sem("column_weights_copied")
            s_gnum = sem("column_summed")
            s_gcols = sem("columns_done")
            s_gfree = sem("block_buffers_free")
            s_gyx = sem("block_loaded")
            s_ghm = sem("block_hidden_multiplied")
            s_gha = sem("block_hidden_activated")
            s_gex = sem("block_experts_multiplied")
            s_gsq = sem("block_variance_ready")
            s_gsd = sem("block_deviation_ready")
            s_gge = sem("block_gate_logits_ready")
            s_ggd = sem("block_gate_exponentials_ready")
            s_gout = sem("block_stored")
            s_dve = sem("vector_step")
            G_LOADS = 3 + 4 + 3

            def wait_alone(eng, s, value):
                eng.wait_ge(s, value)
                eng.nop().then_inc(s_past, 1)

            def each_block(eng, body):
                with eng.Fori(0, FULL) as b:
                    body(b, P)
                body(FULL, OVER)

            def lanes_of(t, b, n):
                return t[b * P:b * P + n, :] if isinstance(b, int) else t[bass.ds(b * P, n), :]

            block = every.enter_context(nc.Block())

            @block.sync
            def _(sp):
                left = sp.value_load(left_count[0:1, 0:1], min_val=0, max_val=E)
                with sp.If(left > 0):
                    e_v = edge_index.rearrange("a (p c) -> a p c", p=P)
                    sp.dma_start(all_src[:, :], e_v[0]).then_inc(s_gin, 16)
                    sp.dma_start(all_dst[:, :], e_v[1]).then_inc(s_gin, 16)
                    sp.dma_start(table_lanes[:, :, :], table.rearrange("(b p) c -> p b c", p=P)).then_inc(s_gin, 16)
                    sp.dma_start(gw1[:, :, :], W1.rearrange("e f c -> f e c")).then_inc(s_gin, 16)
                    sp.dma_start(gw2[:, :, :, :], W2.rearrange("e (k f) c -> f e k c", f=P)).then_inc(s_gin, 16)
                    with nc.allow_non_contiguous_dma(reason="1024 biases, once"):
                        sp.dma_start(gb1[:, :, :], b1.rearrange("e (k f) -> f e k", f=P)).then_inc(s_gin, 16)
                    sp.dma_start(gb2[:, :], b2.rearrange("e f -> (e f)").unsqueeze(0)).then_inc(s_gin, 16)
                    for t, a in ((gbg, b_gat), (ggamma, ln_gamma), (gbeta, ln_beta)):
                        sp.dma_start(t[:, :], a.partition_broadcast(P)).then_inc(s_gin, 16)

                    def body(b, n):
                        sp.wait_ge(s_gfree, b + 1)
                        yb = yT_dram[b // 4] if isinstance(b, int) else yT_dram[bass.ds(b // 4, 1)].rearrange(
                            "a p c -> p (a c)")
                        at = (b % 4) * P
                        yb = yb[:, at:at + P] if isinstance(b, int) else yb[:, bass.ds(at, P)]
                        sp.dma_start(gy[:, :], yb).then_inc(s_gyx, 16)
                        sp.dma_start(gx1[0:n, :], lanes_of(x1_dram, b, n)).then_inc(s_gyx, 16)

                    each_block(sp, body)

            @block.gpsimd
            def _(pool):
                left = pool.value_load(left_count[0:1, 0:1], min_val=0, max_val=E)
                with pool.If(left > 0):
                    nc.gpsimd.iota(node_id[:, :], [[P, NBLK]], base=0, channel_multiplier=1,
                                   allow_small_or_imprecise_dtypes=True).then_inc(s_gid, 1)
                    with pool.Fori(0, ALL_COLS) as k:
                        wait_alone(pool, s_gidx, k + 1)
                        nc.gpsimd.indirect_dma_start(
                            edge_rows[:, :], None, table, bass.IndirectOffsetOnAxis(ap=col_src[:, 0:1], axis=0),
                            bounds_check=N - 1, oob_is_err=False).then_inc(s_grow, 16)

            @block.tensor
            def _(pe):
                left = pe.value_load(left_count[0:1, 0:1], min_val=0, max_val=E)
                with pe.If(left > 0):
                    with pe.Fori(0, ALL_COLS) as k:
                        pe.wait_ge(s_gdiag, k + 1)
                        nc.tensor.matmul(wide_ps[:, :, :], ones[:, :], diag[:, 0:HEADS, :], start=True, stop=True)
                        nc.tensor.matmul(dst_ps[:, :], ones[:, :], diag[:, HEADS, :], start=True, stop=True
                                         ).then_inc(s_gwide, 1)
                        with pe.Fori(0, NBLK) as b:
                            n = k * NBLK + b + 1
                            pe.wait_ge(s_gwz, n)
                            for h in range(HEADS):
                                mm = nc.tensor.transpose(wzT_ps[:, h, :], wz[:, h, 0:P], ident[:, :])
                            mm.then_inc(s_gwt, 1)
                            pe.wait_ge(s_gwc, n)
                            for h in range(HEADS):
                                mm = nc.tensor.matmul(num_ps[:, h * EXP:(h + 1) * EXP], wzT[:, h, :],
                                                      edge_rows[:, h * EXP:(h + 1) * EXP], start=(h == 0), stop=True,
                                                      skip_group_check=True)
                            mm.then_inc(s_gnum, 1)
                    pe.wait_ge(s_gin, 16 * G_LOADS)

                    def body(b, n):
                        pe.wait_ge(s_gyx, (b + 1) * 32)
                        for f in range(EXP * HALF_FF):
                            e, k = divmod(f, HALF_FF)
                            mm = nc.tensor.matmul(ghid_ps[f // 4][:, f % 4, :], gw1[:, e, k * P:(k + 1) * P], gy[:, :],
                                                  start=(f % 4 == 0), stop=True, skip_group_check=True)
                        mm.then_inc(s_ghm, 1)
                        pe.wait_ge(s_gha, b + 1)
                        nc.tensor.matmul(gout_ps[:, :, :], ones[0:1, :], gb2[:, :], start=True, stop=False,
                                         skip_group_check=True)
                        for e in range(EXP):
                            for k in range(HALF_FF):
                                mm = nc.tensor.matmul(gout_ps[:, e, :], ghid[:, e * HALF_FF + k, :], gw2[:, e, k, :],
                                                      start=False, stop=(k == HALF_FF - 1), skip_group_check=True)
                        mm.then_inc(s_gex, 1)

                    each_block(pe, body)

            @block.scalar
            def _(act):
                left = act.value_load(left_count[0:1, 0:1], min_val=0, max_val=E)
                with act.If(left > 0):
                    with act.Fori(0, ALL_COLS) as k:
                        with act.Fori(0, NBLK) as b:
                            n = k * NBLK + b + 1
                            act.wait_ge(s_gz, n)
                            nc.scalar.activation(wz[:, :, :], z[:, :, :], ACT.Exp).then_inc(s_gwz, 1)
                            act.wait_ge(s_gwt, n)
                            nc.scalar.activation(wzT[:, :, :], wzT_ps[:, :, :], ACT.Copy).then_inc(s_gwc, 1)
                    act.wait_ge(s_gin, 16 * G_LOADS)

                    def body(b, n):
                        act.wait_ge(s_ghm, b + 1)
                        for f in range(EXP * HALF_FF):
                            e, k = divmod(f, HALF_FF)
                            ins = nc.scalar.activation(ghid[:, f, :], ghid_ps[f // 4][:, f % 4, :], ACT.Gelu,
                                                       bias=gb1[:, e, k:k + 1])
                        ins.then_inc(s_gha, 1)
                        act.wait_ge(s_gsq, b + 1)
                        nc.scalar.activation(gcol[:, 3, :], gcol[:, 2, :], ACT.Sqrt).then_inc(s_gsd, 1)
                        act.wait_ge(s_gge, b + 1)
                        nc.scalar.activation(gexps[:, :, :], gcmp[:, :, :], ACT.Exp).then_inc(s_ggd, 1)
                        act.wait_ge(s_gcols, b + 1)
                        act.dma_start(lanes_of(out, b, n), gx1[0:n, :]).then_inc(s_gout, 16)

                    each_block(act, body)
                    act.wait_ge(s_gout, (FULL + 1) * 16)

            @block.vector
            def _(dve):
                v = nc.vector
                at = [0, 0]

                def link(ins):
                    at[1] += 1
                    ins.then_inc(s_dve, 1)
                    dve.wait_ge(s_dve, at[0] + at[1])

                left = dve.value_load(left_count[0:1, 0:1], min_val=0, max_val=E)
                with dve.If(left > 0):
                    dve.wait_ge(s_gin, 16 * G_LOADS)
                    dve.wait_ge(s_gid, 1)
                    link(v.tensor_scalar(all_src[:, :], all_src[:, :], float(N - 1), None, ALU.min))
                    a_src, a_dst = table_lanes[:, :, HE:HE + HEADS], table_lanes[:, :, HE + HEADS:ROW]
                    link(v.tensor_tensor(run_max[:, :, :], a_src, a_dst, ALU.add))
                    link(v.scalar_tensor_tensor(out=run_max[:, :, :], in0=run_max[:, :, :], scalar=0.2,
                                                in1=run_max[:, :, :], op0=ALU.mult, op1=ALU.max))
                    link(v.tensor_copy(run_sum[:, :, 0:HE], table_lanes[:, :, 0:HE]))
                    link(v.memset(run_sum[:, :, HE:ND], 1.0))
                    SETUP = at[1]
                    COL_LINKS, BLK_LINKS = 4, 11
                    with dve.Fori(0, ALL_COLS) as k:
                        at[0], at[1] = k * (COL_LINKS + NBLK * BLK_LINKS) + SETUP, 0
                        v.tensor_copy(col_src[:, :], all_src[:, bass.ds(k, 1)]).then_inc(s_gidx, 1)
                        link(v.tensor_copy(col_dst[:, :], all_dst[:, bass.ds(k, 1)]))
                        dve.wait_ge(s_grow, (k + 1) * 16)
                        for h in range(HEADS):
                            v.tensor_scalar(diag[:, h, :], ident[:, :], edge_rows[:, HE + h:HE + h + 1], None, ALU.mult)
                        link(v.tensor_scalar(diag[:, HEADS, :], ident[:, :], col_dst[:, 0:1], None, ALU.mult))
                        v.nop().then_inc(s_gdiag, 1)
                        dve.wait_ge(s_gwide, k + 1)
                        link(v.tensor_copy(as_all[:, :, :], wide_ps[:, :, :]))
                        link(v.tensor_copy(dst_all[:, :], dst_ps[:, :]))
                        v.nop().then_inc(s_past, 1)
                        assert at[1] == COL_LINKS
                        with dve.Fori(0, NBLK) as b:
                            at[0], at[1] = k * (COL_LINKS + NBLK * BLK_LINKS) + b * BLK_LINKS + (SETUP + COL_LINKS), 0
                            n = k * NBLK + b + 1
                            mine, ad = run_max[:, bass.ds(b, 1), :], table_lanes[:, bass.ds(b, 1), HE + HEADS:ROW]
                            zz = z[:, :, 0:P]
                            link(v.tensor_scalar(off[:, :], dst_all[:, :], node_id[:, bass.ds(b, 1)], -BIG,
                                                 ALU.not_equal, ALU.mult))
                            link(v.tensor_tensor(zz, as_all[:, :, :], ad.rearrange("p a h -> p (a h)").unsqueeze(2)
                                                 .broadcast_to([P, HEADS, P]), ALU.add))
                            link(v.scalar_tensor_tensor(out=zz, in0=zz, scalar=0.2, in1=zz, op0=ALU.mult, op1=ALU.max))
                            link(v.tensor_tensor(zz, zz, off[:, :].unsqueeze(1).broadcast_to([P, HEADS, P]), ALU.add))
                            link(v.tensor_reduce(new_max[:, :], zz, AX_X, ALU.max))
                            mine = mine.rearrange("p a h -> p (a h)")
                            link(v.tensor_tensor(new_max[:, :], new_max[:, :], mine, ALU.max))
                            v.tensor_tensor(z[:, :, P], mine, new_max[:, :], ALU.subtract)
                            v.tensor_tensor(zz, zz, new_max[:, :].unsqueeze(2).broadcast_to([P, HEADS, P]),
                                            ALU.subtract).then_inc(s_gz, 1)
                            wait_alone(dve, s_gz, n)
                            link(v.tensor_copy(mine, new_max[:, :]))
                            dve.wait_ge(s_gwz, n)
                            link(v.tensor_reduce(part[:, HE:ND], wz[:, :, 0:P], AX_X, ALU.add))
                            dve.wait_ge(s_gnum, n)
                            link(v.tensor_copy(part[:, 0:HE], num_ps[:, :]))
                            mysum = run_sum[:, bass.ds(b, 1), :].rearrange("p a c -> p (a c)")
                            num, den = mysum[:, 0:HE].rearrange("p (h k) -> p h k", h=HEADS), mysum[:, HE:ND]
                            v.tensor_tensor(num, num, wz[:, :, P:P + 1].broadcast_to([P, HEADS, EXP]), ALU.mult)
                            link(v.tensor_tensor(den, den, wz[:, :, P], ALU.mult))
                            link(v.tensor_tensor(mysum, mysum, part[:, :], ALU.add))
                            GOT = at[1]
                    assert GOT == BLK_LINKS, GOT
                    AFTER = ALL_COLS * (COL_LINKS + NBLK * BLK_LINKS) + SETUP
                    TAIL = [0]
                    v.memset(gx1[:, :], 0.0).then_inc(s_gfree, 1)

                    def body(b, n):
                        at[0], at[1] = b * TAIL[0] + AFTER, 0
                        sums = run_sum[:, b:b + 1, :] if isinstance(b, int) else run_sum[:, bass.ds(b, 1), :]
                        link(v.tensor_scalar(gexps[:, :, :], sums[:, :, HE:ND], 1e-16, None, ALU.add))
                        link(v.reciprocal(gexps[:, :, :], gexps[:, :, :]))
                        h4 = "p b (h k) -> p b h k"
                        link(v.tensor_tensor(gagg[:, :, :].rearrange(h4, h=HEADS), sums[:, :, 0:HE].rearrange(h4, h=HEADS),
                                             gexps[:, :, :].unsqueeze(3).broadcast_to([P, 1, HEADS, EXP]), ALU.mult))
                        center(v, link, gagg[:, :, :], gbg, gsq, gcol, 1).then_inc(s_gsq, 1)
                        dve.wait_ge(s_gsd, b + 1)
                        rank_scores(v, link, gagg[:, :, :], ggamma, gbeta, gcol, gscore, gorder, gcmp, 1
                                    ).then_inc(s_gge, 1)
                        dve.wait_ge(s_ggd, b + 1)
                        link(share_gates(v, link, gorder, gexps, gcol, ggate[:, :, :], 1))
                        dve.wait_ge(s_gyx, (b + 1) * 32)
                        dve.wait_ge(s_gex, b + 1)
                        for e in range(EXP):
                            ins = v.scalar_tensor_tensor(out=gx1[:, :], in0=gout_ps[:, e, :], scalar=ggate[:, 0, e:e + 1],
                                                         in1=gx1[:, :], op0=ALU.mult, op1=ALU.add)
                            if e < EXP - 1:
                                link(ins)
                            else:
                                ins.then_inc(s_gcols, 1)
                        dve.wait_ge(s_gout, (b + 1) * 16)
                        v.nop().then_inc(s_gfree, 1)

                    TAIL[0] = G_TAIL_LINKS
                    each_block(dve, body)
                    assert at[1] == G_TAIL_LINKS, at[1]


_INS = ["x", "adj", "L0_gnn_item_feat", "L0_gnn_W_item", "L0_gnn_b_item", "L0_gnn_W_user", "L0_gnn_b_user",
        "L0_ffn_W_gat", "L0_ffn_att_src", "L0_ffn_att_dst", "L0_ffn_b_gat", "L0_ffn_ln_gamma", "L0_ffn_ln_beta",
        "L0_ffn_W1", "L0_ffn_b1", "L0_ffn_W2", "L0_ffn_b2", "L0_ffn_edge_index"]


def kernel(**inputs):
    import numpy as _np
    import concourse.bacc as _bacc
    from concourse import mybir as _mybir
    from concourse.bass_utils import run_bass_kernel_spmd as _run

    nc = _bacc.Bacc("TRN2", target_bir_lowering=False, num_devices=1)
    arrays, args = {}, []
    for name in _INS:
        a = _np.ascontiguousarray(inputs[name])
        arrays[f"in_{name}_dram"] = a
        args.append(nc.dram_tensor(f"in_{name}_dram", a.shape, _mybir.dt.from_np(a.dtype), kind="ExternalInput").ap())
    out = nc.dram_tensor("out_0_dram", (10000, 128), _mybir.dt.from_np(_np.dtype("float32")), kind="ExternalOutput").ap()
    adj_ffn_kernel(nc, *args, out)
    r = _run(nc, [arrays], core_ids=[0])
    return r.results[0]["out_0_dram"]
```

```python
from contextlib import ExitStack

import concourse.bass as bass
from concourse import mybir

ALU = mybir.AluOpType
ACT = mybir.ActivationFunctionType
F32 = mybir.dt.float32
BF16 = mybir.dt.bfloat16
I32 = mybir.dt.int32
AX_X = mybir.AxisListType.X

P = 128
SRC_BITS = 14
LO_BITS = 7
BIG = float(2.0 ** 100)
LN_EPS = 1e-5
G_TAIL_LINKS = 36


def compact_stages(length):
    return [1 << b for b in range((length - 1).bit_length())]


def center(v, link, agg, bias, squares, col, blocks):
    _, _, width = agg.shape
    link(v.tensor_tensor(agg, agg, bias[:, :].unsqueeze(1).broadcast_to([P, blocks, width]), ALU.add))
    link(v.tensor_reduce(col[:, 0, :], agg, AX_X, ALU.add))
    link(v.tensor_scalar(col[:, 0, :], col[:, 0, :], 1.0 / width, None, ALU.mult))
    link(v.tensor_tensor(agg, agg, col[:, 0, :].unsqueeze(2).broadcast_to([P, blocks, width]), ALU.subtract))
    link(v.tensor_tensor(squares[:, :, :], agg, agg, ALU.mult))
    link(v.tensor_reduce(col[:, 1, :], squares[:, :, :], AX_X, ALU.add))
    return v.tensor_scalar(col[:, 2, :], col[:, 1, :], 1.0 / width, LN_EPS, ALU.mult, ALU.add)


def rank_scores(v, link, agg, gamma, beta, col, score, order, cmpb, blocks):
    width, exp = agg.shape[2], score.shape[2]
    heads = width // exp

    def wide(t):
        return t[:, :].unsqueeze(1).broadcast_to([P, blocks, width])

    link(v.reciprocal(col[:, 4, :], col[:, 3, :]))
    link(v.tensor_tensor(agg, agg, col[:, 4, :].unsqueeze(2).broadcast_to([P, blocks, width]), ALU.mult))
    link(v.tensor_tensor(agg, agg, wide(gamma), ALU.mult))
    link(v.tensor_tensor(agg, agg, wide(beta), ALU.add))
    link(v.tensor_reduce(score[:, :, :], agg.rearrange("p b (h k) -> p b k h", h=heads), AX_X, ALU.add))
    link(v.tensor_scalar(score[:, :, :], score[:, :, :], 1.0 / heads, None, ALU.mult))
    link(v.memset(order[:, :, :], 0.0))
    for j in range(exp):
        sj = score[:, :, j:j + 1]
        if j + 1 < exp:
            n = exp - 1 - j
            link(v.tensor_tensor(cmpb[:, :, 0:n], sj.broadcast_to([P, blocks, n]), score[:, :, j + 1:exp], ALU.is_ge))
            link(v.tensor_tensor(order[:, :, j + 1:exp], order[:, :, j + 1:exp], cmpb[:, :, 0:n], ALU.add))
        if j > 0:
            link(v.tensor_tensor(cmpb[:, :, 0:j], sj.broadcast_to([P, blocks, j]), score[:, :, 0:j], ALU.is_gt))
            link(v.tensor_tensor(order[:, :, 0:j], order[:, :, 0:j], cmpb[:, :, 0:j], ALU.add))
    link(v.tensor_reduce(col[:, 0, :], score[:, :, :], AX_X, ALU.max))
    return v.tensor_tensor(cmpb[:, :, :], score[:, :, :],
                           col[:, 0, :].unsqueeze(2).broadcast_to([P, blocks, exp]), ALU.subtract)


def share_gates(v, link, order, gexp, col, gate, blocks):
    exp = order.shape[2]
    link(v.scalar_tensor_tensor(out=gexp[:, :, :], in0=order[:, :, :], scalar=1.5, in1=gexp[:, :, :],
                                op0=ALU.is_lt, op1=ALU.mult))
    link(v.tensor_reduce(col[:, 1, :], gexp[:, :, :], AX_X, ALU.add))
    link(v.reciprocal(col[:, 5, :], col[:, 1, :]))
    return v.tensor_tensor(gate, gexp[:, :, :], col[:, 5, :].unsqueeze(2).broadcast_to([P, blocks, exp]), ALU.mult)


def adj_ffn_kernel(nc, x, adj, item_feat, W_item, b_item, W_user, b_user, W_gat, att_src, att_dst, b_gat,
                   ln_gamma, ln_beta, W1, b1, W2, b2, edge_index, out):
    N, D = x.shape
    NI = item_feat.shape[0]
    E = edge_index.shape[1]
    HEADS, EXP = att_src.shape
    HE = HEADS * EXP
    FF = W1.shape[2]
    ROW = HE + 2 * HEADS

    BATCH = 512
    NB = -(-N // BATCH)
    GR = BATCH // 32
    LAST_ROWS = N - (NB - 1) * BATCH
    KT = NI // P
    QW = KT * 32
    RES = NI - KT * P
    CHUNKS = [5] * 6 + [4] * 12
    assert sum(CHUNKS) == KT
    COFF = [sum(CHUNKS[:c]) for c in range(len(CHUNKS))]
    NCH = len(CHUNKS)
    CW = max(CHUNKS) * 32
    NRAW = 3
    NT = 2
    assert NCH % NRAW == 0 and NCH % NT == 0

    EC = E // P
    HC = EC // 2
    VH = 736
    VC = 2 * VH
    UC = 480
    NBLK = NB * BATCH // P
    TPB = 6
    CAP = TPB * P
    HG = 8
    OUT_OF_LIST = 131072
    EMPTY = 200 << SRC_BITS
    HIST_FROM = 13
    HIST_N = 26
    HIST_LAST = VC // HG - (NB - 1 - HIST_FROM) * HIST_N
    BASE_AFTER = 8
    assert VC % (2 * HG) == 0 and HIST_N % 2 == 0 and HIST_LAST > 0

    lists = nc.dram_tensor("edge_lists", [NBLK * CAP, 1], I32).ap()
    lanes_dram = nc.dram_tensor("edge_lanes", [NBLK, CAP], BF16).ap()

    with ExitStack() as ctx:
        def sb(name, shape, dt=F32):
            return ctx.enter_context(nc.sbuf_tensor(name, shape, dt))

        def pb(name, shape, dt=F32):
            return ctx.enter_context(nc.psum_tensor(name, shape, dt))

        ident = sb("ident", [P, P])
        identb = sb("identb", [P, P], BF16)
        ones = sb("ones", [P, P])
        iota_lane = sb("iota_lane", [P, P, 24], BF16)
        lane_col = sb("lane_col", [P, 1])
        iota_blk = sb("iota_blk", [P, NBLK])
        clamp_count = sb("clamp_count", [P, NBLK])
        left_count = sb("left_count", [P, 1], I32)

        slot = sb("slot", [P, UC], I32)
        pay = sb("pay", [P, UC], I32)
        w_userT = sb("w_userT", [P, P])
        w_rows = sb("w_rows", [P, ROW])
        bias_user = sb("bias_user", [P, 1])
        h_items = sb("h_items", [P, KT, D])
        h_rest = sb("h_rest", [RES, D])

        source = sb("source", [P, NBLK * TPB], I32)
        prep = ctx.enter_context(ExitStack())

        def psb(name, shape, dt=F32):
            return prep.enter_context(nc.sbuf_tensor(name, shape, dt))

        def psem(name):
            return prep.enter_context(nc.semaphore(name))

        edge_x = psb("edge_x", [P, HC], I32)
        edge_y = psb("edge_y", [P, HC], I32)
        bufA = psb("bufA", [P, HC], I32)
        bufB = psb("bufB", [P, HC], I32)
        bufC = psb("bufC", [P, HC], I32)
        valid = psb("valid", [P, VC], I32)
        codeB = psb("codeB", [P, VC], I32)
        iota_col = psb("iota_col", [P, VH])
        iota_tail = psb("iota_tail", [P, NBLK, HG], BF16)
        tri = psb("tri", [P, P])
        hot_lane = psb("hot_lane", [P, 2, P, HG], BF16)
        hot_blk = psb("hot_blk", [P, 2, NBLK, HG], BF16)
        lane_bf = psb("lane_bf", [P, VC], BF16)
        blk_bf = psb("blk_bf", [P, VC], BF16)
        nval = psb("nval", [P, 5])
        tot = psb("tot", [P, NBLK])
        base = psb("base", [P, NBLK])
        hist_ps = prep.enter_context(nc.psum_tensor("hist_ps", [P, NBLK], F32))
        base_ps = prep.enter_context(nc.psum_tensor("base_ps", [P, NBLK], F32))

        s_ld = psem("edges_loaded")
        s_free = psem("edge_buffers_free")
        s_ldy = psem("second_destinations_loaded")
        s_ldx = psem("second_sources_loaded")
        s_const = psem("constants_ready")
        s_prep = psem("prep_step")
        s_hot = psem("onehots_ready")
        s_hist = psem("onehots_used")
        s_z = psem("histogram_cleared")
        s_tot = psem("totals_ready")
        s_base = psem("bases_ready")
        s_left = psem("leftover_ready")
        s_leftp = psem("leftover_summed")
        s_slot = psem("slots_ready")
        e_halves = edge_index.rearrange("a (p h c) -> a h p c", p=P, h=2)

        def prep_steps(dve, v):
            n = [0]

            def step(ins, width=0):
                n[0] += 1
                ins.then_inc(s_prep, 1)
                yield 0.1 + width / 960.0
                dve.wait_ge(s_prep, n[0])

            def compact(key, shift, length, spare, marks):
                for bit in compact_stages(length):
                    m = length - bit
                    yield from step(v.tensor_scalar(marks, shift, bit, None, ALU.bitwise_and), length / 2)
                    yield from step(v.scalar_tensor_tensor(out=spare, in0=marks, scalar=0.0, in1=shift,
                                                           op0=ALU.is_equal, op1=ALU.mult), length)
                    yield from step(v.copy_predicated(spare[:, 0:m], marks[:, bit:length], shift[:, bit:length]), m)
                    yield from step(v.copy_predicated(key[:, 0:m], marks[:, bit:length], key[:, bit:length]), m)
                    spare, shift = shift, spare

            invalid, holes = bufA[:, :].bitcast(F32), bufB[:, :].bitcast(F32)
            for h, (code, src) in enumerate(((edge_x, edge_y), (edge_y, edge_x))):
                if h == 0:
                    dve.wait_ge(s_ld, 32)
                else:
                    dve.wait_ge(s_ldy, 16)
                yield from step(v.tensor_scalar(invalid, code[:, :], float(N), None, ALU.is_ge), HC / 2)
                yield from step(v.tensor_tensor_scan(holes, invalid, invalid, 0.0, ALU.add, ALU.max), HC)
                yield from step(v.scalar_tensor_tensor(out=bufC[:, :], in0=invalid, scalar=0.0, in1=holes,
                                                       op0=ALU.is_equal, op1=ALU.mult), HC)
                yield from step(v.tensor_scalar(nval[:, h:h + 1], holes[:, HC - 1:HC], -1.0, float(HC),
                                                ALU.mult, ALU.add))
                yield from step(v.tensor_scalar(code[:, :], code[:, :], SRC_BITS, None, ALU.logical_shift_left), HC / 2)
                if h == 1:
                    dve.wait_ge(s_ldx, 16)
                yield from step(v.tensor_scalar(src[:, :], src[:, :], float(N - 1), None, ALU.min), HC / 2)
                yield from step(v.tensor_tensor(code[:, :], code[:, :], src[:, :], ALU.bitwise_or), HC)
                if h == 0:
                    v.nop().then_inc(s_free, 1)
                yield from compact(code[:, :], bufC[:, :], HC, bufB[:, :], bufA[:, :])
                yield from step(v.tensor_copy(valid[:, h * VH:(h + 1) * VH], code[:, 0:VH]), VH / 2)
                if h == 0:
                    v.nop().then_inc(s_free, 1)

            dve.wait_ge(s_const, 1)
            dst_i, work, live_i, clamped_i, loose_i = (t[:, 0:VC] for t in (bufA, bufB, bufC, edge_x, edge_y))
            live, clamped, loose = live_i.bitcast(F32), clamped_i.bitcast(F32), loose_i.bitcast(F32)
            for h in range(2):
                yield from step(v.tensor_scalar(live[:, h * VH:(h + 1) * VH], iota_col[:, :], nval[:, h:h + 1], None,
                                                ALU.is_lt), VH / 2)
            yield from step(v.tensor_scalar(work, valid[:, :], (1 << SRC_BITS) - 1, None, ALU.bitwise_and), VC / 2)
            yield from step(v.scalar_tensor_tensor(out=clamped, in0=work, scalar=float(N - 1), in1=live,
                                                   op0=ALU.is_ge, op1=ALU.mult), VC)
            yield from step(v.scalar_tensor_tensor(out=loose, in0=work, scalar=float(N - 1), in1=live,
                                                   op0=ALU.is_lt, op1=ALU.mult), VC)
            yield from step(v.tensor_scalar(dst_i, valid[:, :], SRC_BITS, None, ALU.logical_shift_right), VC / 2)
            yield from step(v.tensor_scalar(dst_i, dst_i, float(N), None, ALU.min), VC / 2)
            yield from step(v.tensor_scalar(work, dst_i, P - 1, None, ALU.bitwise_and), VC / 2)
            yield from step(v.tensor_copy(lane_bf[:, :], work), VC / 2)
            yield from step(v.tensor_scalar(work, dst_i, LO_BITS, None, ALU.logical_shift_right), VC / 2)
            yield from step(v.scalar_tensor_tensor(out=blk_bf[:, :], in0=clamped, scalar=float(P), in1=work,
                                                   op0=ALU.mult, op1=ALU.add), VC)
            yield from step(v.memset(hot_lane[:, 0, :, 0], 0.0))
            yield from step(v.memset(hot_blk[:, 0, :, 0], 0.0))
            v.nop().then_inc(s_z, 1)

            fixed, holes2, shift2, marks2 = dst_i.bitcast(F32), work.bitcast(F32), live_i, clamped_i
            yield from step(v.tensor_scalar(fixed, loose, 0.0, None, ALU.is_equal), VC / 2)
            yield from step(v.tensor_tensor_scan(holes2, fixed, fixed, 0.0, ALU.add, ALU.max), VC)
            yield from step(v.tensor_tensor(shift2, loose, holes2, ALU.mult), VC)
            yield from step(v.tensor_scalar(nval[:, 2:3], holes2[:, VC - 1:VC], -1.0, float(VC), ALU.mult, ALU.add))
            yield from step(v.tensor_copy(codeB[:, :], valid[:, :]), VC / 2)
            yield from compact(codeB[:, :], shift2, VC, dst_i, marks2)

            c = [b[:, k * UC:(k + 1) * UC] for b in (bufA, bufB) for k in range(HC // UC)]
            blk_of, live2, same, count = (c[k].bitcast(F32) for k in range(4))
            rank, keep = c[4].bitcast(F32), c[5].bitcast(F32)
            short = codeB[:, 0:UC]
            yield from step(v.tensor_scalar(pay[:, :], short, (1 << (SRC_BITS + LO_BITS)) - 1, None,
                                            ALU.bitwise_and), UC / 2)
            yield from step(v.tensor_scalar(c[6], short, SRC_BITS + LO_BITS, None, ALU.logical_shift_right), UC / 2)
            yield from step(v.tensor_scalar(c[6], c[6], float(NBLK - 1), None, ALU.min), UC / 2)
            yield from step(v.tensor_scalar(live2, iota_col[:, 0:UC], nval[:, 2:3], None, ALU.is_lt), UC / 2)
            yield from step(v.scalar_tensor_tensor(out=blk_of, in0=live2, scalar=float(P), in1=c[6],
                                                   op0=ALU.mult, op1=ALU.add), UC)
            yield from step(v.memset(rank, 0.0), UC / 2)
            for b in range(NBLK):
                yield from step(v.tensor_scalar(same, blk_of, iota_blk[:, b:b + 1], None, ALU.is_equal, ALU.add,
                                                accum_out=tot[:, b:b + 1]), UC / 2)
            v.nop().then_inc(s_tot, 1)
            yield "bases"
            dve.wait_ge(s_base, 1)
            yield from step(v.tensor_copy(base[:, :], base_ps[:, :]))
            for b in range(NBLK):
                yield from step(v.tensor_scalar(same, blk_of, iota_blk[:, b:b + 1], None, ALU.is_equal), UC / 2)
                yield from step(v.tensor_tensor_scan(count, same, same, base[:, b:b + 1], ALU.add, ALU.max), UC)
                yield from step(v.copy_predicated(rank, same.bitcast(I32), count), UC)
            yield from step(v.scalar_tensor_tensor(out=keep, in0=rank, scalar=float(CAP), in1=live2,
                                                   op0=ALU.is_le, op1=ALU.mult), UC)
            yield from step(v.tensor_tensor_scan(count, live2, keep, 0.0, ALU.add, ALU.subtract), UC)
            yield from step(v.scalar_tensor_tensor(out=same, in0=blk_of, scalar=float(CAP), in1=rank,
                                                   op0=ALU.mult, op1=ALU.add), UC)
            yield from step(v.tensor_scalar(same, same, float(-(P * CAP + 1 + OUT_OF_LIST)), None, ALU.add), UC / 2)
            yield from step(v.tensor_tensor(same, same, keep, ALU.mult), UC)
            yield from step(v.tensor_scalar(slot[:, :], same, float(OUT_OF_LIST), None, ALU.add), UC / 2)
            v.nop().then_inc(s_slot, 1)
            yield from step(v.tensor_scalar(nval[:, 0:2], nval[:, 0:2], float(-VH), 0.0, ALU.add, ALU.max))
            yield from step(v.tensor_scalar(nval[:, 2:3], nval[:, 2:3], float(-UC), 0.0, ALU.add, ALU.max))
            yield from step(v.tensor_reduce(nval[:, 3:4], nval[:, 0:3], AX_X, ALU.add))
            yield from step(v.tensor_tensor(nval[:, 4:5], nval[:, 3:4], count[:, UC - 1:UC], ALU.add))
            v.nop().then_inc(s_left, 1)

        def run_prep(steps, budget):
            spent = 0.0
            while spent < budget:
                cost = next(steps, None)
                if cost is None or cost == "bases":
                    return False
                spent += cost
            return True

        prep_chain = prep_steps(nc.vector, nc.vector)

        setup = ExitStack()
        with setup:
            def ssb(name, shape, dt=F32):
                return setup.enter_context(nc.sbuf_tensor(name, shape, dt))

            def sem(name):
                return setup.enter_context(nc.semaphore(name))

            items = ssb("items", [P, KT, D])
            items_rest = ssb("items_rest", [RES, D])
            items_t = ssb("items_t", [P, 2, 4, P])
            w_in = ssb("w_in", [P, 2, D])
            w_itemT = ssb("w_itemT", [P, P])
            bias_item = ssb("bias_item", [P, D])
            att = ssb("att", [P, 2, HE])
            att_w = ssb("att_w", [P, 2, HE])
            tr_ps = [setup.enter_context(nc.psum_tensor(f"items_tr{k}", [P, 4, P], F32)) for k in range(2)]
            h_ps = [setup.enter_context(nc.psum_tensor(f"items_h{k}", [P, 4, P], F32)) for k in range(2)]
            empties = ssb("empties", [P, NBLK * TPB], I32)

            s_pool = sem("pool_step")
            s_dve = sem("vector_step")
            s_empty = sem("lists_emptied")
            s_w = sem("weights_loaded")
            s_items = sem("items_loaded")
            s_wt = sem("weights_transposed")
            s_wtc = sem("weights_copied")
            s_itr = sem("items_transposed")
            s_itc = sem("items_copied")
            s_hmm = sem("items_projected")
            s_hc = sem("h_copied")
            W_LOADS = 2 + 1 + 1 + 1 + 2
            QUADS = [list(range(q, min(q + 4, KT))) for q in range(0, KT, 4)] + ["rest"]

            block = setup.enter_context(nc.Block())

            @block.sync
            def _(sp):
                sp.dma_start(edge_x[:, :], e_halves[1, 0]).then_inc(s_ld, 16)
                sp.dma_start(edge_y[:, :], e_halves[0, 0]).then_inc(s_ld, 16)
                sp.dma_start(w_in[:, 0, :], W_item).then_inc(s_w, 16)
                sp.dma_start(w_in[:, 1, :], W_user).then_inc(s_w, 16)
                sp.dma_start(bias_item[:, :], b_item.partition_broadcast(P)).then_inc(s_w, 16)
                sp.dma_start(bias_user[:, :], b_user.unsqueeze(1)).then_inc(s_w, 16)
                sp.dma_start(w_rows[:, 0:HE], W_gat).then_inc(s_w, 16)
                for k, a in enumerate((att_src, att_dst)):
                    sp.dma_start(att[:, k, :], a.rearrange("h k -> (h k)").partition_broadcast(P)).then_inc(s_w, 16)
                for q in range(4):
                    sp.dma_start(items[32 * q:32 * q + 32, :, :],
                                 item_feat[QW * q:QW * (q + 1), :].rearrange("(b c) f -> c b f", c=32)
                                 ).then_inc(s_items, 16)
                sp.dma_start(items_rest[:, :], item_feat[KT * P:NI, :]).then_inc(s_items, 16)
                sp.wait_ge(s_const, 1)
                sp.dma_start(lists.rearrange("(p c) a -> p (c a)", p=P), empties[:, :]).then_inc(s_empty, 16)
                sp.wait_ge(s_empty, 16)

            @block.gpsimd
            def _(pool):
                nc.gpsimd.iota(empties[:, :], [[0, NBLK * TPB]], base=EMPTY, channel_multiplier=0).then_inc(s_pool, 1)
                nc.gpsimd.iota(iota_col[:, :], [[1, VH]], base=0, channel_multiplier=0,
                               allow_small_or_imprecise_dtypes=True).then_inc(s_pool, 1)
                nc.gpsimd.iota(iota_blk[:, :], [[1, NBLK]], base=P, channel_multiplier=0,
                               allow_small_or_imprecise_dtypes=True).then_inc(s_pool, 1)
                nc.gpsimd.iota(iota_tail[:, :, :], [[1, NBLK], [0, HG]], base=P, channel_multiplier=0,
                               allow_small_or_imprecise_dtypes=True).then_inc(s_pool, 1)
                nc.gpsimd.iota(iota_lane[:, :, :], [[1, P], [0, 24]], base=0, channel_multiplier=0,
                               allow_small_or_imprecise_dtypes=True).then_inc(s_pool, 1)
                nc.gpsimd.iota(lane_col[:, :], [[0, 1]], base=0, channel_multiplier=1,
                               allow_small_or_imprecise_dtypes=True).then_inc(s_pool, 1)
                nc.gpsimd.memset(ones[:, :], 1.0).then_inc(s_pool, 1)
                nc.gpsimd.memset(ident[:, :], 0.0).then_inc(s_pool, 1)
                nc.gpsimd.memset(identb[:, :], 0.0).then_inc(s_pool, 1)
                pool.wait_ge(s_pool, 9)
                for m, v in ((ident, 1.0), (identb, 1.0)):
                    nc.gpsimd.affine_select(out=m[:, :], in_=m[:, :], compare_op=ALU.not_equal, fill=v, base=0,
                                            pattern=[[-1, P]], channel_multiplier=1).then_inc(s_pool, 1)
                nc.gpsimd.affine_select(out=tri[:, :], in_=ones[:, :], compare_op=ALU.is_gt, fill=0.0, base=0,
                                        pattern=[[1, P]], channel_multiplier=-1).then_inc(s_pool, 1)
                pool.wait_ge(s_pool, 12)
                pool.nop().then_inc(s_const, 1)
                pool.wait_ge(s_free, 1)
                pool.dma_start(edge_y[:, :], e_halves[1, 1]).then_inc(s_ldy, 16)
                pool.wait_ge(s_w, 16 * W_LOADS)
                for n, quad in enumerate(QUADS):
                    pool.wait_ge(s_hc, n + 1)
                    if quad == "rest":
                        nc.gpsimd.tensor_tensor(h_rest[:, :], h_rest[:, :], bias_item[0:RES, :], ALU.add)
                    else:
                        w = len(quad)
                        nc.gpsimd.tensor_tensor(h_items[:, quad[0]:quad[0] + w, :], h_items[:, quad[0]:quad[0] + w, :],
                                                bias_item[:, :].unsqueeze(1).broadcast_to([P, w, D]), ALU.add)

            @block.tensor
            def _(pe):
                pe.wait_ge(s_const, 1)
                pe.wait_ge(s_w, 16 * W_LOADS)
                for k in range(2):
                    nc.tensor.transpose(h_ps[0][:, k, :], w_in[:, k, :], ident[:, :]).then_inc(s_wt, 1)
                pe.wait_ge(s_items, 16 * 5)
                pe.wait_ge(s_wtc, 2)

                def turn(n):
                    if n >= 2:
                        pe.wait_ge(s_itc, n - 1)
                    if QUADS[n] == "rest":
                        mm = nc.tensor.transpose(tr_ps[n % 2][:, 0, 0:RES], items_rest[:, :], ident[0:RES, 0:RES])
                    else:
                        for k, b in enumerate(QUADS[n]):
                            mm = nc.tensor.transpose(tr_ps[n % 2][:, k, :], items[:, b, :], ident[:, :])
                    mm.then_inc(s_itr, 1)

                turn(0)
                for n, quad in enumerate(QUADS):
                    if n + 1 < len(QUADS):
                        turn(n + 1)
                    pe.wait_ge(s_itc, n + 1)
                    if n >= 2:
                        pe.wait_ge(s_hc, n - 1)
                    m = RES if quad == "rest" else P
                    for k in range(1 if quad == "rest" else len(quad)):
                        mm = nc.tensor.matmul(h_ps[n % 2][0:m, k, :], items_t[:, n % 2, k, 0:m], w_itemT[:, :],
                                              start=(k == 0), stop=True, skip_group_check=True)
                    mm.then_inc(s_hmm, 1)

            @block.scalar
            def _(act):
                act.wait_ge(s_wt, 2)
                nc.scalar.activation(w_itemT[:, :], h_ps[0][:, 0, :], ACT.Copy).then_inc(s_wtc, 1)
                nc.scalar.activation(w_userT[:, :], h_ps[0][:, 1, :], ACT.Copy).then_inc(s_wtc, 1)
                for n in range(len(QUADS) + 1):
                    if n < len(QUADS):
                        act.wait_ge(s_itr, n + 1)
                        if n >= 2:
                            act.wait_ge(s_hmm, n - 1)
                        if QUADS[n] == "rest":
                            nc.scalar.activation(items_t[:, n % 2, 0, 0:RES], tr_ps[n % 2][:, 0, 0:RES],
                                                 ACT.Copy).then_inc(s_itc, 1)
                        else:
                            w = len(QUADS[n])
                            nc.scalar.activation(items_t[:, n % 2, 0:w, :], tr_ps[n % 2][:, 0:w, :],
                                                 ACT.Copy).then_inc(s_itc, 1)
                    if n >= 1:
                        act.wait_ge(s_hmm, n)
                        quad = QUADS[n - 1]
                        if quad == "rest":
                            nc.scalar.activation(h_rest[:, :], h_ps[(n - 1) % 2][0:RES, 0, :],
                                                 ACT.Copy).then_inc(s_hc, 1)
                        else:
                            nc.scalar.activation(h_items[:, quad[0]:quad[0] + len(quad), :],
                                                 h_ps[(n - 1) % 2][:, 0:len(quad), :], ACT.Copy).then_inc(s_hc, 1)

            @block.vector
            def _(dve):
                n = [0]
                v = nc.vector

                def link(ins):
                    n[0] += 1
                    ins.then_inc(s_dve, 1)
                    dve.wait_ge(s_dve, n[0])

                dve.wait_ge(s_w, 16 * W_LOADS)
                for k in range(2):
                    link(v.tensor_tensor(att_w[:, k, :], w_rows[:, 0:HE], att[:, k, :], ALU.mult))
                    link(v.tensor_reduce(w_rows[:, HE + HEADS * k:HE + HEADS * (k + 1)],
                                         att_w[:, k, :].rearrange("p (h k) -> p h k", h=HEADS), AX_X, ALU.add))

                run_prep(prep_chain, 40.0)

        x1_dram = nc.dram_tensor("x1_rows", [NB * BATCH, D], F32).ap()
        yT_dram = nc.dram_tensor("normed_columns", [NB, P, BATCH], F32).ap()
        table = nc.dram_tensor("node_table", [NB * BATCH, ROW], F32).ap()
        one = ExitStack()
        with one:
            def osb(name, shape, dt=F32):
                return one.enter_context(nc.sbuf_tensor(name, shape, dt))

            def sem(name):
                return one.enter_context(nc.semaphore(name))

            raw = osb("raw", [P, NRAW, GR * CW])
            turned = osb("turned", [P, NT, GR * CW])
            raw_rest = osb("raw_rest", [32, GR, 32])
            turned_rest = osb("turned_rest", [32, GR, 32])
            list_rows = bufA[0:NBLK, 0:CAP]
            lane_rows = bufB[0:NBLK, 0:CAP // 2].bitcast(BF16)
            xt = osb("xt", [P, 2, 4, D])
            u = osb("u", [P, 4, D])
            uT = osb("uT", [P, BATCH])
            rT = osb("rT", [P, BATCH])
            x1 = osb("x1", [P, 2, 4, D])
            y = osb("y", [P, 4, D])
            yT = osb("yT", [P, BATCH])
            rows = osb("rows", [P, 2, 4, ROW])
            stats = osb("stats", [P, 2, 4, 6])
            meanvar = osb("meanvar", [P, 2, 4, 2])
            dev = osb("dev", [P, 2, 4])
            rdev = osb("rdev", [P, 2, 4])
            shift = osb("shift", [P, 2, 4])
            PREP_US = 0.8
            RANK_US = 1.5
            LAST_COLS = -(-LAST_ROWS // 32) * 32
            acc = [one.enter_context(nc.psum_tensor(f"acc{k}", [P, BATCH], F32)) for k in range(2)]
            u_ps = one.enter_context(nc.psum_tensor("u_ps", [P, 4, P], F32))
            r_ps = one.enter_context(nc.psum_tensor("r_ps", [P, 4, P], F32))
            y_ps = one.enter_context(nc.psum_tensor("y_ps", [P, 4, P], F32))
            row_ps = one.enter_context(nc.psum_tensor("row_ps", [P, 4, ROW], F32))

            s_raw = [sem(f"adj_loaded{k}") for k in range(NRAW)]
            s_turn = sem("adj_turned")
            s_mm = sem("chunk_multiplied")
            s_rawr = sem("rest_loaded")
            s_turnr = sem("rest_turned")
            s_mmr = sem("rest_multiplied")
            s_x = [sem(f"x_loaded{k}") for k in range(2)]
            s_var = sem("variances_ready")
            s_dev = sem("deviations_ready")
            s_inv = sem("inverses_ready")
            s_u = sem("u_ready")
            s_ut = sem("u_turned")
            s_utc = sem("uT_copied")
            s_wu = sem("batch_multiplied")
            s_relu = sem("relu_done")
            s_rt = sem("r_turned")
            s_x1 = sem("x1_ready")
            s_y = sem("y_ready")
            s_yt = sem("y_turned")
            s_ytc = sem("yT_copied")
            s_row = sem("rows_projected")
            s_rowc = sem("rows_copied")
            s_x1st = [sem(f"x1_stored{k}") for k in range(2)]
            s_ytst = sem("yT_stored")
            s_rowst = [sem(f"rows_stored{k}") for k in range(2)]
            s_dve = sem("vector_step")
            s_scat = sem("edges_scattered")
            s_zero = sem("rest_cleared")
            s_lists = sem("lists_loaded")
            s_rows2 = sem("lane_rows_ready")
            s_lanes = sem("lane_rows_stored")
            s_past = sem("waits_passed")

            def wait(eng, s, value):
                if not isinstance(value, int) or value > 0:
                    eng.wait_ge(s, value)

            def wait_alone(eng, s, value):
                wait(eng, s, value)
                if not isinstance(value, int):
                    eng.nop().then_inc(s_past, 1)

            def batches(eng, body, tail=None):
                for i in range(3):
                    body(i, i % 2)
                with eng.Fori(0, (NB - 4) // 2) as k:
                    body(k * 2 + 3, 1)
                    body(k * 2 + 4, 0)
                body(NB - 1, 1)
                if tail is not None:
                    tail(NB, 0)

            def half(i, par):
                return i // 2 if isinstance(i, int) else (i - par) // 2

            block = one.enter_context(nc.Block())

            @block.gpsimd
            def _(pool):
                pool.wait_ge(s_free, 2)
                pool.dma_start(edge_x[:, :], e_halves[0, 1]).then_inc(s_ldx, 16)
                pool.wait_ge(s_slot, 1)
                for j in range(UC):
                    nc.gpsimd.indirect_dma_start(
                        lists, bass.IndirectOffsetOnAxis(ap=slot[:, j:j + 1], axis=0), pay[:, j:j + 1], None,
                        bounds_check=NBLK * CAP - 1, oob_is_err=False).then_inc(s_scat, 16)
                pool.wait_ge(s_scat, 16 * UC)
                pool.dma_start(source[:, :].rearrange("p (b t) -> p b t", b=NBLK),
                               lists.rearrange("(b p t) a -> p b (t a)", b=NBLK, p=P)).then_inc(s_lists, 16)
                pool.dma_start(list_rows[:, :], lists.rearrange("(b c) a -> b (c a)", b=NBLK)).then_inc(s_lists, 16)
                pool.wait_ge(s_rows2, 1)
                pool.dma_start(lanes_dram, lane_rows[:, :]).then_inc(s_lanes, 16)
                pool.wait_ge(s_lanes, 16)

            @block.sync
            def _(sp):
                def body(i, par):
                    last = isinstance(i, int) and i == NB - 1
                    n_rows = LAST_ROWS if last else BATCH
                    whole, over = divmod(n_rows, 32)
                    u0 = i * BATCH

                    def load_rows(dst, cols, signal):
                        src = adj[bass.ds(u0, 32 * whole), cols] if not isinstance(u0, int) else adj[u0:u0 + 32 * whole, cols]
                        sp.dma_start(dst[:, 0:whole, :], src.rearrange("(g r) c -> r g c", r=32)).then_inc(signal, 16)
                        if over:
                            sp.dma_start(dst[0:over, whole, :], adj[u0 + 32 * whole:u0 + n_rows, cols]).then_inc(signal, 16)

                    def rows_of(t, n, i):
                        at = i * BATCH
                        return t[at:at + n, :] if isinstance(at, int) else t[bass.ds(at, n), :]

                    if isinstance(i, int) and i == 0:
                        sp.wait_ge(s_zero, 1)
                    wait_alone(sp, s_x1, i - 1)
                    whole_x, over_x = divmod(n_rows, P)
                    sp.dma_start(xt[:, par, 0:whole_x, :],
                                 rows_of(x, whole_x * P, i).rearrange("(t p) f -> p t f", p=P)).then_inc(s_x[par], 16)
                    if over_x:
                        sp.dma_start(xt[0:over_x, par, whole_x, :], x[u0 + whole_x * P:u0 + n_rows, :]
                                     ).then_inc(s_x[par], 16)
                    wait_alone(sp, s_turnr, i)
                    load_rows(raw_rest[:, :, 0:RES], slice(KT * P, NI), s_rawr)
                    for c, nb in enumerate(CHUNKS):
                        wait_alone(sp, s_turn, i * NCH + c - NRAW + 1)
                        for q in range(4):
                            c0 = QW * q + 32 * COFF[c]
                            load_rows(raw[32 * q:32 * q + 32, c % NRAW, 0:GR * 32 * nb].rearrange(
                                "p (g w) -> p g w", g=GR), slice(c0, c0 + 32 * nb), s_raw[c % NRAW])

                batches(sp, body)

            @block.tensor
            def _(pe):
                def histogram(g0, n, c):
                    for idx in range(c * n // NCH, (c + 1) * n // NCH):
                        pe.wait_ge(s_hot, g0 + idx + 1)
                        for j in range(HG):
                            mm = nc.tensor.matmul(hist_ps[:, :], hot_lane[:, idx % 2, :, j], hot_blk[:, idx % 2, :, j],
                                                  start=False, stop=False, skip_group_check=True)
                        mm.then_inc(s_hist, 1)

                def turn_r(i):
                    pe.wait_ge(s_relu, i)
                    wait(pe, s_x1, i - 1)
                    for k in range(4):
                        mm = nc.tensor.transpose(r_ps[:, k, :], rT[:, k * P:(k + 1) * P], ident[:, :])
                    mm.then_inc(s_rt, 1)

                def turn_y(i):
                    pe.wait_ge(s_y, i)
                    wait(pe, s_ytc, i - 1)
                    for k in range(4):
                        mm = nc.tensor.transpose(y_ps[:, k, :], y[:, k, :], ident[:, :])
                    mm.then_inc(s_yt, 1)

                def project(i):
                    pe.wait_ge(s_ytc, i)
                    wait(pe, s_rowc, i - 1)
                    for k in range(4):
                        mm = nc.tensor.matmul(row_ps[:, k, :], yT[:, k * P:(k + 1) * P], w_rows[:, :],
                                              start=(k == 0), stop=True, skip_group_check=True)
                    mm.then_inc(s_row, 1)

                def body(i, par, hist=None):
                    first = isinstance(i, int) and i == 0
                    cols = LAST_COLS if isinstance(i, int) and i == NB - 1 else BATCH
                    wait(pe, s_relu, i - 1)
                    pe.wait_ge(s_turnr, i + 1)
                    nc.tensor.matmul(acc[par][:, 0:cols], h_rest[:, :], turned_rest[0:RES, 0:cols // 32, :], start=True, stop=False,
                                     skip_group_check=True).then_inc(s_mmr, 1)
                    for c, nb in enumerate(CHUNKS):
                        pe.wait_ge(s_turn, i * NCH + c + 1)
                        t = turned[:, c % NT, 0:GR * 32 * nb].rearrange("p (g b r) -> p g b r", g=GR, b=nb)
                        for b in range(nb):
                            mm = nc.tensor.matmul(acc[par][:, 0:cols], h_items[:, COFF[c] + b, :], t[:, 0:cols // 32, b, :],
                                                  start=False, stop=False, skip_group_check=True)
                        mm.then_inc(s_mm, 1)
                        if hist is not None:
                            histogram(*hist, c)
                        if c == 2 and not first:
                            turn_r(i)
                        if c == 5:
                            pe.wait_ge(s_u, i + 1)
                            wait(pe, s_utc, i)
                            for k in range(4):
                                mm = nc.tensor.transpose(u_ps[:, k, :], u[:, k, :], ident[:, :])
                            mm.then_inc(s_ut, 1)
                        if c == 11 and not first:
                            turn_y(i)
                        if c == 15 and not first:
                            project(i)
                    pe.wait_ge(s_utc, i + 1)
                    nc.tensor.matmul(acc[par][:, 0:cols], w_userT[:, :], uT[:, 0:cols], start=False, stop=True,
                                     skip_group_check=True).then_inc(s_wu, 1)

                def tail(i, par):
                    turn_r(i)
                    turn_y(i)
                    project(i)

                for i in range(3):
                    body(i, i % 2)
                with pe.Fori(0, (BASE_AFTER - 2) // 2) as k:
                    body(k * 2 + 3, 1)
                    body(k * 2 + 4, 0)
                pe.wait_ge(s_tot, 1)
                nc.tensor.matmul(base_ps[:, :], tri[:, :], tot[:, :], start=True, stop=True).then_inc(s_base, 1)
                with pe.Fori(0, (HIST_FROM - 1 - BASE_AFTER) // 2) as k:
                    body(k * 2 + BASE_AFTER + 1, 1)
                    body(k * 2 + BASE_AFTER + 2, 0)
                pe.wait_ge(s_z, 1)
                nc.tensor.matmul(hist_ps[:, :], hot_lane[:, 0, :, 0], hot_blk[:, 0, :, 0], start=True, stop=False,
                                 skip_group_check=True).then_inc(s_hist, 2)
                with pe.Fori(0, (NB - 1 - HIST_FROM) // 2) as k:
                    body(k * 2 + HIST_FROM, 1, (k * (2 * HIST_N), HIST_N))
                    body(k * 2 + HIST_FROM + 1, 0, (k * (2 * HIST_N) + HIST_N, HIST_N))
                body(NB - 1, 1, ((NB - 1 - HIST_FROM) * HIST_N, HIST_LAST))
                pe.wait_ge(s_left, 1)
                nc.tensor.matmul(base_ps[:, 0:1], ones[:, :], nval[:, 4:5], start=True, stop=True).then_inc(s_leftp, 1)
                tail(NB, 0)

            @block.scalar
            def _(act):
                def relu(i, par):
                    act.wait_ge(s_wu, i)
                    wait(act, s_rt, i - 1)
                    nc.scalar.activation(rT[:, :], acc[par][:, :], ACT.Relu, bias=bias_user[:, 0:1]).then_inc(s_relu, 1)

                def root(which, value):
                    act.wait_ge(s_var, value)
                    nc.scalar.activation(dev[:, which, :], meanvar[:, which, :, 1], ACT.Sqrt).then_inc(s_dev, 1)

                def normalize(dst, src, which, value):
                    act.wait_ge(s_inv, value)
                    for k in range(4):
                        ins = nc.scalar.activation(dst[:, k, :], src[:, k, :], ACT.Identity,
                                                   bias=shift[:, which, k:k + 1], scale=rdev[:, which, k:k + 1])
                    return ins

                def finish(i, par):
                    act.wait_ge(s_yt, i)
                    wait(act, s_row, i - 1)
                    wait(act, s_ytst, (i - 1) * 16)
                    nc.scalar.activation(yT[:, :], y_ps[:, :, :], ACT.Copy).then_inc(s_ytc, 1)
                    act.wait_ge(s_ytc, i)
                    act.dma_start(yT_dram[i - 1] if isinstance(i, int) else
                                  yT_dram[bass.ds(i - 1, 1)].rearrange("a p c -> p (a c)"), yT[:, :]).then_inc(s_ytst, 16)
                    act.wait_ge(s_row, i)
                    wait(act, s_rowst[par], half(i - 1, par) * 16)
                    nc.scalar.activation(rows[:, par, :, :], row_ps[:, :, :], ACT.Copy).then_inc(s_rowc, 1)
                    act.wait_ge(s_rowc, i)
                    act.dma_start(dram_rows(table, i), rows[:, par, :, :]).then_inc(s_rowst[par], 16)

                def dram_rows(t, i):
                    at = (i - 1) * BATCH
                    r = t[at:at + BATCH, :] if isinstance(at, int) else t[bass.ds(at, BATCH), :]
                    return r.rearrange("(t p) f -> p t f", p=P)

                def body(i, par):
                    first = isinstance(i, int) and i == 0
                    if not first:
                        relu(i, 1 - par)
                    root(0, 1 if first else i * 2)
                    normalize(u, xt[:, par, :, :], 0, 1 if first else i * 2).then_inc(s_u, 1)
                    act.wait_ge(s_ut, i + 1)
                    wait(act, s_wu, i)
                    nc.scalar.activation(uT[:, :], u_ps[:, :, :], ACT.Copy).then_inc(s_utc, 1)
                    if not first:
                        root(1, i * 2 + 1)
                        normalize(y, x1[:, 1 - par, :, :], 1, i * 2 + 1).then_inc(s_y, 1)
                        act.wait_ge(s_x1, i)
                        act.dma_start(dram_rows(x1_dram, i), x1[:, 1 - par, :, :]).then_inc(s_x1st[1 - par], 16)
                        finish(i, 1 - par)

                def tail(i, par):
                    relu(i, 1)
                    root(1, i * 2)
                    normalize(y, x1[:, 1, :, :], 1, i * 2).then_inc(s_y, 1)
                    act.wait_ge(s_x1, i)
                    act.dma_start(dram_rows(x1_dram, i), x1[:, 1, :, :]).then_inc(s_x1st[1], 16)
                    finish(i, 1)
                    for k in range(2):
                        act.wait_ge(s_x1st[k], NB // 2 * 16)
                        act.wait_ge(s_rowst[k], NB // 2 * 16)
                    act.wait_ge(s_ytst, NB * 16)

                batches(act, body, tail)

            @block.vector
            def _(dve):
                v = nc.vector
                at = [0, 0]

                def link(ins):
                    at[1] += 1
                    ins.then_inc(s_dve, 1)
                    dve.wait_ge(s_dve, at[0] + at[1])

                def spread(src, which):
                    for k in range(4):
                        ins = v.bn_stats(stats[:, which, k, :], src[:, k, :])
                    at[1] += 1
                    ins.then_inc(s_dve, 1)
                    wait_alone(dve, s_dve, at[0] + at[1])
                    for k in range(4):
                        ins = v.bn_aggr(meanvar[:, which, k, :], stats[:, which, k, :])
                    link(ins)
                    v.tensor_scalar(meanvar[:, which, :, 1], meanvar[:, which, :, 1], LN_EPS, None,
                                    ALU.add).then_inc(s_var, 1)

                def invert(which, value):
                    dve.wait_ge(s_dev, value)
                    link(v.reciprocal(rdev[:, which, :], dev[:, which, :]))
                    v.scalar_tensor_tensor(out=shift[:, which, :], in0=meanvar[:, which, :, 0], scalar=-1.0,
                                           in1=rdev[:, which, :], op0=ALU.mult, op1=ALU.mult).then_inc(s_inv, 1)

                def x1_stats(i, par):
                    dve.wait_ge(s_rt, i)
                    wait(dve, s_x1st[par], half(i - 1, par) * 16)
                    ins = v.tensor_tensor(x1[:, par, :, :], r_ps[:, :, :], xt[:, par, :, :], ALU.add)
                    ins.then_inc(s_x1, 1)
                    dve.wait_ge(s_x1, i)
                    spread(x1[:, par, :, :], 1)

                def onehots(g0, n, c):
                    for idx in range(c * n // NCH, (c + 1) * n // NCH):
                        dve.wait_ge(s_hist, g0 + idx + 1 if not isinstance(g0 + idx, int) or g0 + idx else 2)
                        at_g = (g0 + idx) * HG
                        key = slice(at_g, at_g + HG) if isinstance(at_g, int) else bass.ds(at_g, HG)
                        v.tensor_tensor(hot_lane[:, idx % 2, :, :], lane_bf[:, key].unsqueeze(1).broadcast_to([P, P, HG]),
                                        iota_lane[:, :, 0:HG], ALU.is_equal)
                        v.tensor_tensor(hot_blk[:, idx % 2, :, :],
                                        blk_bf[:, key].unsqueeze(1).broadcast_to([P, NBLK, HG]),
                                        iota_tail[:, :, :], ALU.is_equal).then_inc(s_hot, 1)

                going = [True]

                def prepare(i):
                    if going[0] or i > BASE_AFTER:
                        going[0] = run_prep(prep_chain, RANK_US if i > BASE_AFTER else PREP_US)

                def body(i, par, hist=None):
                    first = isinstance(i, int) and i == 0
                    at[0], at[1] = (0, 0) if first else ((i - 1) * 6 + 3, 0)
                    last = isinstance(i, int) and i == NB - 1
                    if first:
                        v.memset(xt[:, :, :, :], 0.0)
                        v.memset(raw_rest[:, :, :], 0.0).then_inc(s_zero, 1)
                    wait(dve, s_mmr, i)
                    dve.wait_ge(s_rawr, (i + 1) * 16 + (16 if last else 0))
                    v.transpose(turned_rest[:, :, :].rearrange("p g r -> p (g r)"),
                                raw_rest[:, :, :].rearrange("p g r -> p (g r)")).then_inc(s_turnr, 1)
                    for c, nb in enumerate(CHUNKS):
                        n = (LAST_COLS if last else BATCH) * nb
                        wait(dve, s_mm, i * NCH + c - NT + 1)
                        extra = 64 * (c // NRAW + 1) if last else 0
                        dve.wait_ge(s_raw[c % NRAW], (i * (NCH // NRAW) + c // NRAW + 1) * 64 + extra)
                        v.transpose(turned[:, c % NT, 0:n], raw[:, c % NRAW, 0:n]).then_inc(s_turn, 1)
                        if hist is not None:
                            onehots(*hist, c)
                        else:
                            prepare(i)
                        if c == 1:
                            dve.wait_ge(s_x[par], half(i, par) * 16 + 16 + (16 if last else 0))
                            spread(xt[:, par, :, :], 0)
                        if c == 3:
                            invert(0, 1 if first else i * 2)
                        if c == 6 and not first:
                            x1_stats(i, 1 - par)
                        if c == 9 and not first:
                            invert(1, i * 2 + 1)

                def tail(i, par):
                    at[0], at[1] = (NB - 1) * 6 + 3, 0
                    x1_stats(i, 1)
                    invert(1, i * 2)
                    dve.wait_ge(s_lists, 32)
                    v.tensor_scalar(source[:, :], source[:, :], (1 << SRC_BITS) - 1, None, ALU.bitwise_and)
                    link(v.tensor_scalar(list_rows, list_rows, SRC_BITS, None, ALU.logical_shift_right))
                    v.tensor_copy(lane_rows.rearrange("b (t p) -> b t p", p=P),
                                  list_rows.rearrange("b (p t) -> b t p", p=P)).then_inc(s_rows2, 1)
                    dve.wait_ge(s_hist, 2 + VC // HG)
                    v.tensor_copy(clamp_count[:, :], hist_ps[:, :])
                    dve.wait_ge(s_leftp, 1)
                    v.tensor_copy(left_count[:, :], base_ps[:, 0:1])

                for i in range(HIST_FROM):
                    body(i, i % 2)
                    if i == BASE_AFTER and going[0]:
                        going[0] = run_prep(prep_chain, 1e9)
                run_prep(prep_chain, 1e9)
                with dve.Fori(0, (NB - 1 - HIST_FROM) // 2) as k:
                    body(k * 2 + HIST_FROM, 1, (k * (2 * HIST_N), HIST_N))
                    body(k * 2 + HIST_FROM + 1, 0, (k * (2 * HIST_N) + HIST_N, HIST_N))
                body(NB - 1, 1, ((NB - 1 - HIST_FROM) * HIST_N, HIST_LAST))
                tail(NB, 0)

        prep.close()

        UB = BATCH // P
        UT = UB * TPB
        TRI = 3
        NTRI = UT // TRI
        PARTS = 3
        HALVES = FF // P
        NF = EXP * HALVES
        TP8 = 8
        NTP = UT // TP8
        MX = NTRI * HEADS
        ND = HE + HEADS

        def slots(eng, body, tail=None):
            for i in range(3):
                body(i, i % 2)
            with eng.Fori(0, (NB - 4) // 2) as k:
                body(k * 2 + 3, 1)
                body(k * 2 + 4, 0)
            body(NB - 1, 1)
            if tail is not None:
                tail(NB, 0)

        def seen(i, par):
            return i // 2 if isinstance(i, int) else (i - par) // 2

        def from_(i, least):
            return not isinstance(i, int) or i >= least

        nd_all = sb("nd_all", [P, NBLK, ND])

        two = ExitStack()
        with two:
            def tsb(name, shape, dt=F32):
                return two.enter_context(nc.sbuf_tensor(name, shape, dt))

            def sem(name):
                return two.enter_context(nc.semaphore(name))

            source_now = tsb("source_now", [P, 2, UT], I32)
            nodes = tsb("nodes", [P, NBLK, ROW])
            last_row = tsb("last_row", [P, ROW])
            no_clamp = tsb("no_clamp", [P, NBLK])
            floor_max = tsb("floor_max", [P, NBLK, HEADS])
            e_self = tsb("e_self", [P, NBLK, 2, HEADS])
            part_sel = tsb("part_sel", [PARTS * HEADS, HEADS, P], BF16)

            gath = tsb("gath", [P, 2, UT, ROW])
            held = tsb("held", [P, 2, UT, ROW])
            lane_bc = tsb("lane_bc", [P, 2, UB * CAP], BF16)
            as_cut = tsb("as_cut", [P, UT, PARTS, HEADS], BF16)
            as_res = tsb("as_res", [P, UT, HEADS])
            asT = tsb("asT", [PARTS * HEADS, UT * P], BF16)
            maskT = tsb("maskT", [P, UT, P], BF16)
            hotT = tsb("hotT", [P, 2, UT, P], BF16)
            hot = tsb("hot", [P, 2, UT, P], BF16)
            junk = tsb("junk", [P, 4, TRI * P], BF16)
            mx = tsb("mx", [P, UB, 2, HEADS])
            am = tsb("am", [P, UB, 2 * HEADS])
            tmp4 = tsb("tmp4", [P, UB, HEADS])
            am_cut = tsb("am_cut", [P, UB, PARTS, 2 * HEADS], BF16)
            am_res = tsb("am_res", [P, UB, 2 * HEADS])
            am_e = tsb("am_e", [P, UT, 2 * HEADS])
            logit = tsb("logit", [P, UT + 2 * UB, HEADS])
            weight = tsb("weight", [P, UT + 2 * UB, HEADS])
            pay_e = tsb("pay_e", [P, UT, ND])
            pay_cut = tsb("pay_cut", [P, UT, PARTS, ND], BF16)
            pay_res = tsb("pay_res", [P, UT, ND])
            own = tsb("own", [P, UB, ND])
            own_b = tsb("own_b", [P, UB, HE])
            nd = tsb("nd", [P, UB, ND])

            as_ps = [two.enter_context(nc.psum_tensor(f"as_rows{k}", [P, TRI * P], F32)) for k in range(HEADS)]
            am_ps = [two.enter_context(nc.psum_tensor(f"am_rows{k}", [P, UT // 2 * PARTS * 2 * HEADS], F32))
                     for k in range(2)]
            turn_ps = two.enter_context(nc.psum_tensor("turned_ps", [P, TP8 * P], BF16))
            agg_ps = two.enter_context(nc.psum_tensor("agg", [P, UB, PARTS, ND], F32))

            s_in = sem("setup_loaded")
            s_sel = sem("selectors_ready")
            s_past = sem("waits_passed")
            s_idx = sem("indices_copied")
            s_gath = [sem(f"rows_gathered{k}") for k in range(2)]
            s_held = sem("rows_held")
            s_bc = [sem(f"lanes_spread{k}") for k in range(2)]
            s_ast = sem("as_cut_ready")
            s_tp = sem("as_turned")
            s_tpc = sem("as_copied")
            s_hotT = sem("lane_onehots_ready")
            s_ht = sem("onehots_turned")
            s_htc = sem("onehots_copied")
            s_mask = sem("masks_ready")
            s_as = sem("as_spread")
            s_mx = sem("maxima_taken")
            s_am = sem("am_ready")
            s_ame = sem("am_spread")
            s_amr = sem("am_read")
            s_log = sem("logits_ready")
            s_exp = sem("weights_ready")
            s_pay = sem("payload_ready")
            s_agg = sem("payload_summed")
            s_nd = sem("sums_read")
            s_dve = sem("vector_step")
            SETUP_LOADS = 2

            def wait_alone(eng, s, value):
                eng.wait_ge(s, value)
                if not isinstance(value, int):
                    eng.nop().then_inc(s_past, 1)

            block = two.enter_context(nc.Block())

            @block.sync
            def _(sp):
                sp.dma_start(nodes[:, :, :], table.rearrange("(b p) c -> p b c", p=P)).then_inc(s_in, 16)
                sp.dma_start(last_row[:, :], table[N - 1, :].partition_broadcast(P)).then_inc(s_in, 16)

                def body(i, par):
                    if from_(i, 2):
                        wait_alone(sp, s_hotT, i - 1)
                    lanes = lanes_dram[i * UB:(i + 1) * UB, :] if isinstance(i, int) else lanes_dram[bass.ds(i * UB, UB), :]
                    sp.dma_start(lane_bc[:, par, :], lanes.rearrange("b c -> (b c)").partition_broadcast(P)
                                 ).then_inc(s_bc[par], 16)

                slots(sp, body)

            @block.gpsimd
            def _(pool):
                nc.gpsimd.memset(part_sel[:, :, :], 0.0).then_inc(s_sel, 1)
                for k in range(PARTS):
                    pool.wait_ge(s_sel, 1 + k)
                    nc.gpsimd.affine_select(out=part_sel[:, :, :], in_=part_sel[:, :, :], compare_op=ALU.not_equal,
                                            fill=1.0, base=-HEADS * k, pattern=[[-1, HEADS], [0, P]],
                                            channel_multiplier=1).then_inc(s_sel, 1)
                def body(i, par):
                    if from_(i, 2):
                        wait_alone(pool, s_held, i - 1)
                        pool.wait_ge(s_gath[par], seen(i, par) * 16 * UT)
                    at = i * UT
                    nc.gpsimd.tensor_copy(source_now[:, par, :], source[:, at:at + UT] if isinstance(at, int) else
                                          source[:, bass.ds(at, UT)]).then_inc(s_idx, 1)
                    wait_alone(pool, s_idx, i + 1)
                    for t in range(UT):
                        nc.gpsimd.indirect_dma_start(
                            gath[:, par, t, :], None, table,
                            bass.IndirectOffsetOnAxis(ap=source_now[:, par, t:t + 1], axis=0),
                            bounds_check=N - 1, oob_is_err=False).then_inc(s_gath[par], 16)

                slots(pool, body)

            @block.tensor
            def _(pe):
                def turn_as(i, k):
                    if k == 0:
                        pe.wait_ge(s_ast, i + 1)
                        if from_(i, 1):
                            pe.wait_ge(s_htc, i * NTP)
                    else:
                        pe.wait_ge(s_tpc, i * NTP + k)
                    for t in range(TP8):
                        mm = nc.tensor.transpose(turn_ps[0:PARTS * HEADS, t * P:(t + 1) * P],
                                                 as_cut[:, k * TP8 + t, :, :].rearrange("p a h -> p (a h)"), identb[:, :])
                    mm.then_inc(s_tp, 1)

                def turn_hot(i, par, k):
                    if k == 0:
                        pe.wait_ge(s_tpc, (i + 1) * NTP)
                        pe.wait_ge(s_hotT, i + 1)
                    else:
                        pe.wait_ge(s_htc, i * NTP + k)
                    for t in range(TP8):
                        mm = nc.tensor.transpose(turn_ps[:, t * P:(t + 1) * P], hotT[:, par, k * TP8 + t, :], identb[:, :])
                    mm.then_inc(s_ht, 1)

                def spread_as(i, tri):
                    pe.wait_ge(s_tpc, i * NTP + (tri * TRI + TRI - 1) // TP8 + 1)
                    for h in range(HEADS):
                        if from_(i, 1) or tri >= 1:
                            pe.wait_ge(s_mx, i * MX + (tri - 1) * HEADS + h + 1)
                        nc.tensor.matmul(as_ps[h][:, :], part_sel[:, h, :], asT[:, tri * TRI * P:(tri + 1) * TRI * P],
                                         start=True, stop=True).then_inc(s_as, 1)

                def spread_am(i, par):
                    pe.wait_ge(s_am, i + 1)
                    if from_(i, 1):
                        pe.wait_ge(s_amr, i * 2)
                    for k in range(2):
                        for t in range(UT // 2):
                            n = k * (UT // 2) + t
                            w = PARTS * 2 * HEADS
                            mm = nc.tensor.matmul(am_ps[k][:, t * w:(t + 1) * w], hotT[:, par, n, :],
                                                  am_cut[:, n // TPB, :, :], start=(t == 0), stop=True,
                                                  skip_group_check=True)
                        mm.then_inc(s_ame, 1)

                def gather_sum(i, par):
                    pe.wait_ge(s_pay, i)
                    pe.wait_ge(s_htc, i * NTP)
                    if from_(i, 2):
                        pe.wait_ge(s_nd, i - 1)
                    for t in range(UT):
                        mm = nc.tensor.matmul(agg_ps[:, t // TPB, :, :], hot[:, par, t, :], pay_cut[:, t, :, :],
                                              start=(t == 0), stop=(t % TPB == TPB - 1), skip_group_check=True)
                    mm.then_inc(s_agg, 1)

                pe.wait_ge(s_sel, 1 + PARTS)

                def body(i, par):
                    turn_as(i, 0)
                    turn_as(i, 1)
                    spread_as(i, 0)
                    spread_as(i, 1)
                    turn_as(i, 2)
                    for tri in range(2, NTRI):
                        spread_as(i, tri)
                        if tri in (3, 5, 7):
                            turn_hot(i, par, (tri - 3) // 2)
                    if from_(i, 1):
                        gather_sum(i, 1 - par)
                    spread_am(i, par)

                def tail(i, par):
                    gather_sum(i, 1 - par)

                slots(pe, body, tail)

            @block.scalar
            def _(act):
                def weights(i):
                    act.wait_ge(s_log, i)
                    nc.scalar.activation(weight[:, :, :], logit[:, :, :], ACT.Exp).then_inc(s_exp, 1)

                def copy_turned(i, k):
                    act.wait_ge(s_tp, i * NTP + k + 1)
                    if k == 0 and from_(i, 1):
                        act.wait_ge(s_as, i * MX)
                    nc.scalar.activation(asT[:, k * TP8 * P:(k + 1) * TP8 * P], turn_ps[0:PARTS * HEADS, :], ACT.Copy
                                         ).then_inc(s_tpc, 1)

                def mask(i, par, k):
                    if k == 0:
                        act.wait_ge(s_hotT, i + 1)
                        if from_(i, 1):
                            act.wait_ge(s_mx, i * MX)
                    nc.scalar.activation(maskT[:, k * TP8:(k + 1) * TP8, :], hotT[:, par, k * TP8:(k + 1) * TP8, :],
                                         ACT.Copy, bias=-BIG, scale=BIG).then_inc(s_mask, 1)

                def body(i, par):
                    act.wait_ge(s_gath[par], (seen(i, par) + 1) * 16 * UT)
                    if from_(i, 2):
                        act.wait_ge(s_pay, i - 1)
                    nc.scalar.activation(held[:, par, :, :], gath[:, par, :, :], ACT.Copy).then_inc(s_held, 1)
                    mask(i, par, 0)
                    if from_(i, 1):
                        weights(i)
                    copy_turned(i, 0)
                    mask(i, par, 1)
                    copy_turned(i, 1)
                    mask(i, par, 2)
                    copy_turned(i, 2)
                    for k in range(NTP):
                        act.wait_ge(s_ht, i * NTP + k + 1)
                        if k == 0 and from_(i, 2):
                            act.wait_ge(s_agg, i - 1)
                        nc.scalar.activation(hot[:, par, k * TP8:(k + 1) * TP8, :].rearrange("p t l -> p (t l)"),
                                             turn_ps[:, :], ACT.Copy).then_inc(s_htc, 1)

                def tail(i, par):
                    weights(i)

                slots(act, body, tail)

            @block.vector
            def _(dve):
                v = nc.vector
                at = [0, 0]
                LINKS = [0]

                def link(ins):
                    at[1] += 1
                    ins.then_inc(s_dve, 1)
                    dve.wait_ge(s_dve, at[0] + at[1])

                def cut(parts, value, residue):
                    link(v.tensor_copy(parts(0), value))
                    link(v.tensor_tensor(residue, value, parts(0), ALU.subtract))
                    link(v.tensor_copy(parts(1), residue))
                    link(v.tensor_tensor(residue, residue, parts(1), ALU.subtract))
                    return v.tensor_copy(parts(2), residue)

                def leaky(t):
                    link(v.scalar_tensor_tensor(out=t, in0=t, scalar=0.2, in1=t, op0=ALU.mult, op1=ALU.max))

                dve.wait_ge(s_in, 16 * SETUP_LOADS)
                a_src, a_dst = nodes[:, :, HE:HE + HEADS], nodes[:, :, HE + HEADS:ROW]
                last_as = last_row[:, HE:HE + HEADS].unsqueeze(1).broadcast_to([P, NBLK, HEADS])
                link(v.tensor_scalar(no_clamp[:, :], clamp_count[:, :], 0.0, -BIG, ALU.is_equal, ALU.mult))
                link(v.tensor_tensor(floor_max[:, :, :], last_as,
                                     no_clamp[:, :].unsqueeze(2).broadcast_to([P, NBLK, HEADS]), ALU.add))
                link(v.tensor_tensor(floor_max[:, :, :], floor_max[:, :, :], a_src, ALU.max))
                link(v.tensor_tensor(e_self[:, :, 0, :], a_src, a_dst, ALU.add))
                link(v.tensor_tensor(e_self[:, :, 1, :], last_as, a_dst, ALU.add))
                leaky(e_self[:, :, :, :])
                SETUP_LINKS = at[1]

                def blk(t, i, *rest):
                    b0 = i * UB
                    key = slice(b0, b0 + UB) if isinstance(i, int) else bass.ds(b0, UB)
                    return t[(slice(None), key) + rest]

                h4 = "p b (h k) -> p b h k"

                def logits(i, par):
                    half_t = UT // 2
                    w = PARTS * 2 * HEADS
                    for k in range(2):
                        dve.wait_ge(s_ame, i * 2 + k - 1)
                        v.tensor_reduce(am_e[:, k * half_t:(k + 1) * half_t, :],
                                        am_ps[k][:, 0:half_t * w].rearrange("p (t a c) -> p t c a", t=half_t, a=PARTS),
                                        AX_X, ALU.add).then_inc(s_amr, 1)
                    dve.wait_ge(s_amr, i * 2)
                    lg = logit[:, 0:UT, :]
                    link(v.tensor_tensor(lg, held[:, par, :, HE:HE + HEADS], am_e[:, :, 0:HEADS], ALU.add))
                    leaky(lg)
                    v.tensor_tensor(lg, lg, am_e[:, :, HEADS:2 * HEADS], ALU.subtract).then_inc(s_log, 1)

                def payload(i, par):
                    dve.wait_ge(s_exp, i)
                    wt = weight[:, 0:UT, :]
                    v.tensor_copy(pay_e[:, :, HE:ND], wt)
                    link(v.tensor_tensor(pay_e[:, :, 0:HE].rearrange("p t (h k) -> p t h k", h=HEADS),
                                         held[:, par, :, 0:HE].rearrange("p t (h k) -> p t h k", h=HEADS),
                                         wt.unsqueeze(3).broadcast_to([P, UT, HEADS, EXP]), ALU.mult))
                    cut(lambda k: pay_cut[:, :, k, :], pay_e[:, :, :], pay_res[:, :, :]).then_inc(s_pay, 1)
                    sw = weight[:, UT:UT + 2 * UB, :].rearrange("p (b s) h -> p b s h", s=2)
                    w_self, w_last = sw[:, :, 0, :], sw[:, :, 1, :]
                    v.tensor_tensor(own[:, :, 0:HE].rearrange(h4, h=HEADS),
                                    blk(nodes, i - 1, slice(0, HE)).rearrange(h4, h=HEADS),
                                    w_self.unsqueeze(3).broadcast_to([P, UB, HEADS, EXP]), ALU.mult)
                    link(v.tensor_tensor(w_last, w_last, blk(clamp_count, i - 1).unsqueeze(2).broadcast_to([P, UB, HEADS]),
                                         ALU.mult))
                    v.tensor_tensor(own[:, :, HE:ND], w_self, w_last, ALU.add)
                    link(v.tensor_tensor(own_b[:, :, :].rearrange(h4, h=HEADS),
                                         last_row[:, 0:HE].unsqueeze(1).broadcast_to([P, UB, HE]).rearrange(h4, h=HEADS),
                                         w_last.unsqueeze(3).broadcast_to([P, UB, HEADS, EXP]), ALU.mult))
                    link(v.tensor_tensor(own[:, :, 0:HE], own[:, :, 0:HE], own_b[:, :, :], ALU.add))

                def sums(i):
                    dve.wait_ge(s_agg, i)
                    link(v.tensor_reduce(nd[:, :, :], agg_ps[:, :, :, :].rearrange("p b a c -> p b c a"), AX_X, ALU.add))
                    v.tensor_tensor(blk(nd_all, i - 1, slice(None)), nd[:, :, :], own[:, :, :], ALU.add
                                    ).then_inc(s_nd, 1)

                def body(i, par):
                    first = isinstance(i, int) and i == 0
                    at[0], at[1] = (SETUP_LINKS, 0) if first else \
                        (SETUP_LINKS + LINKS[0] + (i - 1) * LINKS[-1], 0) if not (isinstance(i, int) and i == 1) else \
                        (SETUP_LINKS + LINKS[0], 0)
                    dve.wait_ge(s_bc[par], (seen(i, par) + 1) * 16)
                    v.tensor_scalar(hotT[:, par, :, :].rearrange("q t p -> q (t p)"), lane_bc[:, par, :],
                                    lane_col[:, 0:1], None, ALU.is_equal).then_inc(s_hotT, 1)
                    if not first:
                        logits(i, 1 - par)
                    dve.wait_ge(s_held, i + 1)
                    if not first:
                        dve.wait_ge(s_tp, i * NTP)
                    g_as = held[:, par, :, HE:HE + HEADS]
                    cut(lambda k: as_cut[:, :, k, :], g_as, as_res[:, :, :]).then_inc(s_ast, 1)
                    if not first:
                        payload(i, 1 - par)
                    wait_alone(dve, s_mask, i + 1)
                    for tri in range(NTRI):
                        for h in range(HEADS):
                            n = tri * HEADS + h
                            wait_alone(dve, s_as, i * MX + n + 1)
                            v.tensor_tensor_reduce(
                                out=junk[:, h, :], in0=as_ps[h][:, :],
                                in1=maskT[:, tri * TRI:(tri + 1) * TRI, :].rearrange("q t p -> q (t p)"),
                                scale=1.0, scalar=-BIG, op0=ALU.add, op1=ALU.max,
                                accum_out=mx[:, tri // 2, tri % 2, h:h + 1]).then_inc(s_mx, 1)
                    v.tensor_copy(am[:, :, 0:HEADS], blk(nodes, i, slice(HE + HEADS, ROW)))
                    dve.wait_ge(s_mx, (i + 1) * MX)
                    m = am[:, :, HEADS:2 * HEADS]
                    link(v.tensor_tensor(m, mx[:, :, 0, :], mx[:, :, 1, :], ALU.max))
                    link(v.tensor_tensor(m, m, blk(floor_max, i, slice(None)), ALU.max))
                    link(v.tensor_tensor(m, m, am[:, :, 0:HEADS], ALU.add))
                    leaky(m)
                    cut(lambda k: am_cut[:, :, k, :], am[:, :, :], am_res[:, :, :]).then_inc(s_am, 1)
                    sl = logit[:, UT:UT + 2 * UB, :].rearrange("p (b s) h -> p b s h", s=2)
                    link(v.tensor_tensor(sl, blk(e_self, i, slice(None), slice(None)),
                                         m.unsqueeze(2).broadcast_to([P, UB, 2, HEADS]), ALU.subtract))
                    link(v.tensor_scalar(logit[:, UT:UT + 2 * UB, :], logit[:, UT:UT + 2 * UB, :], 0.0, None, ALU.min))
                    if not first:
                        sums(i)
                    if first or (isinstance(i, int) and i == 1):
                        LINKS.append(at[1])
                        if first:
                            LINKS[0] = at[1]
                    assert at[1] == (LINKS[0] if first else LINKS[-1])

                def tail(i, par):
                    at[0], at[1] = SETUP_LINKS + LINKS[0] + (i - 1) * LINKS[-1], 0
                    logits(i, 1 - par)
                    payload(i, 1 - par)
                    sums(i)

                slots(dve, body, tail)

        three = ExitStack()
        with three:
            def tsb(name, shape, dt=F32):
                return three.enter_context(nc.sbuf_tensor(name, shape, dt))

            def sem(name):
                return three.enter_context(nc.semaphore(name))

            NHID, NOUT = 4, 4
            LAST_BLOCKS = -(-LAST_ROWS // P)
            w1_sb = tsb("w1_sb", [P, EXP, FF])
            w2_sb = tsb("w2_sb", [P, EXP, HALVES, D])
            b1_sb = tsb("b1_sb", [P, EXP, HALVES])
            b2_row = tsb("b2_row", [1, EXP * D])
            b2_res = tsb("b2_res", [1, EXP * D])
            b2_cut = tsb("b2_cut", [1, PARTS, EXP * D], BF16)
            b2_parts = tsb("b2_parts", [PARTS, EXP * D], BF16)
            onesb = tsb("onesb", [PARTS, P], BF16)
            yTu = tsb("yTu", [P, 2, BATCH])
            x1u = tsb("x1u", [P, 2, UB, D])
            gate = tsb("gate", [P, NBLK, EXP])
            gate_now = tsb("gate_now", [P, 2, UB, EXP])
            bg = tsb("bg", [P, HE])
            gamma = tsb("gamma", [P, HE])
            beta = tsb("beta", [P, HE])
            tmp16 = tsb("tmp16", [P, NBLK, HE])
            tmp16b = tsb("tmp16b", [P, NBLK, HE])
            inv = tsb("inv", [P, NBLK, HEADS])
            col = tsb("col", [P, 6, NBLK])
            score = tsb("score", [P, NBLK, EXP])
            cmpb = tsb("cmpb", [P, NBLK, EXP])
            order = tsb("order", [P, NBLK, EXP])
            gexp = tsb("gexp", [P, NBLK, EXP])
            hidden = tsb("hidden", [P, 2, NF, BATCH])
            hid_ps = [three.enter_context(nc.psum_tensor(f"hid{k}", [P, BATCH], F32)) for k in range(NHID)]
            out_ps = [three.enter_context(nc.psum_tensor(f"experts{k}", [P, EXP, D], F32)) for k in range(NOUT)]

            s_norm = sem("norm_weights_loaded")
            s_in = sem("experts_loaded")
            s_sq = sem("score_variance_ready")
            s_sqd = sem("score_deviation_ready")
            s_ge = sem("gate_logits_ready")
            s_ged = sem("gate_exponentials_ready")
            s_b2 = sem("b2_parts_ready")
            s_b2m = sem("b2_parts_moved")
            s_sel = sem("ones_ready")
            s_past = sem("waits_passed")
            s_y2 = [sem(f"y_loaded{k}") for k in range(2)]
            s_x2 = [sem(f"x1_loaded{k}") for k in range(2)]
            s_hid = sem("hidden_multiplied")
            s_gelu = sem("hidden_activated")
            s_ex = sem("experts_multiplied")
            s_comb = sem("experts_combined")
            s_outst = [sem(f"out_stored{k}") for k in range(2)]
            s_dve = sem("vector_step")
            SETUP_LOADS = 4

            def wait_alone(eng, s, value):
                eng.wait_ge(s, value)
                if not isinstance(value, int):
                    eng.nop().then_inc(s_past, 1)

            block = three.enter_context(nc.Block())

            @block.sync
            def _(sp):
                for t, a in ((bg, b_gat), (gamma, ln_gamma), (beta, ln_beta)):
                    sp.dma_start(t[:, :], a.partition_broadcast(P)).then_inc(s_norm, 16)
                sp.dma_start(w1_sb[:, :, :], W1.rearrange("e f c -> f e c")).then_inc(s_in, 16)
                sp.dma_start(w2_sb[:, :, :, :], W2.rearrange("e (k f) c -> f e k c", f=P)).then_inc(s_in, 16)
                with nc.allow_non_contiguous_dma(reason="1024 biases, once"):
                    sp.dma_start(b1_sb[:, :, :], b1.rearrange("e (k f) -> f e k", f=P)).then_inc(s_in, 16)
                sp.dma_start(b2_row[:, :], b2.rearrange("e f -> (e f)").unsqueeze(0)).then_inc(s_in, 16)

                def body(i, par):
                    if from_(i, 2):
                        wait_alone(sp, s_hid, (i - 1) * NF)
                    sp.dma_start(yTu[:, par, :], yT_dram[i] if isinstance(i, int) else
                                 yT_dram[bass.ds(i, 1)].rearrange("a p c -> p (a c)")).then_inc(s_y2[par], 16)
                    if from_(i, 2):
                        wait_alone(sp, s_outst[par], seen(i, par) * 16)
                    rows_i = x1_dram[i * BATCH:(i + 1) * BATCH, :] if isinstance(i, int) else \
                        x1_dram[bass.ds(i * BATCH, BATCH), :]
                    sp.dma_start(x1u[:, par, :, :], rows_i.rearrange("(t p) f -> p t f", p=P)).then_inc(s_x2[par], 16)
                    if isinstance(i, int) and i == 0:
                        sp.wait_ge(s_b2, 1)
                        for k in range(PARTS):
                            sp.dma_start(b2_parts[k:k + 1, :], b2_cut[0:1, k, :]).then_inc(s_b2m, 16)

                slots(sp, body)

            @block.gpsimd
            def _(pool):
                nc.gpsimd.memset(onesb[:, :], 1.0).then_inc(s_sel, 1)

            @block.tensor
            def _(pe):
                def layer1(i, par, f):
                    n = i * NF + f
                    if from_(n, NHID):
                        pe.wait_ge(s_gelu, n - NHID + 1)
                    e, k = divmod(f, HALVES)
                    cols = LAST_COLS if isinstance(i, int) and i == NB - 1 else BATCH
                    nc.tensor.matmul(hid_ps[f % NHID][:, 0:cols], w1_sb[:, e, k * P:(k + 1) * P], yTu[:, par, 0:cols],
                                     start=True, stop=True).then_inc(s_hid, 1)

                def layer2(i, par, b):
                    if b == 0:
                        pe.wait_ge(s_gelu, i * NF)
                    n = (i - 1) * UB + b
                    if from_(n, NOUT):
                        pe.wait_ge(s_comb, n - NOUT + 1)
                    nc.tensor.matmul(out_ps[b % NOUT][:, :, :], onesb[:, :], b2_parts[:, :], start=True, stop=False,
                                     skip_group_check=True)
                    for e in range(EXP):
                        for k in range(HALVES):
                            mm = nc.tensor.matmul(out_ps[b % NOUT][:, e, :],
                                                  hidden[:, par, e * HALVES + k, b * P:(b + 1) * P],
                                                  w2_sb[:, e, k, :], start=False, stop=(k == HALVES - 1),
                                                  skip_group_check=True)
                    mm.then_inc(s_ex, 1)

                pe.wait_ge(s_in, 16 * SETUP_LOADS)

                def body(i, par):
                    pe.wait_ge(s_y2[par], seen(i, par) * 16 + 16)
                    for f in range(NF):
                        layer1(i, par, f)
                        if f % 2 == 1 and from_(i, 1):
                            if isinstance(i, int) and i == 1 and f == 1:
                                pe.wait_ge(s_b2m, 16 * PARTS)
                                pe.wait_ge(s_sel, 1)
                            layer2(i, 1 - par, f // 2)

                def tail(i, par):
                    for b in range(LAST_BLOCKS):
                        layer2(i, 1 - par, b)

                slots(pe, body, tail)

            @block.scalar
            def _(act):
                act.wait_ge(s_in, 16 * SETUP_LOADS)

                def gelu(i, par, f):
                    act.wait_ge(s_hid, i * NF + f + 1)
                    if f == 0 and from_(i, 2):
                        act.wait_ge(s_ex, (i - 1) * UB)
                    e, k = divmod(f, HALVES)
                    cols = LAST_COLS if isinstance(i, int) and i == NB - 1 else BATCH
                    nc.scalar.activation(hidden[:, par, f, 0:cols], hid_ps[f % NHID][:, 0:cols], ACT.Gelu,
                                         bias=b1_sb[:, e, k:k + 1]).then_inc(s_gelu, 1)

                def store(i, par):
                    last = isinstance(i, int) and i == NB
                    act.wait_ge(s_comb, (i - 1) * UB + LAST_BLOCKS if last else i * UB)
                    at = (i - 1) * BATCH
                    rows_n = LAST_ROWS if last else BATCH
                    whole, over = divmod(rows_n, P)
                    o = out[at:at + whole * P, :] if isinstance(at, int) else out[bass.ds(at, whole * P), :]
                    act.dma_start(o.rearrange("(t p) f -> p t f", p=P), x1u[:, par, 0:whole, :]).then_inc(s_outst[par], 16)
                    if over:
                        act.dma_start(out[at + whole * P:at + rows_n, :], x1u[0:over, par, whole, :]
                                      ).then_inc(s_outst[par], 16)

                def body(i, par):
                    for f in range(NF):
                        gelu(i, par, f)
                    if isinstance(i, int) and i == 0:
                        act.wait_ge(s_sq, 1)
                        nc.scalar.activation(col[:, 3, :], col[:, 2, :], ACT.Sqrt).then_inc(s_sqd, 1)
                    if isinstance(i, int) and i == 1:
                        act.wait_ge(s_ge, 1)
                        nc.scalar.activation(gexp[:, :, :], cmpb[:, :, :], ACT.Exp).then_inc(s_ged, 1)
                    if from_(i, 1):
                        store(i, 1 - par)

                def tail(i, par):
                    store(i, 1 - par)
                    act.wait_ge(s_outst[0], NB // 2 * 16)
                    act.wait_ge(s_outst[1], NB // 2 * 16 + 16)

                slots(act, body, tail)

            @block.vector
            def _(dve):
                v = nc.vector
                at = [0, 0]

                def link(ins):
                    at[1] += 1
                    ins.then_inc(s_dve, 1)
                    dve.wait_ge(s_dve, at[0] + at[1])

                dve.wait_ge(s_in, 16 * SETUP_LOADS)
                link(v.tensor_copy(b2_cut[:, 0, :], b2_row[:, :]))
                link(v.tensor_tensor(b2_res[:, :], b2_row[:, :], b2_cut[:, 0, :], ALU.subtract))
                link(v.tensor_copy(b2_cut[:, 1, :], b2_res[:, :]))
                link(v.tensor_tensor(b2_res[:, :], b2_res[:, :], b2_cut[:, 1, :], ALU.subtract))
                v.tensor_copy(b2_cut[:, 2, :], b2_res[:, :]).then_inc(s_b2, 1)
                h4 = "p b (h k) -> p b h k"
                dve.wait_ge(s_norm, 16 * 3)
                link(v.tensor_scalar(inv[:, :, :], nd_all[:, :, HE:ND], 1e-16, None, ALU.add))
                link(v.reciprocal(inv[:, :, :], inv[:, :, :]))
                link(v.tensor_tensor(tmp16[:, :, :].rearrange(h4, h=HEADS),
                                     nd_all[:, :, 0:HE].rearrange(h4, h=HEADS),
                                     inv[:, :, :].unsqueeze(3).broadcast_to([P, NBLK, HEADS, EXP]), ALU.mult))
                center(v, link, tmp16[:, :, :], bg, tmp16b, col, NBLK).then_inc(s_sq, 1)
                dve.wait_ge(s_sqd, 1)
                rank_scores(v, link, tmp16[:, :, :], gamma, beta, col, score, order, cmpb, NBLK).then_inc(s_ge, 1)
                dve.wait_ge(s_ged, 1)
                link(share_gates(v, link, order, gexp, col, gate[:, :, :], NBLK))
                SETUP_LINKS = at[1]
                UNIT_LINKS = UB * (EXP - 1) + 1

                def combine(i, par, b):
                    dve.wait_ge(s_ex, (i - 1) * UB + b + 1)
                    for e in range(EXP):
                        ins = v.scalar_tensor_tensor(out=x1u[:, par, b, :], in0=out_ps[b % NOUT][:, e, :],
                                                     scalar=gate_now[:, par, b, e:e + 1], in1=x1u[:, par, b, :],
                                                     op0=ALU.mult, op1=ALU.add)
                        if e < EXP - 1:
                            link(ins)
                        else:
                            ins.then_inc(s_comb, 1)

                def body(i, par):
                    if not from_(i, 1):
                        return
                    at[0], at[1] = SETUP_LINKS + (i - 1) * UNIT_LINKS, 0
                    at_b = (i - 1) * UB
                    g = gate[:, at_b:at_b + UB, :] if isinstance(i, int) else gate[:, bass.ds(at_b, UB), :]
                    link(v.tensor_copy(gate_now[:, 1 - par, :, :], g))
                    dve.wait_ge(s_x2[1 - par], seen(i - 1, 1 - par) * 16 + 16)
                    last = isinstance(i, int) and i == NB
                    for b in range(LAST_BLOCKS if last else UB):
                        combine(i, 1 - par, b)
                    assert last or at[1] == UNIT_LINKS

                slots(dve, body, body)

        ALL_COLS = EC
        FULL = N // P
        OVER = N - FULL * P
        HALF_FF = FF // P
        every = ExitStack()
        with every:
            def gsb(name, shape, dt=F32):
                return every.enter_context(nc.sbuf_tensor(name, shape, dt))

            def gps(name, shape):
                return every.enter_context(nc.psum_tensor(name, shape, F32))

            def sem(name):
                return every.enter_context(nc.semaphore(name))

            all_src = gsb("all_src", [P, EC], I32)
            all_dst = gsb("all_dst", [P, EC], I32)
            col_src = gsb("col_src", [P, 1], I32)
            col_dst = gsb("col_dst", [P, 1])
            table_lanes = gsb("table_lanes", [P, NBLK, ROW])
            node_id = gsb("node_id", [P, NBLK])
            edge_rows = gsb("edge_rows", [P, ROW])
            diag = gsb("diag", [P, HEADS + 1, P])
            as_all = gsb("as_all", [P, HEADS, P])
            dst_all = gsb("dst_all", [P, P])
            off = gsb("off", [P, P])
            z = gsb("z", [P, HEADS, P + 1])
            wz = gsb("wz", [P, HEADS, P + 1])
            wzT = gsb("wzT", [P, HEADS, P])
            run_max = gsb("run_max", [P, NBLK, HEADS])
            run_sum = gsb("run_sum", [P, NBLK, ND])
            new_max = gsb("new_max", [P, HEADS])
            part = gsb("part", [P, ND])
            gw1 = gsb("gw1", [P, EXP, FF])
            gw2 = gsb("gw2", [P, EXP, HALF_FF, D])
            gb1 = gsb("gb1", [P, EXP, HALF_FF])
            gb2 = gsb("gb2", [1, EXP * D])
            gbg, ggamma, gbeta = gsb("gbg", [P, HE]), gsb("ggamma", [P, HE]), gsb("gbeta", [P, HE])
            gy = gsb("gy", [P, P])
            gx1 = gsb("gx1", [P, D])
            ghid = gsb("ghid", [P, EXP * HALF_FF, P])
            gagg = gsb("gagg", [P, 1, HE])
            gsq = gsb("gsq", [P, 1, HE])
            gcol = gsb("gcol", [P, 6, 1])
            gscore, gcmp, gorder, gexps, ggate = (gsb(n, [P, 1, EXP]) for n in
                                                  ("gscore", "gcmp", "gorder", "gexps", "ggate"))
            wide_ps = gps("wide_ps", [P, HEADS, P])
            dst_ps = gps("dst_ps", [P, P])
            wzT_ps = gps("wzT_ps", [P, HEADS, P])
            num_ps = gps("num_ps", [P, HE])
            ghid_ps = [gps(f"ghid_ps{k}", [P, 4, P]) for k in range(2)]
            gout_ps = gps("gout_ps", [P, EXP, D])

            s_past = sem("waits_passed")
            s_gin = sem("general_loaded")
            s_gid = sem("node_ids_ready")
            s_gidx = sem("column_sources_ready")
            s_grow = sem("column_rows_gathered")
            s_gdiag = sem("diagonals_ready")
            s_gwide = sem("column_spread")
            s_gz = sem("column_logits_ready")
            s_gwz = sem("column_weights_ready")
            s_gwt = sem("column_weights_turned")
            s_gwc = sem("column_weights_copied")
            s_gnum = sem("column_summed")
            s_gcols = sem("columns_done")
            s_gfree = sem("block_buffers_free")
            s_gyx = sem("block_loaded")
            s_ghm = sem("block_hidden_multiplied")
            s_gha = sem("block_hidden_activated")
            s_gex = sem("block_experts_multiplied")
            s_gsq = sem("block_variance_ready")
            s_gsd = sem("block_deviation_ready")
            s_gge = sem("block_gate_logits_ready")
            s_ggd = sem("block_gate_exponentials_ready")
            s_gout = sem("block_stored")
            s_dve = sem("vector_step")
            G_LOADS = 3 + 4 + 3

            def wait_alone(eng, s, value):
                eng.wait_ge(s, value)
                eng.nop().then_inc(s_past, 1)

            def each_block(eng, body):
                with eng.Fori(0, FULL) as b:
                    body(b, P)
                body(FULL, OVER)

            def lanes_of(t, b, n):
                return t[b * P:b * P + n, :] if isinstance(b, int) else t[bass.ds(b * P, n), :]

            block = every.enter_context(nc.Block())

            @block.sync
            def _(sp):
                left = sp.value_load(left_count[0:1, 0:1], min_val=0, max_val=E)
                with sp.If(left > 0):
                    e_v = edge_index.rearrange("a (p c) -> a p c", p=P)
                    sp.dma_start(all_src[:, :], e_v[0]).then_inc(s_gin, 16)
                    sp.dma_start(all_dst[:, :], e_v[1]).then_inc(s_gin, 16)
                    sp.dma_start(table_lanes[:, :, :], table.rearrange("(b p) c -> p b c", p=P)).then_inc(s_gin, 16)
                    sp.dma_start(gw1[:, :, :], W1.rearrange("e f c -> f e c")).then_inc(s_gin, 16)
                    sp.dma_start(gw2[:, :, :, :], W2.rearrange("e (k f) c -> f e k c", f=P)).then_inc(s_gin, 16)
                    with nc.allow_non_contiguous_dma(reason="1024 biases, once"):
                        sp.dma_start(gb1[:, :, :], b1.rearrange("e (k f) -> f e k", f=P)).then_inc(s_gin, 16)
                    sp.dma_start(gb2[:, :], b2.rearrange("e f -> (e f)").unsqueeze(0)).then_inc(s_gin, 16)
                    for t, a in ((gbg, b_gat), (ggamma, ln_gamma), (gbeta, ln_beta)):
                        sp.dma_start(t[:, :], a.partition_broadcast(P)).then_inc(s_gin, 16)

                    def body(b, n):
                        sp.wait_ge(s_gfree, b + 1)
                        yb = yT_dram[b // 4] if isinstance(b, int) else yT_dram[bass.ds(b // 4, 1)].rearrange(
                            "a p c -> p (a c)")
                        at = (b % 4) * P
                        yb = yb[:, at:at + P] if isinstance(b, int) else yb[:, bass.ds(at, P)]
                        sp.dma_start(gy[:, :], yb).then_inc(s_gyx, 16)
                        sp.dma_start(gx1[0:n, :], lanes_of(x1_dram, b, n)).then_inc(s_gyx, 16)

                    each_block(sp, body)

            @block.gpsimd
            def _(pool):
                left = pool.value_load(left_count[0:1, 0:1], min_val=0, max_val=E)
                with pool.If(left > 0):
                    nc.gpsimd.iota(node_id[:, :], [[P, NBLK]], base=0, channel_multiplier=1,
                                   allow_small_or_imprecise_dtypes=True).then_inc(s_gid, 1)
                    with pool.Fori(0, ALL_COLS) as k:
                        wait_alone(pool, s_gidx, k + 1)
                        nc.gpsimd.indirect_dma_start(
                            edge_rows[:, :], None, table, bass.IndirectOffsetOnAxis(ap=col_src[:, 0:1], axis=0),
                            bounds_check=N - 1, oob_is_err=False).then_inc(s_grow, 16)

            @block.tensor
            def _(pe):
                left = pe.value_load(left_count[0:1, 0:1], min_val=0, max_val=E)
                with pe.If(left > 0):
                    with pe.Fori(0, ALL_COLS) as k:
                        pe.wait_ge(s_gdiag, k + 1)
                        nc.tensor.matmul(wide_ps[:, :, :], ones[:, :], diag[:, 0:HEADS, :], start=True, stop=True)
                        nc.tensor.matmul(dst_ps[:, :], ones[:, :], diag[:, HEADS, :], start=True, stop=True
                                         ).then_inc(s_gwide, 1)
                        with pe.Fori(0, NBLK) as b:
                            n = k * NBLK + b + 1
                            pe.wait_ge(s_gwz, n)
                            for h in range(HEADS):
                                mm = nc.tensor.transpose(wzT_ps[:, h, :], wz[:, h, 0:P], ident[:, :])
                            mm.then_inc(s_gwt, 1)
                            pe.wait_ge(s_gwc, n)
                            for h in range(HEADS):
                                mm = nc.tensor.matmul(num_ps[:, h * EXP:(h + 1) * EXP], wzT[:, h, :],
                                                      edge_rows[:, h * EXP:(h + 1) * EXP], start=(h == 0), stop=True,
                                                      skip_group_check=True)
                            mm.then_inc(s_gnum, 1)
                    pe.wait_ge(s_gin, 16 * G_LOADS)

                    def body(b, n):
                        pe.wait_ge(s_gyx, (b + 1) * 32)
                        for f in range(EXP * HALF_FF):
                            e, k = divmod(f, HALF_FF)
                            mm = nc.tensor.matmul(ghid_ps[f // 4][:, f % 4, :], gw1[:, e, k * P:(k + 1) * P], gy[:, :],
                                                  start=(f % 4 == 0), stop=True, skip_group_check=True)
                        mm.then_inc(s_ghm, 1)
                        pe.wait_ge(s_gha, b + 1)
                        nc.tensor.matmul(gout_ps[:, :, :], ones[0:1, :], gb2[:, :], start=True, stop=False,
                                         skip_group_check=True)
                        for e in range(EXP):
                            for k in range(HALF_FF):
                                mm = nc.tensor.matmul(gout_ps[:, e, :], ghid[:, e * HALF_FF + k, :], gw2[:, e, k, :],
                                                      start=False, stop=(k == HALF_FF - 1), skip_group_check=True)
                        mm.then_inc(s_gex, 1)

                    each_block(pe, body)

            @block.scalar
            def _(act):
                left = act.value_load(left_count[0:1, 0:1], min_val=0, max_val=E)
                with act.If(left > 0):
                    with act.Fori(0, ALL_COLS) as k:
                        with act.Fori(0, NBLK) as b:
                            n = k * NBLK + b + 1
                            act.wait_ge(s_gz, n)
                            nc.scalar.activation(wz[:, :, :], z[:, :, :], ACT.Exp).then_inc(s_gwz, 1)
                            act.wait_ge(s_gwt, n)
                            nc.scalar.activation(wzT[:, :, :], wzT_ps[:, :, :], ACT.Copy).then_inc(s_gwc, 1)
                    act.wait_ge(s_gin, 16 * G_LOADS)

                    def body(b, n):
                        act.wait_ge(s_ghm, b + 1)
                        for f in range(EXP * HALF_FF):
                            e, k = divmod(f, HALF_FF)
                            ins = nc.scalar.activation(ghid[:, f, :], ghid_ps[f // 4][:, f % 4, :], ACT.Gelu,
                                                       bias=gb1[:, e, k:k + 1])
                        ins.then_inc(s_gha, 1)
                        act.wait_ge(s_gsq, b + 1)
                        nc.scalar.activation(gcol[:, 3, :], gcol[:, 2, :], ACT.Sqrt).then_inc(s_gsd, 1)
                        act.wait_ge(s_gge, b + 1)
                        nc.scalar.activation(gexps[:, :, :], gcmp[:, :, :], ACT.Exp).then_inc(s_ggd, 1)
                        act.wait_ge(s_gcols, b + 1)
                        act.dma_start(lanes_of(out, b, n), gx1[0:n, :]).then_inc(s_gout, 16)

                    each_block(act, body)
                    act.wait_ge(s_gout, (FULL + 1) * 16)

            @block.vector
            def _(dve):
                v = nc.vector
                at = [0, 0]

                def link(ins):
                    at[1] += 1
                    ins.then_inc(s_dve, 1)
                    dve.wait_ge(s_dve, at[0] + at[1])

                left = dve.value_load(left_count[0:1, 0:1], min_val=0, max_val=E)
                with dve.If(left > 0):
                    dve.wait_ge(s_gin, 16 * G_LOADS)
                    dve.wait_ge(s_gid, 1)
                    link(v.tensor_scalar(all_src[:, :], all_src[:, :], float(N - 1), None, ALU.min))
                    a_src, a_dst = table_lanes[:, :, HE:HE + HEADS], table_lanes[:, :, HE + HEADS:ROW]
                    link(v.tensor_tensor(run_max[:, :, :], a_src, a_dst, ALU.add))
                    link(v.scalar_tensor_tensor(out=run_max[:, :, :], in0=run_max[:, :, :], scalar=0.2,
                                                in1=run_max[:, :, :], op0=ALU.mult, op1=ALU.max))
                    link(v.tensor_copy(run_sum[:, :, 0:HE], table_lanes[:, :, 0:HE]))
                    link(v.memset(run_sum[:, :, HE:ND], 1.0))
                    SETUP = at[1]
                    COL_LINKS, BLK_LINKS = 4, 11
                    with dve.Fori(0, ALL_COLS) as k:
                        at[0], at[1] = k * (COL_LINKS + NBLK * BLK_LINKS) + SETUP, 0
                        v.tensor_copy(col_src[:, :], all_src[:, bass.ds(k, 1)]).then_inc(s_gidx, 1)
                        link(v.tensor_copy(col_dst[:, :], all_dst[:, bass.ds(k, 1)]))
                        dve.wait_ge(s_grow, (k + 1) * 16)
                        for h in range(HEADS):
                            v.tensor_scalar(diag[:, h, :], ident[:, :], edge_rows[:, HE + h:HE + h + 1], None, ALU.mult)
                        link(v.tensor_scalar(diag[:, HEADS, :], ident[:, :], col_dst[:, 0:1], None, ALU.mult))
                        v.nop().then_inc(s_gdiag, 1)
                        dve.wait_ge(s_gwide, k + 1)
                        link(v.tensor_copy(as_all[:, :, :], wide_ps[:, :, :]))
                        link(v.tensor_copy(dst_all[:, :], dst_ps[:, :]))
                        v.nop().then_inc(s_past, 1)
                        assert at[1] == COL_LINKS
                        with dve.Fori(0, NBLK) as b:
                            at[0], at[1] = k * (COL_LINKS + NBLK * BLK_LINKS) + b * BLK_LINKS + (SETUP + COL_LINKS), 0
                            n = k * NBLK + b + 1
                            mine, ad = run_max[:, bass.ds(b, 1), :], table_lanes[:, bass.ds(b, 1), HE + HEADS:ROW]
                            zz = z[:, :, 0:P]
                            link(v.tensor_scalar(off[:, :], dst_all[:, :], node_id[:, bass.ds(b, 1)], -BIG,
                                                 ALU.not_equal, ALU.mult))
                            link(v.tensor_tensor(zz, as_all[:, :, :], ad.rearrange("p a h -> p (a h)").unsqueeze(2)
                                                 .broadcast_to([P, HEADS, P]), ALU.add))
                            link(v.scalar_tensor_tensor(out=zz, in0=zz, scalar=0.2, in1=zz, op0=ALU.mult, op1=ALU.max))
                            link(v.tensor_tensor(zz, zz, off[:, :].unsqueeze(1).broadcast_to([P, HEADS, P]), ALU.add))
                            link(v.tensor_reduce(new_max[:, :], zz, AX_X, ALU.max))
                            mine = mine.rearrange("p a h -> p (a h)")
                            link(v.tensor_tensor(new_max[:, :], new_max[:, :], mine, ALU.max))
                            v.tensor_tensor(z[:, :, P], mine, new_max[:, :], ALU.subtract)
                            v.tensor_tensor(zz, zz, new_max[:, :].unsqueeze(2).broadcast_to([P, HEADS, P]),
                                            ALU.subtract).then_inc(s_gz, 1)
                            wait_alone(dve, s_gz, n)
                            link(v.tensor_copy(mine, new_max[:, :]))
                            dve.wait_ge(s_gwz, n)
                            link(v.tensor_reduce(part[:, HE:ND], wz[:, :, 0:P], AX_X, ALU.add))
                            dve.wait_ge(s_gnum, n)
                            link(v.tensor_copy(part[:, 0:HE], num_ps[:, :]))
                            mysum = run_sum[:, bass.ds(b, 1), :].rearrange("p a c -> p (a c)")
                            num, den = mysum[:, 0:HE].rearrange("p (h k) -> p h k", h=HEADS), mysum[:, HE:ND]
                            v.tensor_tensor(num, num, wz[:, :, P:P + 1].broadcast_to([P, HEADS, EXP]), ALU.mult)
                            link(v.tensor_tensor(den, den, wz[:, :, P], ALU.mult))
                            link(v.tensor_tensor(mysum, mysum, part[:, :], ALU.add))
                            GOT = at[1]
                    assert GOT == BLK_LINKS, GOT
                    AFTER = ALL_COLS * (COL_LINKS + NBLK * BLK_LINKS) + SETUP
                    v.memset(gx1[:, :], 0.0).then_inc(s_gfree, 1)

                    def body(b, n):
                        at[0], at[1] = b * G_TAIL_LINKS + AFTER, 0
                        sums = run_sum[:, b:b + 1, :] if isinstance(b, int) else run_sum[:, bass.ds(b, 1), :]
                        link(v.tensor_scalar(gexps[:, :, :], sums[:, :, HE:ND], 1e-16, None, ALU.add))
                        link(v.reciprocal(gexps[:, :, :], gexps[:, :, :]))
                        h4 = "p b (h k) -> p b h k"
                        link(v.tensor_tensor(gagg[:, :, :].rearrange(h4, h=HEADS), sums[:, :, 0:HE].rearrange(h4, h=HEADS),
                                             gexps[:, :, :].unsqueeze(3).broadcast_to([P, 1, HEADS, EXP]), ALU.mult))
                        center(v, link, gagg[:, :, :], gbg, gsq, gcol, 1).then_inc(s_gsq, 1)
                        dve.wait_ge(s_gsd, b + 1)
                        rank_scores(v, link, gagg[:, :, :], ggamma, gbeta, gcol, gscore, gorder, gcmp, 1
                                    ).then_inc(s_gge, 1)
                        dve.wait_ge(s_ggd, b + 1)
                        link(share_gates(v, link, gorder, gexps, gcol, ggate[:, :, :], 1))
                        dve.wait_ge(s_gyx, (b + 1) * 32)
                        dve.wait_ge(s_gex, b + 1)
                        for e in range(EXP):
                            ins = v.scalar_tensor_tensor(out=gx1[:, :], in0=gout_ps[:, e, :], scalar=ggate[:, 0, e:e + 1],
                                                         in1=gx1[:, :], op0=ALU.mult, op1=ALU.add)
                            if e < EXP - 1:
                                link(ins)
                            else:
                                ins.then_inc(s_gcols, 1)
                        dve.wait_ge(s_gout, (b + 1) * 16)
                        v.nop().then_inc(s_gfree, 1)

                    each_block(dve, body)
                    assert at[1] == G_TAIL_LINKS, at[1]


_INS = ["x", "adj", "L0_gnn_item_feat", "L0_gnn_W_item", "L0_gnn_b_item", "L0_gnn_W_user", "L0_gnn_b_user",
        "L0_ffn_W_gat", "L0_ffn_att_src", "L0_ffn_att_dst", "L0_ffn_b_gat", "L0_ffn_ln_gamma", "L0_ffn_ln_beta",
        "L0_ffn_W1", "L0_ffn_b1", "L0_ffn_W2", "L0_ffn_b2", "L0_ffn_edge_index"]


def kernel(**inputs):
    import numpy as _np
    import concourse.bacc as _bacc
    from concourse import mybir as _mybir
    from concourse.bass_utils import run_bass_kernel_spmd as _run

    nc = _bacc.Bacc("TRN2", target_bir_lowering=False, num_devices=1)
    arrays, args = {}, []
    for name in _INS:
        a = _np.ascontiguousarray(inputs[name])
        arrays[f"in_{name}_dram"] = a
        args.append(nc.dram_tensor(f"in_{name}_dram", a.shape, _mybir.dt.from_np(a.dtype), kind="ExternalInput").ap())
    out = nc.dram_tensor("out_0_dram", (10000, 128), _mybir.dt.from_np(_np.dtype("float32")), kind="ExternalOutput").ap()
    adj_ffn_kernel(nc, *args, out)
    r = _run(nc, [arrays], core_ids=[0])
    return r.results[0]["out_0_dram"]
```
